# Optimizing a Trainium2 kernel written in Bass

```python
import numpy as np
import jax
import jax.numpy as jnp

def _softmax(x, axis=-1):
    return jax.nn.softmax(x, axis=axis)

def _gelu(x):
    return jax.nn.gelu(x, approximate=True)

def _silu(x):
    return jax.nn.silu(x)

def _sigmoid(x):
    return jax.nn.sigmoid(x)

def _layernorm(x, axis=-1, eps=1e-05):
    m = jnp.mean(x, axis=axis, keepdims=True)
    v = jnp.var(x, axis=axis, keepdims=True)
    return (x - m) / jnp.sqrt(v + eps)

def _scatter_add(tgt, idx, src, axis=0):
    return tgt.at[idx].add(src)

def _segment_sum(src, seg, n):
    return jax.ops.segment_sum(src, seg, n)
kernel_name = 'mk_adaln_d1_jaxref_r8_e5762d'

def setup_inputs(seed: int=0):
    np.random.seed(seed)
    _w = jnp.asarray

    def _L0_attn_setup():
        import jax, jax.numpy as jnp
        import numpy as np
        D_MODEL = 128
        N_LAYER = 4
        EXPAND = 2
        HEADDIM = 32
        D_STATE = 128
        D_CONV = 4
        NGROUPS = 1
        D_INNER = EXPAND * D_MODEL
        NHEADS = D_INNER // HEADDIM
        CONV_DIM = D_INNER + 2 * NGROUPS * D_STATE
        D_IN_PROJ = 2 * D_INNER + 2 * NGROUPS * D_STATE + NHEADS
        BATCH, SEQLEN = (4, 256)

        def _rmsnorm(x, w, eps=1e-05):
            return x * jax.lax.rsqrt(jnp.mean(x * x, axis=-1, keepdims=True) + eps) * w

        def _mamba2_layer(h, Wi, cw, cb, dtb, Alog, Dh, gw, Wo):
            B, L, _ = h.shape
            zxbcdt = h @ Wi
            z, xBC, dt = jnp.split(zxbcdt, [D_INNER, D_INNER + CONV_DIM], axis=-1)
            xp = jnp.pad(xBC, ((0, 0), (D_CONV - 1, 0), (0, 0)))
            conv = cb + sum((xp[:, k:k + L, :] * cw[:, k] for k in range(D_CONV)))
            xBC = jax.nn.silu(conv)
            xs, Bm, Cm = jnp.split(xBC, [D_INNER, D_INNER + D_STATE], axis=-1)
            xs = xs.reshape(B, L, NHEADS, HEADDIM)
            dt = jax.nn.softplus(dt + dtb)
            A = -jnp.exp(Alog)
            dA = jnp.exp(dt * A)
            dtx = dt[..., None] * xs

            def step(hs, inp):
                dA_t, dtx_t, B_t, C_t = inp
                hs = hs * dA_t[:, :, None, None] + dtx_t[..., None] * B_t[:, None, None, :]
                y = jnp.einsum('bhpn,bn->bhp', hs, C_t)
                return (hs, y)
            h0 = jnp.zeros((B, NHEADS, HEADDIM, D_STATE), h.dtype)
            _, ys = jax.lax.scan(step, h0, (dA.swapaxes(0, 1), dtx.swapaxes(0, 1), Bm.swapaxes(0, 1), Cm.swapaxes(0, 1)))
            y = ys.swapaxes(0, 1) + Dh[None, None, :, None] * xs
            y = y.reshape(B, L, D_INNER)
            y = _rmsnorm(y * jax.nn.silu(z), gw)
            return y @ Wo
        key = jax.random.key(seed)
        ks = jax.random.split(key, 8)
        x = jax.random.normal(ks[0], (BATCH, SEQLEN, D_MODEL), jnp.float32)
        s_in = 1.0 / np.sqrt(D_MODEL)
        s_out = 1.0 / np.sqrt(D_INNER)
        W_in = jax.random.normal(ks[1], (N_LAYER, D_MODEL, D_IN_PROJ), jnp.float32) * s_in
        conv_w = jax.random.normal(ks[2], (N_LAYER, CONV_DIM, D_CONV), jnp.float32) * 0.5
        conv_b = jnp.zeros((N_LAYER, CONV_DIM), jnp.float32)
        dt = jax.random.uniform(ks[3], (N_LAYER, NHEADS), jnp.float32, 0.001, 0.1)
        dt_bias = jnp.log(jnp.expm1(dt))
        A_log = jnp.log(jax.random.uniform(ks[4], (N_LAYER, NHEADS), jnp.float32, 1.0, 16.0))
        D = jnp.ones((N_LAYER, NHEADS), jnp.float32)
        gate_norm_w = jnp.ones((N_LAYER, D_INNER), jnp.float32)
        W_out = jax.random.normal(ks[5], (N_LAYER, D_INNER, D_MODEL), jnp.float32) * s_out
        block_norm_w = jnp.ones((N_LAYER, D_MODEL), jnp.float32)
        final_norm_w = jnp.ones((D_MODEL,), jnp.float32)
        return dict(x=x, W_in=W_in, conv_w=conv_w, conv_b=conv_b, dt_bias=dt_bias, A_log=A_log, D=D, gate_norm_w=gate_norm_w, W_out=W_out, block_norm_w=block_norm_w, final_norm_w=final_norm_w)
    _L0_attn_in = _L0_attn_setup()

    def _L0_ffn_setup():
        import jax, jax.numpy as jnp
        import numpy as np
        D, H, O, E, TOPK = (128, 512, 128, 8, 2)
        B, S = (4, 128)
        key = jax.random.key(seed)
        ks = jax.random.split(key, 12)
        std = 0.02
        return {'hidden_states': jax.random.normal(ks[0], (B, S, D), dtype=jnp.float32), 'norm_weight': jnp.ones((D,), dtype=jnp.float32), 'router_w': jax.random.normal(ks[1], (E, D), dtype=jnp.float32) * std, 'sw1': jax.random.normal(ks[2], (D, H), dtype=jnp.float32) * (1.0 / np.sqrt(D)), 'sb1': jnp.zeros((H,), dtype=jnp.float32), 'sw2': jax.random.normal(ks[3], (H, O), dtype=jnp.float32) * (1.0 / np.sqrt(H)), 'sb2': jnp.zeros((O,), dtype=jnp.float32), 'ew1': jax.random.normal(ks[4], (E, D, H), dtype=jnp.float32) * (1.0 / np.sqrt(D)), 'eb1': jnp.zeros((E, H), dtype=jnp.float32), 'ew2': jax.random.normal(ks[5], (E, H, O), dtype=jnp.float32) * (1.0 / np.sqrt(H)), 'eb2': jnp.zeros((E, O), dtype=jnp.float32)}
    _L0_ffn_in = _L0_ffn_setup()
    _L0_c = _w((lambda *s: np.random.randn(*s).astype(np.float32) * 0.05)(8, 128))
    _L0_wmod = _w((lambda *s: np.random.randn(*s).astype(np.float32) * 0.05)(128, 6 * 128) * 128 ** (-0.5))
    _d = {'L0_attn_x': _L0_attn_in['x'], 'L0_attn_W_in': _L0_attn_in['W_in'], 'L0_attn_conv_w': _L0_attn_in['conv_w'], 'L0_attn_conv_b': _L0_attn_in['conv_b'], 'L0_attn_dt_bias': _L0_attn_in['dt_bias'], 'L0_attn_A_log': _L0_attn_in['A_log'], 'L0_attn_D': _L0_attn_in['D'], 'L0_attn_gate_norm_w': _L0_attn_in['gate_norm_w'], 'L0_attn_W_out': _L0_attn_in['W_out'], 'L0_attn_block_norm_w': _L0_attn_in['block_norm_w'], 'L0_attn_final_norm_w': _L0_attn_in['final_norm_w'], 'L0_ffn_norm_weight': _L0_ffn_in['norm_weight'], 'L0_ffn_router_w': _L0_ffn_in['router_w'], 'L0_ffn_sw1': _L0_ffn_in['sw1'], 'L0_ffn_sb1': _L0_ffn_in['sb1'], 'L0_ffn_sw2': _L0_ffn_in['sw2'], 'L0_ffn_sb2': _L0_ffn_in['sb2'], 'L0_ffn_ew1': _L0_ffn_in['ew1'], 'L0_ffn_eb1': _L0_ffn_in['eb1'], 'L0_ffn_ew2': _L0_ffn_in['ew2'], 'L0_ffn_eb2': _L0_ffn_in['eb2'], 'L0_c': _L0_c, 'L0_wmod': _L0_wmod}
    _x0 = _d['L0_attn_x']
    _d['L0_attn_x'] = jax.random.normal(jax.random.fold_in(jax.random.key(seed), 1), (8, 512, 128), dtype=_x0.dtype)
    del _x0
    return _d

def reference(L0_attn_x, L0_attn_W_in, L0_attn_conv_w, L0_attn_conv_b, L0_attn_dt_bias, L0_attn_A_log, L0_attn_D, L0_attn_gate_norm_w, L0_attn_W_out, L0_attn_block_norm_w, L0_attn_final_norm_w, L0_ffn_norm_weight, L0_ffn_router_w, L0_ffn_sw1, L0_ffn_sb1, L0_ffn_sw2, L0_ffn_sb2, L0_ffn_ew1, L0_ffn_eb1, L0_ffn_ew2, L0_ffn_eb2, L0_c, L0_wmod):

    def _L0_attn_ref(x, W_in, conv_w, conv_b, dt_bias, A_log, D, gate_norm_w, W_out, block_norm_w, final_norm_w):
        import jax, jax.numpy as jnp
        import numpy as np
        D_MODEL = 128
        N_LAYER = 4
        EXPAND = 2
        HEADDIM = 32
        D_STATE = 128
        D_CONV = 4
        NGROUPS = 1
        D_INNER = EXPAND * D_MODEL
        NHEADS = D_INNER // HEADDIM
        CONV_DIM = D_INNER + 2 * NGROUPS * D_STATE
        D_IN_PROJ = 2 * D_INNER + 2 * NGROUPS * D_STATE + NHEADS
        BATCH, SEQLEN = (4, 256)

        def _rmsnorm(x, w, eps=1e-05):
            return x * jax.lax.rsqrt(jnp.mean(x * x, axis=-1, keepdims=True) + eps) * w

        def _mamba2_layer(h, Wi, cw, cb, dtb, Alog, Dh, gw, Wo):
            B, L, _ = h.shape
            zxbcdt = h @ Wi
            z, xBC, dt = jnp.split(zxbcdt, [D_INNER, D_INNER + CONV_DIM], axis=-1)
            xp = jnp.pad(xBC, ((0, 0), (D_CONV - 1, 0), (0, 0)))
            conv = cb + sum((xp[:, k:k + L, :] * cw[:, k] for k in range(D_CONV)))
            xBC = jax.nn.silu(conv)
            xs, Bm, Cm = jnp.split(xBC, [D_INNER, D_INNER + D_STATE], axis=-1)
            xs = xs.reshape(B, L, NHEADS, HEADDIM)
            dt = jax.nn.softplus(dt + dtb)
            A = -jnp.exp(Alog)
            dA = jnp.exp(dt * A)
            dtx = dt[..., None] * xs

            def step(hs, inp):
                dA_t, dtx_t, B_t, C_t = inp
                hs = hs * dA_t[:, :, None, None] + dtx_t[..., None] * B_t[:, None, None, :]
                y = jnp.einsum('bhpn,bn->bhp', hs, C_t)
                return (hs, y)
            h0 = jnp.zeros((B, NHEADS, HEADDIM, D_STATE), h.dtype)
            _, ys = jax.lax.scan(step, h0, (dA.swapaxes(0, 1), dtx.swapaxes(0, 1), Bm.swapaxes(0, 1), Cm.swapaxes(0, 1)))
            y = ys.swapaxes(0, 1) + Dh[None, None, :, None] * xs
            y = y.reshape(B, L, D_INNER)
            y = _rmsnorm(y * jax.nn.silu(z), gw)
            return y @ Wo
        h = x
        for l in range(N_LAYER):
            h = h + _mamba2_layer(_rmsnorm(h, block_norm_w[l]), W_in[l], conv_w[l], conv_b[l], dt_bias[l], A_log[l], D[l], gate_norm_w[l], W_out[l])
        return _rmsnorm(h, final_norm_w)

    def _L0_ffn_ref(hidden_states, norm_weight, router_w, sw1, sb1, sw2, sb2, ew1, eb1, ew2, eb2):
        import jax, jax.numpy as jnp
        import numpy as np
        D, H, O, E, TOPK = (128, 512, 128, 8, 2)
        B, S = (4, 128)
        b, s, d = hidden_states.shape
        var = jnp.mean(jnp.square(hidden_states), axis=-1, keepdims=True)
        normed = hidden_states * jax.lax.rsqrt(var + 1e-08) * norm_weight
        shared = jnp.maximum(normed @ sw1 + sb1, 0.0) @ sw2 + sb2
        flat = normed.reshape(-1, d)
        T = flat.shape[0]
        probs = jax.nn.sigmoid(flat @ router_w.T)
        scores, idx = jax.lax.top_k(probs, TOPK)
        w = scores / (jnp.sum(scores, axis=-1, keepdims=True) + 1e-06)
        comb = jnp.zeros((T, E), dtype=flat.dtype)
        comb = comb.at[jnp.arange(T)[:, None], idx].add(w)
        h = jnp.maximum(jnp.einsum('td,edh->teh', flat, ew1) + eb1[None, :, :], 0.0)
        eo = jnp.einsum('teh,eho->teo', h, ew2) + eb2[None, :, :]
        routed = jnp.einsum('teo,te->to', eo, comb)
        return shared + routed.reshape(b, s, -1)
    x = L0_attn_x
    mod = (_silu(L0_c) @ L0_wmod).reshape(L0_c.shape[0], 6, 1, -1)
    sa, ca, ga, sb, cb, gb = (mod[:, 0], mod[:, 1], mod[:, 2], mod[:, 3], mod[:, 4], mod[:, 5])
    ga = (2 * (ga >= 0) - 1) * jnp.maximum(jnp.abs(ga), 0.25)
    gb = (2 * (gb >= 0) - 1) * jnp.maximum(jnp.abs(gb), 0.25)
    h = _layernorm(x, axis=-1) * (1 + ca) + sa
    x = x + ga * _L0_attn_ref(h, L0_attn_W_in, L0_attn_conv_w, L0_attn_conv_b, L0_attn_dt_bias, L0_attn_A_log, L0_attn_D, L0_attn_gate_norm_w, L0_attn_W_out, L0_attn_block_norm_w, L0_attn_final_norm_w)
    h = _layernorm(x, axis=-1) * (1 + cb) + sb
    x = x + gb * _L0_ffn_ref(h, L0_ffn_norm_weight, L0_ffn_router_w, L0_ffn_sw1, L0_ffn_sb1, L0_ffn_sw2, L0_ffn_sb2, L0_ffn_ew1, L0_ffn_eb1, L0_ffn_ew2, L0_ffn_eb2)
    return x

_drawn_inputs = setup_inputs


def setup_inputs(seed=0):
    import zlib

    import numpy as np

    out = dict(_drawn_inputs(seed))
    spreads = {'L0_attn_conv_b': (0.0, 0.1),
     'L0_attn_D': (1.0, 0.2),
     'L0_attn_gate_norm_w': (1.0, 0.2),
     'L0_attn_block_norm_w': (1.0, 0.2),
     'L0_attn_final_norm_w': (1.0, 0.2),
     'L0_ffn_norm_weight': (1.0, 0.2),
     'L0_ffn_sb1': (0.0, 0.462),
     'L0_ffn_sb2': (0.0, 0.302),
     'L0_ffn_eb1': (0.0, 0.686),
     'L0_ffn_eb2': (0.0, 0.48)}
    factors = {}
    for name, (base, spread) in spreads.items():
        noise = np.random.default_rng([zlib.crc32(name.encode()), seed]).standard_normal(out[name].shape)
        drawn = base * np.exp(spread * noise) if base else spread * noise
        out[name] = jnp.asarray(drawn.astype(out[name].dtype))
    for name, factor in factors.items():
        out[name] = (out[name] * factor).astype(out[name].dtype)
    return out
```

```python
import concourse.bass as bass
from concourse import mybir
from contextlib import ExitStack

F32 = mybir.dt.float32
BF16 = mybir.dt.bfloat16
F32R = mybir.dt.float32r
ACT = mybir.ActivationFunctionType
ALU = mybir.AluOpType
AX = mybir.AxisListType

P = 128
NB, L, DM = 8, 512, 128
NL, DI, NH, HD, DS = 4, 256, 8, 32, 128
CH = 128
NC = L // CH
NE, HE = 8, 512
STEPS = NL * NB
EXPLN = "natural_log_exp_and_others"

C_WDT, C_BNW, C_CW, C_CB, C_DTB, C_NA, C_D, C_GW = 0, 32, 33, 49, 53, 54, 55, 57
NPAR = 60
NX = NE + 1
HT = HE // P
F_B1, F_B2, F_NW, F_FW, F_RW = 0, NX * HT, NX * HT + NX, NX * HT + NX + 1, NX * HT + NX + 2
NPAR2 = F_RW + NE
K_ID, K_MASK, K_SEL, K_SELX = 0, 128, 640, 1664
K_SELD, K_M1, K_M2, K_EPS5, K_EPS8, K_TRI = 1920, 1952, 1953, 1954, 1955, 1956
NCST = K_TRI + 64
W_COL = [DI, DI + P, 2 * DI, 2 * DI + DS, 0, P]
SILU_TURN = [2, 3, 0, 1, 4, 5]
X0, X1, TB, TC = 0, 1, 2, 3


def wait(eng, sem, value):
    if isinstance(value, int) and value <= 0:
        return
    eng.wait_ge(sem, value)


def build(nc, x, w_in, w_out, par, cst, c_t, wmod, par2, w1, w2, out):
    ctx = ExitStack()
    with ctx:
        scope = [ctx]

        def sb(name, cols, dt=F32, parts=P):
            return scope[0].enter_context(nc.sbuf_tensor(name, [parts, cols], dt))

        def sem(name):
            return ctx.enter_context(nc.semaphore(name))

        bank = [ctx.enter_context(nc.psum_tensor(f"bank{i}", [P, 512], F32)) for i in range(8)]

        h = sb("h", NB * L)
        xT = sb("xT", NB * L)
        PAR = sb("PAR", NL * NPAR)
        CST = sb("CST", NCST)
        MOD = sb("MOD", 48)
        ident = CST[:, K_ID:K_ID + P]
        eps5, eps8 = CST[:, K_EPS5:K_EPS5 + 1], CST[:, K_EPS8:K_EPS8 + 1]
        mean128 = sb("mean128", P)
        mean256 = sb("mean256", P)
        idb, onesb = sb("idb", P, BF16), sb("onesb", P, BF16)
        maskb = sb("maskb", 512, BF16)
        selb, nselb = sb("selb", 1024, BF16), sb("nselb", 1024, BF16)
        selxb = sb("selxb", 256, BF16)
        ones_row = sb("ones_row", P)
        PAR2 = sb("PAR2", NPAR2)
        RAW = [sb(f"RAW{w}", NX * HE) for w in range(2)]
        scope[0] = ExitStack()
        WA = [sb(f"WA{t}", P) for t in range(6)]
        WDT = sb("WDT", 32)
        WO_raw, WO = sb("WO_raw", 2 * DM), sb("WO", 2 * DM)
        sqh, lnm, rB, hn = sb("sqh", L), sb("lnm", L), sb("rB", L), sb("hn", L)
        cv = [sb(f"cv{t}", L) for t in range(4)]
        xbc = [sb(f"xbc{t}", L) for t in range(4)]
        zs = sb("zs", 2 * 2 * L)
        u, ax, ex, ln1 = sb("u", P), sb("ax", P), sb("ex", P), sb("ln1", P)
        dt_, dA, cum, r1, r2 = sb("dt_", P), sb("dA", P), sb("cum", P), sb("r1", P), sb("r2", P)
        p0, p1, p2 = sb("p0", P, BF16), sb("p1", P, BF16), sb("p2", P, BF16)
        ecs, wdec, spend = sb("ecs", P), sb("wdec", P), sb("spend", 32, BF16)
        P4 = sb("P4", L, BF16, parts=32)
        DTW, dec = sb("DTW", 2 * P), sb("dec", 32)
        xtok = [sb(f"xtok{c}", 384) for c in range(NC)]
        dtx = [sb(f"dtx{c}", DI) for c in range(NC)]
        xw = [sb(f"xw{c}", DI) for c in range(NC - 1)]
        E = [sb(f"E{g}", 512) for g in range(2)]
        M = [sb(f"M{g}", 512) for g in range(2)]
        S = [None] + [sb(f"S{c}", DI) for c in range(1, NC)]
        stmp = sb("stmp", DI)
        E2 = [sb(f"E2_{t}", 384) for t in range(2)]
        yt = [sb(f"yt{t}", L) for t in range(2)]
        ti = [sb(f"ti{t}", 384) for t in range(2)]
        y2 = [sb(f"y2_{t}", L) for t in range(2)]
        sqy = [sb(f"sqy{t}", L) for t in range(2)]
        lnY, rY, o_sb = sb("lnY", L), sb("rY", L), sb("o_sb", L)
        xin = sb("xin", NB * L)
        bst, mv, rstd, lnv = sb("bst", 32 * 6), sb("mv", 64), sb("rstd", 32), sb("lnv", 32)
        xn = sb("xn", 2 * L)
        cT, cS, wm = sb("cT", NB), sb("cS", NB), sb("wm", 6 * DM)
        gsg = sb("gsg", 16)
        scope[0].close()

        scope[0] = ctx
        WH = [sb(f"WH{w}", NX * HE, F32R) for w in range(2)]
        WL = [sb(f"WL{w}", NX * HE, F32R) for w in range(2)]
        nH, nL = sb("nH", 2 * L, F32R), sb("nL", 2 * L, F32R)
        hr = [RAW[0][:, t * L:(t + 1) * L] for t in range(HT)]
        hH = [sb(f"hH{t}", L, F32R) for t in range(HT)]
        hL = [sb(f"hL{t}", L, F32R) for t in range(HT)]
        sqf, lnf, rf, nT = sb("sqf", L), sb("lnf", L), sb("rf", L), sb("nT", L)
        pr, prx, rnk, pm, cmb, cr = [sb(n, 32) for n in ("pr", "prx", "rnk", "pm", "cmb", "cr")]
        cgt, ceq = sb("cgt", 256), sb("ceq", 256)
        csum = sb("csum", 4)
        C3 = sb("C3", P, BF16)
        CT = sb("CT", L, BF16, parts=32)
        eb, ec, acc, fo, ob = [RAW[1][:, t * L:(t + 1) * L] for t in range(5)]
        gaf = sb("gaf", NB)

        s_cst, s_x, s_par, s_mod = sem("cst_in"), sem("x_in"), sem("par_in"), sem("mod_in")
        const_v, const_p = sem("const_v"), sem("const_p")
        bn_v, rstd_a, xn_v, xt_mm, xt_ev = sem("bn_v"), sem("rstd_a"), sem("xn_v"), sem("xt_mm"), sem("xt_ev")
        cs_a, mod_mm, mod_v = sem("cs_a"), sem("mod_mm"), sem("mod_v")
        wa = [sem(f"wa{t}") for t in range(6)]
        s_wo, p4_in = sem("wo_in"), sem("p4_in")
        wdt_a, hup, sqh_a, ms_mm, rb_a, hn_v = sem("wdt_a"), sem("hup"), sem("sqh_a"), sem("ms_mm"), sem("rb_a"), sem("hn_v")
        dt_mm, pj_mm, tap_v, silu_a, dtc_v, dta_a, tr_mm = sem("dt_mm"), sem("pj_mm"), sem("tap_v"), sem("silu_a"), sem("dtc_v"), sem("dta_a"), sem("tr_mm")
        g_mm, t_mm, t_ev, d_mm, e_a, m_v, y_mm = sem("g_mm"), sem("t_mm"), sem("t_ev"), sem("d_mm"), sem("e_a"), sem("m_v"), sem("y_mm")
        px_p, st_mm, s_v, e2_mm, e2_a, yi_mm = sem("px_p"), sem("st_mm"), sem("s_v"), sem("e2_mm"), sem("e2_a"), sem("yi_mm")
        dx_v, fin_v, fin_p, wos_a = sem("dx_v"), sem("fin_v"), sem("fin_p"), sem("wos_a")
        sq_a, ss_mm, ry_a, out_mm, o_v = sem("sq_a"), sem("ss_mm"), sem("ry_a"), sem("out_mm"), sem("o_v")
        s_ffw, s_out = sem("ffw_in"), sem("out_done")
        wh_a, wl_v, c3_v = sem("wh_a"), sem("wl_v"), sem("c3_v")
        pa, pv, pm_mm = sem("prep_a"), sem("prep_v"), sem("prep_mm")
        u_mm, r_a, r_v, hi_a, lo_v, dn_mm = sem("u_mm"), sem("r_a"), sem("r_v"), sem("hi_a"), sem("lo_v"), sem("dn_mm")
        cb_mm, eo_a, ec_v, acc_p, fo_v, ft_mm, ob_a = [sem(n) for n in ("cb_mm", "eo_a", "ec_v", "acc_p", "fo_v", "ft_mm", "ob_a")]

        def steps(eng, body):
            body(0, A=True, B=False, C=False, N=True)
            body(1, A=True, B=True, C=False, N=True)
            body(2, A=True, B=True, C=True, N=True)
            with eng.Fori(3, STEPS - 1) as k:
                body(k, A=True, B=True, C=True, N=True)
            body(STEPS - 1, A=True, B=True, C=True, N=False)
            body(STEPS, A=False, B=True, C=True, N=False)
            body(STEPS + 1, A=False, B=False, C=True, N=False)

        def blocks(eng, body):
            body(0, prep=True)
            body(1, prep=True)
            with eng.Fori(2, NB - 1) as b:
                body(b, prep=True)
            body(NB - 1, prep=False)

        block = ctx.enter_context(nc.Block())

        @block.sync
        def _(sp):
            def rows(src, at, n):
                return src[bass.ds(at, P * n)].rearrange("(p n) -> p n", n=n)

            sp.dma_start(CST[:, :], cst).then_inc(s_cst, 16)
            for q in range(4):
                sp.dma_start(xin[:, q * 1024:(q + 1) * 1024].rearrange("p (n d) -> p n d", d=DM),
                             x[q * 1024:(q + 1) * 1024, :].rearrange("(n p) d -> p n d", p=P)).then_inc(s_x, 16)
            sp.dma_start(cT[:, :], c_t).then_inc(s_mod, 16)
            sp.dma_start(wm[:, :], wmod).then_inc(s_mod, 16)
            sp.dma_start(PAR[:, :], par).then_inc(s_par, 16)
            for t in range(6):
                sp.dma_start(WA[t][:, :], rows(w_in, t * P * P, P)).then_inc(wa[t], 16)
            sp.dma_start(PAR2[:, :], par2).then_inc(s_ffw, 16)
            for w, src in enumerate((w1, w2)):
                sp.dma_start(RAW[w][:, :], src).then_inc(s_ffw, 16)

            def body(k, A, B, C, N):
                if B:
                    j = k - 1
                    at_j = sp.snap(j // NB * (2 * DM * P))
                    wait(sp, wos_a, 2 * j)
                    sp.dma_start(WO_raw[:, :], rows(w_out, at_j, 2 * DM)).then_inc(s_wo, 16)
                if N:
                    at = [sp.snap((k + 1) // NB * (6 * P * P) + t * P * P) for t in range(6)]
                for t in range(6):
                    if N:
                        wait(sp, pj_mm, 6 * k + t + 1)
                        sp.dma_start(WA[t][:, :], rows(w_in, at[t], P)).then_inc(wa[t], 16)
                if A:
                    if B:
                        wait(sp, e2_mm, 2 * k)
                    wait(sp, dtc_v, 11 * k + 9)
                    for c in range(NC):
                        sp.dma_start(P4[:, c * CH:(c + 1) * CH], p2[32 * c:32 * c + 32, :]).then_inc(p4_in, 16)

            steps(sp, body)

            sp.wait_ge(s_ffw, 48)

            def store(b):
                first_row = sp.snap(b * L)
                sp.wait_ge(ob_a, b + 1)
                sp.dma_start(out[bass.ds(first_row, L), :].rearrange("(s p) d -> p s d", p=P),
                             ob.rearrange("p (s d) -> p s d", s=4)).then_inc(s_out, 16)

            store(0)
            with sp.Fori(1, NB) as b:
                store(b)
            sp.wait_ge(s_out, 16 * NB)

        @block.tensor
        def _(pe):
            mm = nc.tensor.matmul
            pe.wait_ge(cs_a, 1)
            pe.wait_ge(s_mod, 32)
            for i in range(6):
                ins = mm(bank[4][:, 8 * i:8 * i + 8], wm[:, i * DM:(i + 1) * DM], cS[:, :], start=True, stop=True)
            ins.then_inc(mod_mm, 1)
            pe.wait_ge(s_cst, 16)

            def turn_input(b):
                for half, free in enumerate((hup, xt_ev)):
                    wait(pe, xn_v, 3 * b + 2 + half)
                    wait(pe, free, b)
                    for n in range(4):
                        ins = nc.tensor.transpose(bank[half][:, n * P:(n + 1) * P],
                                                  xn[:, half * L + n * P:half * L + (n + 1) * P], ident)
                    ins.then_inc(xt_mm, 1)

            turn_input(0)
            with pe.Fori(1, NB) as b:
                turn_input(b)

            def body(k, A, B, C, N):
                j, i2 = k - 1, k - 2
                if A:
                    wait(pe, hn_v, k + 1)
                    wait(pe, wdt_a, k + 1)
                    wait(pe, dta_a, 6 * k)
                    for c in range(NC):
                        ins = mm(bank[4][32 * c:32 * c + 32, 0:CH], WDT[:, :], hn[:, c * CH:(c + 1) * CH],
                                 start=True, stop=True, tile_position=(0, 32 * c))
                    ins.then_inc(dt_mm, 1)

                def project(t):
                    wait(pe, wa[t], 16 * (k + 1))
                    if t < 2:
                        wait(pe, silu_a, 6 * k - 1 + t)
                    else:
                        wait(pe, tap_v, 16 * k + 4 * (t - 1))
                    mm(bank[t % 2][:, :], WA[t][:, :], hn[:, :], start=True, stop=True).then_inc(pj_mm, 1)

                if A:
                    project(0)
                    project(1)
                if C:
                    wait(pe, sq_a, 2 * (i2 + 1))
                    wait(pe, fin_v, 4 * (i2 + 1))
                    mm(bank[3][:, :], mean256[:, :], sqy[0][:, :], start=True, stop=False)
                    mm(bank[3][:, :], mean256[:, :], sqy[1][:, :], start=False, stop=True).then_inc(ss_mm, 1)
                    wait(pe, wos_a, 2 * (i2 + 1))
                    mm(bank[2][:, :], WO[:, 0:DM], y2[0][:, :], start=True, stop=False)
                    mm(bank[2][:, :], WO[:, DM:2 * DM], y2[1][:, :], start=False, stop=True).then_inc(out_mm, 1)

                def turn(c):
                    if c == 0:
                        wait(pe, silu_a, 6 * j + 4)
                        if A:
                            wait(pe, dtc_v, 11 * k + 1)
                        else:
                            wait(pe, dta_a, 6 * k)
                    elif c == 1:
                        if C:
                            wait(pe, ry_a, 2 * i2 + 1)
                    else:
                        wait(pe, t_ev, 4 * j + c - 1)
                    dst = bank[4 if c % 2 == 0 else 3]
                    for n, t in enumerate((X0, X1, TB)):
                        ins = nc.tensor.transpose(dst[:, n * P:(n + 1) * P], xbc[t][:, c * CH:(c + 1) * CH], ident)
                    ins.then_inc(t_mm, 1)

                def decays(c):
                    for g in range(2):
                        i = 2 * c + g
                        if i >= 2:
                            wait(pe, e_a, 8 * j + i - 1)
                        elif i == 0:
                            wait(pe, p4_in, 64 * (j + 1))
                            if C:
                                wait(pe, o_v, i2 + 1)
                        else:
                            wait(pe, t_ev, 4 * j + 4)
                        dst = bank[2 + g]
                        pc = P4[:, c * CH:(c + 1) * CH]
                        mm(dst[:, :], idb[:, :], maskb[:, :], start=True, stop=False)
                        mm(dst[:, :], pc, nselb[0:32, g * 512:(g + 1) * 512], start=False, stop=False)
                        for n in range(4):
                            hh = 4 * g + n
                            ins = mm(dst[:, n * P:(n + 1) * P], selb[0:32, hh * P:(hh + 1) * P], pc,
                                     start=False, stop=(n == 3))
                        ins.then_inc(d_mm, 1)

                def within(c):
                    wait(pe, m_v, 8 * j + 2 * c + 2)
                    wait(pe, px_p, 7 * j + 2 * c + 1)
                    if c == 0:
                        wait(pe, fin_v, 4 * j - 1)
                    for hh in range(NH):
                        q = 32 * (hh % 4)
                        ins = mm(bank[6 + hh // 4][q:q + 32, c * CH:(c + 1) * CH], dtx[c][:, hh * HD:(hh + 1) * HD],
                                 M[hh // 4][:, (hh % 4) * CH:(hh % 4 + 1) * CH], start=True, stop=True,
                                 tile_position=(0, q))
                    ins.then_inc(y_mm, 1)

                if B:
                    wait(pe, silu_a, 6 * j + 2)
                    wait(pe, e2_a, 2 * j)
                    for c in range(NC):
                        cs = slice(c * CH, (c + 1) * CH)
                        ins = mm(bank[5][:, cs], xbc[TB][:, cs], xbc[TC][:, cs], start=True, stop=True)
                    ins.then_inc(g_mm, 1)
                    for c in range(NC):
                        turn(c)
                    decays(0)
                    decays(1)
                if A:
                    project(2)
                if B:
                    within(0)
                    decays(2)
                if A:
                    project(3)
                if B:
                    within(1)
                    decays(3)
                    within(2)
                    wait(pe, px_p, 7 * j + 4)
                    wait(pe, t_ev, 4 * j + 4)
                    mm(bank[4][:, 0:DI], xtok[0][:, 256:384], xw[0][:, :], start=True, stop=True)
                    mm(bank[4][:, DI:2 * DI], xtok[1][:, 256:384], xw[1][:, :], start=True, stop=True).then_inc(st_mm, 1)
                if A:
                    project(4)
                if B:
                    within(3)
                    wait(pe, s_v, 5 * j + 3)
                    wait(pe, px_p, 7 * j + 6)
                    mm(bank[4][:, 0:DI], xtok[2][:, 256:384], xw[2][:, :], start=True, stop=True).then_inc(st_mm, 1)
                if A:
                    project(5)
                if B:
                    wait(pe, m_v, 8 * j + 8)
                    mm(bank[5][:, 128:512], selxb[0:32, 0:P], P4[:, 128:512], start=True, stop=True).then_inc(e2_mm, 1)
                    wait(pe, s_v, 5 * j + 5)
                    for t in range(2):
                        wait(pe, e_a, 8 * j + 7 + t)
                        for c in range(1, NC):
                            cs = slice(c * CH, (c + 1) * CH)
                            ins = mm(bank[2 + t][:, cs], S[c][:, t * P:(t + 1) * P], xbc[TC][:, cs], start=True, stop=True)
                        ins.then_inc(yi_mm, 1)
                if A:
                    wait(pe, dtc_v, 11 * k + 10)
                    if B:
                        wait(pe, s_v, 5 * j + 5)
                    nc.tensor.transpose(bank[4][:, 0:P], dt_[:, :], ident)
                    nc.tensor.transpose(bank[4][:, P:2 * P], wdec[:, :], ident).then_inc(tr_mm, 1)
                if B:
                    wait(pe, e2_a, 2 * j + 1)
                    mm(bank[5][:, 128:512], selxb[0:32, P:2 * P], P4[:, 128:512], start=True, stop=True).then_inc(e2_mm, 1)
                if A:
                    wait(pe, dta_a, 6 * k + 5)
                    wait(pe, dtc_v, 11 * k + 11)
                    mm(bank[4][:, 256:288], onesb[:, :], spend[:, :], start=True, stop=True).then_inc(tr_mm, 1)
                if N:
                    n = k + 1
                    wait(pe, sqh_a, n + 1)
                    if B:
                        wait(pe, e2_a, 2 * j + 2)
                    mm(bank[5][:, :], mean128[:, :], sqh[:, :], start=True, stop=True).then_inc(ms_mm, 1)

            pe.wait_ge(const_v, 2)
            pe.wait_ge(sqh_a, 1)
            mm(bank[5][:, :], mean128[:, :], sqh[:, :], start=True, stop=True).then_inc(ms_mm, 1)
            pe.wait_ge(const_v, 9)
            steps(pe, body)

            def square_mean(n):
                wait(pe, pa, 11 * n + 1)
                wait(pe, pv, 25 * n)
                mm(bank[7][:, :], mean128[:, :], sqf[:, :], start=True, stop=True).then_inc(pm_mm, 1)

            def mean(n):
                wait(pe, pv, 25 * n + 2)
                wait(pe, pa, 11 * n + 2)
                mm(bank[7][:, :], mean128[:, :], xT[:, bass.ds(n * L, L)], start=True, stop=True).then_inc(pm_mm, 1)

            def variance(n):
                wait(pe, pa, 11 * n + 4)
                mm(bank[7][:, :], mean128[:, :], sqf[:, :], start=True, stop=True).then_inc(pm_mm, 1)

            def square_mean_2(n):
                wait(pe, pa, 11 * n + 7)
                mm(bank[7][:, :], mean128[:, :], sqf[:, :], start=True, stop=True).then_inc(pm_mm, 1)

            def logits(n):
                wait(pe, pv, 25 * n + 6)
                for c in range(4):
                    ins = mm(bank[7][:, 8 * c:8 * c + 8], nT[:, c * P:(c + 1) * P], PAR2[:, F_RW:F_RW + NE],
                             start=True, stop=True)
                ins.then_inc(pm_mm, 1)

            def turn_weights(n):
                wait(pe, pv, 25 * n + 24)
                for c in range(4):
                    ins = nc.tensor.transpose(bank[7][:, :].bitcast(BF16)[0:32, c * P:(c + 1) * P],
                                              C3[:, 32 * c:32 * c + 32], idb[:, :])
                ins.then_inc(pm_mm, 1)

            NEXT = {4: square_mean, 11: mean, 16: variance, 24: square_mean_2, 29: logits}
            OWN = {2: turn_weights}

            def body_ff(b, prep):
                first = isinstance(b, int) and b == 0
                for e in range(NX):
                    q = b * NX + e
                    down = not (first and e == 0)
                    ep = (e - 1) % NX
                    for t in range(HT):
                        if e == 0 and t == 0:
                            wait(pe, pv, 25 * b + 7)
                            wait(pe, pa, 11 * b + 10)
                        if first and t == 0:
                            wait(pe, wl_v, 2 * e + 1)
                        if t < HT - 1:
                            wait(pe, r_a, 3 * q - 2 + t)
                        else:
                            wait(pe, r_v, q)
                        w = slice(e * HE + t * P, e * HE + (t + 1) * P)
                        nh = nH[:, bass.ds((b % 2) * L, L)]
                        nl = nL[:, bass.ds((b % 2) * L, L)]
                        mm(bank[t][:, :], WH[0][:, w], nh, start=True, stop=False)
                        mm(bank[t][:, :], WH[0][:, w], nl, start=False, stop=False)
                        mm(bank[t][:, :], WL[0][:, w], nh, start=False, stop=True).then_inc(u_mm, 1)
                        if down:
                            down_product(q - 1, ep, t, first)
                        if prep and HT * e + t in NEXT:
                            NEXT[HT * e + t](b + 1)
                        if HT * e + t in OWN:
                            OWN[HT * e + t](b)
                    if down and ep > 0:
                        wait(pe, ec_v, b * NE - 1 if e == 0 else b * NE + ep - 1)
                        if ep == 1:
                            wait(pe, pv, 25 * b + 25)
                            wait(pe, ob_a, b)
                        mm(bank[6][:, :], selb[0:32, (ep - 1) * P:ep * P], CT[:, :],
                           start=True, stop=True).then_inc(cb_mm, 1)
                    if e == 1 and not first:
                        turn_out(b - 1)

            def down_product(q, e, t, first):
                if t == 0:
                    wait(pe, eo_a, q if e == 0 else q - 1)
                    if first:
                        wait(pe, wl_v, 2 * e + 2)
                wait(pe, lo_v, HT * q + t + 1)
                wait(pe, hi_a, HT * q + t + 1)
                w = slice(e * HE + t * P, e * HE + (t + 1) * P)
                dst = bank[4 + e % 2]
                mm(dst[:, :], WH[1][:, w], hH[t][:, :], start=(t == 0), stop=False)
                mm(dst[:, :], WH[1][:, w], hL[t][:, :], start=False, stop=False)
                mm(dst[:, :], WL[1][:, w], hH[t][:, :], start=False, stop=(t == HT - 1)).then_inc(dn_mm, 1)

            def turn_out(b):
                wait(pe, fo_v, b + 1)
                wait(pe, ec_v, NE * (b + 1))
                for c in range(4):
                    ins = nc.tensor.transpose(bank[6][:, c * P:(c + 1) * P], fo[:, c * P:(c + 1) * P], ident)
                ins.then_inc(ft_mm, 1)

            pe.wait_ge(s_ffw, 48)
            for piece in NEXT.values():
                piece(0)
            blocks(pe, body_ff)
            for t in range(HT):
                down_product(NB * NX - 1, NX - 1, t, False)
            wait(pe, ec_v, NB * NE - 1)
            mm(bank[6][:, :], selb[0:32, (NE - 1) * P:NE * P], CT[:, :],
               start=True, stop=True).then_inc(cb_mm, 1)
            turn_out(NB - 1)

        @block.scalar
        def _(act):
            f = nc.scalar.activation
            act.wait_ge(s_mod, 32)
            f(cS[:, :], cT[:, :], ACT.Silu).then_inc(cs_a, 1)
            nc.scalar.preload_act_table_set(EXPLN)
            act.wait_ge(s_par, 16)
            act.wait_ge(s_cst, 16)
            na = PAR[:, :].rearrange("p (l n) -> p l n", n=NPAR)[:, :, C_NA]
            f(na, na, ACT.Exp).then_inc(rstd_a, 1)
            act.wait_ge(bn_v, 64)
            f(lnv[:, :], mv[:, :].rearrange("p (n two) -> p n two", two=2)[:, :, 1], ACT.Ln, bias=eps5).then_inc(rstd_a, 1)
            act.wait_ge(rstd_a, 2)
            f(rstd[:, :], lnv[:, :], ACT.Exp, scale=-0.5).then_inc(rstd_a, 1)
            act.wait_ge(mod_v, 6)
            with act.Fori(0, NB) as b:
                hb = act.snap(b * L)
                act.wait_ge(xt_mm, 2 * b + 1)
                f(h[:, bass.ds(hb, L)], bank[0][:, :], ACT.Identity, scale=MOD[:, bass.ds(b + 8, 1)],
                  bias=MOD[:, bass.ds(b, 1)]).then_inc(hup, 1)
                act.wait_ge(xt_mm, 2 * b + 2)
                f(xT[:, bass.ds(hb, L)], bank[1][:, :], ACT.Copy).then_inc(xt_ev, 1)

            def norm_square(n):
                wait(act, dt_mm, n)
                f(WDT[:, :], PAR[:, bass.ds(n // NB * NPAR + C_WDT, 32)], ACT.Copy).then_inc(wdt_a, 1)
                wait(act, hup, n + 1)
                wait(act, ms_mm, n)
                f(sqh[:, :], h[:, bass.ds(n % NB * L, L)], ACT.Square).then_inc(sqh_a, 1)

            def norm_root(n):
                wait(act, ms_mm, n + 1)
                wait(act, hn_v, n)
                f(lnm[:, :], bank[5][:, :], ACT.Ln, bias=eps5).then_inc(rb_a, 1)
                wait(act, rb_a, 2 * n + 1)
                f(rB[:, :], lnm[:, :], ACT.Exp, scale=-0.5).then_inc(rb_a, 1)

            def body(k, A, B, C, N):
                j, i2 = k - 1, k - 2
                if C:
                    for t in range(2):
                        wait(act, fin_p, 4 * i2 + 2 + 2 * t)
                        wait(act, ss_mm, i2)
                        f(sqy[t][:, :], y2[t][:, :], ACT.Square).then_inc(sq_a, 1)
                nc.scalar.preload_act_table_set(EXPLN)
                if C:
                    wait(act, ss_mm, i2 + 1)
                    wait(act, o_v, i2)
                    f(lnY[:, :], bank[3][:, :], ACT.Ln, bias=eps5).then_inc(ry_a, 1)
                    wait(act, ry_a, 2 * i2 + 1)
                    f(rY[:, :], lnY[:, :], ACT.Exp, scale=-0.5).then_inc(ry_a, 1)
                if A:
                    wait(act, dtc_v, 11 * k + 1)
                    f(ax[:, :], u[:, :], ACT.Abs).then_inc(dta_a, 1)
                    wait(act, dta_a, 6 * k + 1)
                    f(ex[:, :], ax[:, :], ACT.Exp, scale=-1.0).then_inc(dta_a, 1)
                    wait(act, dta_a, 6 * k + 2)
                    f(ln1[:, :], ex[:, :], ACT.Ln, bias=1.0).then_inc(dta_a, 1)

                def decay_exp(i):
                    wait(act, d_mm, 8 * j + i + 1)
                    wait(act, m_v, 8 * j + i - 1)
                    f(E[i % 2][:, :], bank[2 + i % 2][:, :], ACT.Exp).then_inc(e_a, 1)

                if B:
                    for c in range(NC):
                        wait(act, t_mm, 4 * j + c + 1)
                        if c == 0:
                            wait(act, px_p, 7 * j)
                            wait(act, st_mm, 2 * j)
                        f(xtok[c][:, :], bank[4 if c % 2 == 0 else 3][:, 0:384], ACT.Copy).then_inc(t_ev, 1)
                    for i in range(4):
                        decay_exp(i)
                if A:
                    wait(act, dtc_v, 11 * k + 4)
                    f(ecs[:, :], cum[:, :], ACT.Exp, scale=-1.0, bias=cum[:, CH - 1:CH]).then_inc(dta_a, 1)
                if B:
                    for i in range(4, 6):
                        decay_exp(i)
                    wait(act, s_wo, 16 * (j + 1))
                    wait(act, out_mm, j)
                    gw = act.snap(j // NB * NPAR + C_GW)
                    for t in range(2):
                        f(WO[:, t * DM:(t + 1) * DM], WO_raw[:, t * DM:(t + 1) * DM], ACT.Copy,
                          scale=PAR[:, bass.ds(gw + t, 1)]).then_inc(wos_a, 1)
                    for i in range(6, 8):
                        decay_exp(i)
                if N:
                    norm_square(k + 1)
                if B:
                    wait(act, e2_mm, 2 * j + 1)
                    wait(act, fin_v, 4 * j)
                    f(E2[0][:, :], bank[5][:, 128:512], ACT.Exp).then_inc(e2_a, 1)
                if A:
                    wait(act, tr_mm, 2 * k + 1)
                    wait(act, px_p, 7 * k)
                    f(DTW[:, :], bank[4][:, 0:256], ACT.Copy).then_inc(dta_a, 1)
                if B:
                    wait(act, e2_mm, 2 * j + 2)
                    f(E2[1][:, :], bank[5][:, 128:512], ACT.Exp).then_inc(e2_a, 1)
                if A:
                    wait(act, tr_mm, 2 * k + 2)
                    wait(act, s_v, 5 * k)
                    f(dec[:, :], bank[4][:, 256:288], ACT.Exp).then_inc(dta_a, 1)
                if N:
                    norm_root(k + 1)
                if A:
                    for turn, t in enumerate((TB, TC, X0, X1)):
                        wait(act, tap_v, 16 * k + 4 * (t + 1))
                        if t == TB:
                            wait(act, t_mm, 4 * k)
                        elif t == TC:
                            wait(act, yi_mm, 2 * k)
                        else:
                            wait(act, dx_v, 2 * k)
                        f(xbc[t][:, :], cv[t][:, :], ACT.Silu).then_inc(silu_a, 1)
                    for t in range(2):
                        wait(act, pj_mm, 6 * k + 5 + t)
                        wait(act, fin_p, 4 * (k - 1))
                        f(zs[:, bass.ds((k % 2) * 2 * L + t * L, L)], bank[t][:, :], ACT.Silu).then_inc(silu_a, 1)

            norm_square(0)
            norm_root(0)
            steps(act, body)

            act.wait_ge(s_ffw, 48)
            act.wait_ge(hup, NB + STEPS)
            act.wait_ge(fin_v, 4 * STEPS)
            for e in range(NX):
                for w in range(2):
                    cs = slice(e * HE, (e + 1) * HE)
                    f(WH[w][:, cs], RAW[w][:, cs], ACT.Copy).then_inc(wh_a, 1)

            def root(n, count, eps):
                f(lnf[:, :], bank[7][:, :], ACT.Ln, bias=eps).then_inc(pa, 1)
                wait(act, pa, 11 * n + count)
                f(rf[:, :], lnf[:, :], ACT.Exp, scale=-0.5).then_inc(pa, 1)

            def square_h(n):
                f(sqf[:, :], h[:, bass.ds(n * L, L)], ACT.Square).then_inc(pa, 1)

            def root_h(n):
                wait(act, pm_mm, 6 * n + 1)
                root(n, 2, eps5)

            def square_x(n):
                wait(act, pv, 25 * n + 3)
                f(sqf[:, :], nT[:, :], ACT.Square).then_inc(pa, 1)

            def root_x(n):
                wait(act, pm_mm, 6 * n + 3)
                root(n, 5, eps5)

            def square_m(n):
                wait(act, pv, 25 * n + 5)
                f(sqf[:, :], nT[:, :], ACT.Square).then_inc(pa, 1)

            def root_m(n):
                wait(act, pm_mm, 6 * n + 4)
                root(n, 8, eps8)

            def halve(n):
                wait(act, pv, 25 * n + 6)
                f(nH[:, bass.ds((n % 2) * L, L)], nT[:, :], ACT.Copy).then_inc(pa, 1)

            def exp_logits(n):
                wait(act, pm_mm, 6 * n + 5)
                f(pr[:, :], bank[7][:, 0:32], ACT.Exp, scale=-1.0).then_inc(pa, 1)

            NEXT = {2: square_h, 6: root_h, 14: square_x, 18: root_x, 22: square_m, 26: root_m, 28: halve, 31: exp_logits}

            def finish(q, e):
                wait(act, dn_mm, HT * (q + 1))
                if e == 0:
                    f(acc, bank[4][:, :], ACT.Identity, bias=PAR2[:, F_B2:F_B2 + 1]).then_inc(eo_a, 1)
                else:
                    f(eb, bank[4 + e % 2][:, :], ACT.Identity,
                      bias=PAR2[:, F_B2 + e:F_B2 + e + 1]).then_inc(eo_a, 1)

            def body_ff(b, prep):
                first = isinstance(b, int) and b == 0
                for e in range(NX):
                    q = b * NX + e
                    for t in range(HT):
                        if t < HT - 1:
                            wait(act, u_mm, HT * q + t + 1)
                            wait(act, lo_v, HT * (q - 1) + t + 1)
                            f(hr[t], bank[t][:, :], ACT.Relu,
                              bias=PAR2[:, F_B1 + HT * e + t:F_B1 + HT * e + t + 1]).then_inc(r_a, 1)
                            wait(act, r_a, 3 * q + t + 1)
                        else:
                            wait(act, r_v, q + 1)
                        wait(act, dn_mm, HT * (q - 1) + t + 1)
                        f(hH[t][:, :], hr[t], ACT.Copy).then_inc(hi_a, 1)
                        if prep and HT * e + t in NEXT:
                            NEXT[HT * e + t](b + 1)
                    if not (first and e == 0):
                        ep = (e - 1) % NX
                        if ep == 0:
                            wait(act, fo_v, b)
                        elif ep == 1:
                            if not first:
                                wait(act, ec_v, NE * b)
                        else:
                            wait(act, ec_v, NE * b + ep - 1 if e > 0 else NE * b - 1)
                        finish(q - 1, ep)
                    if e == 2 and not first:
                        copy_out(b - 1)

            def copy_out(b):
                wait(act, ft_mm, b + 1)
                wait(act, s_out, 16 * b)
                f(ob, bank[6][:, :], ACT.Copy).then_inc(ob_a, 1)

            for piece in NEXT.values():
                piece(0)
            blocks(act, body_ff)
            wait(act, ec_v, NE * NB - 1)
            finish(NB * NX - 1, NX - 1)
            copy_out(NB - 1)

        @block.vector
        def _(dve):
            tt, ts, stt = nc.vector.tensor_tensor, nc.vector.tensor_scalar, nc.vector.scalar_tensor_tensor
            cp = nc.vector.tensor_copy
            nc.vector.memset(mean128[:, :], 1.0 / DM).then_inc(const_v, 1)
            nc.vector.memset(mean256[:, :], 1.0 / DI).then_inc(const_v, 1)
            nc.vector.memset(ones_row[:, :], 1.0).then_inc(const_v, 1)
            nc.vector.memset(onesb[:, :], 1.0).then_inc(const_v, 1)
            dve.wait_ge(s_cst, 16)
            cp(idb[:, :], ident).then_inc(const_v, 1)
            cp(maskb[:, :], CST[:, K_MASK:K_MASK + 512]).then_inc(const_v, 1)
            cp(selb[:, :], CST[:, K_SEL:K_SEL + 1024]).then_inc(const_v, 1)
            ts(nselb[:, :], CST[:, K_SEL:K_SEL + 1024], -1.0, None, ALU.mult).then_inc(const_v, 1)
            cp(selxb[:, :], CST[:, K_SELX:K_SELX + 256]).then_inc(const_v, 1)
            dve.wait_ge(s_x, 64)
            with dve.Fori(0, 32) as n:
                nc.vector.bn_stats(bst[:, bass.ds(n * 6, 6)], xin[:, bass.ds(n * P, P)]).then_inc(bn_v, 1)
            dve.wait_ge(bn_v, 32)
            for n in range(32):
                nc.vector.bn_aggr(mv[:, 2 * n:2 * n + 2], bst[:, 6 * n:6 * n + 6]).then_inc(bn_v, 1)
            dve.wait_ge(mod_mm, 1)
            dve.wait_ge(rstd_a, 1)
            cp(MOD[:, :], bank[4][:, 0:48]).then_inc(mod_v, 1)
            ts(PAR[:, :].rearrange("p (l n) -> p l n", n=NPAR)[:, :, C_NA],
               PAR[:, :].rearrange("p (l n) -> p l n", n=NPAR)[:, :, C_NA], -1.0, None, ALU.mult).then_inc(const_p, 1)
            dve.wait_ge(mod_v, 1)
            m3 = MOD[:, :].rearrange("p (a i b) -> p a i b", a=2, i=3)
            g2 = gsg[:, :].rearrange("p (a b) -> p a b", a=2)
            ts(m3[:, :, 1, :], m3[:, :, 1, :], 1.0, None, ALU.add).then_inc(mod_v, 1)
            ts(g2, m3[:, :, 2, :], 0.0, 2.0, ALU.is_ge, ALU.mult).then_inc(mod_v, 1)
            dve.wait_ge(mod_v, 3)
            ts(g2, g2, -1.0, None, ALU.add).then_inc(mod_v, 1)
            dve.wait_ge(mod_v, 4)
            tt(m3[:, :, 2, :], m3[:, :, 2, :], g2, ALU.mult).then_inc(mod_v, 1)
            dve.wait_ge(mod_v, 5)
            stt(out=m3[:, :, 2, :], in0=m3[:, :, 2, :], scalar=0.25, in1=g2, op0=ALU.max, op1=ALU.mult).then_inc(mod_v, 1)
            dve.wait_ge(rstd_a, 3)
            mvv = mv[:, :].rearrange("p (n two) -> p n two", two=2)

            def normalise(b):
                xb = xin[:, bass.ds(b * L, L)]
                xnv = xn[:, 0:L].rearrange("p (n d) -> p n d", d=DM)
                mean = mv[:, bass.ds(b * 8, 8)].rearrange("p (n two) -> p n two", two=2)[:, :, 0:1].to_broadcast([P, 4, DM])
                rs = rstd[:, bass.ds(b * 4, 4)].unsqueeze(2).to_broadcast([P, 4, DM])
                wait(dve, xt_mm, 2 * b)
                tt(xnv, xb.rearrange("p (n d) -> p n d", d=DM), mean, ALU.subtract).then_inc(xn_v, 1)
                wait(dve, xn_v, 3 * b + 1)
                tt(xnv, xnv, rs, ALU.mult).then_inc(xn_v, 1)
                cp(xn[:, L:2 * L], xb).then_inc(xn_v, 1)

            normalise(0)
            with dve.Fori(1, NB) as b:
                normalise(b)

            def body(k, A, B, C, N):
                j, i2 = k - 1, k - 2
                if A:
                    pk = dve.snap(k // NB * NPAR)
                    wait(dve, dt_mm, k + 1)
                    ts(u[:, :], bank[4][:, 0:CH], PAR[:, bass.ds(pk + C_DTB, 1)], None, ALU.add).then_inc(dtc_v, 1)

                def convolve(t):
                    cw = pk + C_CW + 4 * t
                    wait(dve, pj_mm, 6 * k + t + 1)
                    wait(dve, silu_a, 6 * (k - 1) + SILU_TURN[t] + 1)
                    src = bank[t % 2]
                    ts(cv[t][:, :], src[:, :], PAR[:, bass.ds(cw + 3, 1)], PAR[:, bass.ds(pk + C_CB + t, 1)],
                       ALU.mult, ALU.add).then_inc(tap_v, 1)
                    for s in range(1, 4):
                        wait(dve, tap_v, 16 * k + 4 * t + s)
                        stt(out=cv[t][:, s:L], in0=src[:, 0:L - s], scalar=PAR[:, bass.ds(cw + 3 - s, 1)],
                            in1=cv[t][:, s:L], op0=ALU.mult, op1=ALU.add).then_inc(tap_v, 1)

                def apply_decay(i):
                    c = i // 2
                    wait(dve, e_a, 8 * j + i + 1)
                    if i == 0:
                        wait(dve, g_mm, j + 1)
                    wait(dve, y_mm, 4 * j + c)
                    tt(M[i % 2][:, :].rearrange("p (n t) -> p n t", n=4),
                       E[i % 2][:, :].rearrange("p (n t) -> p n t", n=4),
                       bank[5][:, c * CH:(c + 1) * CH].unsqueeze(1).to_broadcast([P, 4, CH]),
                       ALU.mult).then_inc(m_v, 1)

                if A:
                    convolve(0)
                if C:
                    wait(dve, out_mm, i2 + 1)
                    wait(dve, ry_a, 2 * i2 + 2)
                    wait(dve, hup, NB + i2)
                    tt(o_sb[:, :], bank[2][:, :], rY[:, :], ALU.mult).then_inc(o_v, 1)
                if A:
                    convolve(1)
                if B:
                    pj = dve.snap(j // NB * NPAR)
                    for t in range(2):
                        wait(dve, silu_a, 6 * j + 3 + t)
                        wait(dve, fin_p, 4 * j - 2 + 2 * t)
                        ts(yt[t][:, :], xbc[t][:, :], PAR[:, bass.ds(pj + C_D + t, 1)], None, ALU.mult).then_inc(dx_v, 1)
                if A:
                    wait(dve, dta_a, 6 * k + 3)
                    wait(dve, tr_mm, 2 * k)
                    stt(out=dt_[:, :], in0=u[:, :], scalar=0.0, in1=ln1[:, :], op0=ALU.max, op1=ALU.add).then_inc(dtc_v, 1)
                if B:
                    apply_decay(0)
                if A:
                    wait(dve, dtc_v, 11 * k + 2)
                    ts(dA[:, :], dt_[:, :], PAR[:, bass.ds(pk + C_NA, 1)], None, ALU.mult).then_inc(dtc_v, 1)
                if B:
                    apply_decay(1)
                if A:
                    wait(dve, dtc_v, 11 * k + 3)
                    nc.vector.tensor_tensor_scan(cum[:, :], ones_row[:, :], dA[:, :], 0.0, ALU.mult, ALU.add).then_inc(dtc_v, 1)
                    convolve(2)
                    cp(p0[:, :], cum[:, :]).then_inc(dtc_v, 1)
                if B:
                    apply_decay(2)
                if A:
                    wait(dve, dtc_v, 11 * k + 5)
                    stt(out=r1[:, :], in0=p0[:, :], scalar=CST[:, K_M1:K_M1 + 1], in1=cum[:, :],
                        op0=ALU.mult, op1=ALU.add).then_inc(dtc_v, 1)
                if B:
                    apply_decay(3)
                if A:
                    wait(dve, dtc_v, 11 * k + 6)
                    cp(p1[:, :], r1[:, :]).then_inc(dtc_v, 1)
                    convolve(3)
                    wait(dve, dtc_v, 11 * k + 7)
                    stt(out=r2[:, :], in0=p1[:, :], scalar=CST[:, K_M2:K_M2 + 1], in1=r1[:, :],
                        op0=ALU.mult, op1=ALU.add).then_inc(dtc_v, 1)
                if B:
                    apply_decay(4)
                if A:
                    wait(dve, dtc_v, 11 * k + 8)
                    wait(dve, p4_in, 64 * k)
                    cp(p2[:, :], r2[:, :]).then_inc(dtc_v, 1)
                if B:
                    apply_decay(5)
                if A:
                    wait(dve, dta_a, 6 * k + 4)
                    tt(wdec[:, :], dt_[:, :], ecs[:, :], ALU.mult).then_inc(dtc_v, 1)
                    wait(dve, dtc_v, 11 * k + 9)
                    ts(spend[:, :], CST[:, K_SELD:K_SELD + 32], p2[:, CH - 1:CH], None, ALU.mult).then_inc(dtc_v, 1)
                if B:
                    apply_decay(6)
                    apply_decay(7)
                    wait(dve, st_mm, 2 * j + 1)
                    wait(dve, yi_mm, 2 * j)
                    cp(S[1][:, :], bank[4][:, 0:DI]).then_inc(s_v, 1)
                    for c in range(2, NC):
                        wait(dve, s_v, 5 * j + 2 * c - 3)
                        tt(stmp[:, :].rearrange("p (h d) -> p h d", h=NH), S[c - 1][:, :].rearrange("p (h d) -> p h d", h=NH),
                           dec[:, (c - 1) * NH:c * NH].unsqueeze(2).to_broadcast([P, NH, HD]), ALU.mult).then_inc(s_v, 1)
                        wait(dve, s_v, 5 * j + 2 * c - 2)
                        if c == 3:
                            wait(dve, st_mm, 2 * j + 2)
                        new = bank[4][:, DI:2 * DI] if c == 2 else bank[4][:, 0:DI]
                        tt(S[c][:, :], stmp[:, :], new, ALU.add).then_inc(s_v, 1)
                    for t in range(2):
                        if t == 0:
                            wait(dve, y_mm, 4 * j + 4)
                        wait(dve, dx_v, 2 * j + 1 + t)
                        tt(yt[t][:, :], yt[t][:, :], bank[6 + t][:, :], ALU.add).then_inc(fin_v, 1)
                        wait(dve, yi_mm, 2 * j + 1 + t)
                        wait(dve, e2_a, 2 * j + 1 + t)
                        tt(ti[t][:, :], bank[2 + t][:, 128:512], E2[t][:, :], ALU.mult).then_inc(fin_v, 1)
                if N:
                    norm_apply(k + 1)

            def norm_apply(n):
                wait(dve, rb_a, 2 * n + 2)
                wait(dve, pj_mm, 6 * n)
                stt(out=hn[:, :], in0=h[:, bass.ds(n % NB * L, L)], scalar=PAR[:, bass.ds(n // NB * NPAR + C_BNW, 1)],
                    in1=rB[:, :], op0=ALU.mult, op1=ALU.mult).then_inc(hn_v, 1)

            norm_apply(0)
            steps(dve, body)

            dve.wait_ge(s_ffw, 48)
            dve.wait_ge(hup, NB + STEPS)
            tt(gaf[:, :], MOD[:, 16:24], PAR2[:, F_FW:F_FW + 1].to_broadcast([P, NB]), ALU.mult).then_inc(c3_v, 1)
            nc.vector.memset(C3[:, :], 0.0).then_inc(c3_v, 1)
            dve.wait_ge(c3_v, 2)

            def v(ins, n=0, own=None):
                ins.then_inc(pv, 1)
                if own:
                    wait(dve, pv, 25 * n + own)

            def four(t):
                return t[:, :].rearrange("p (s e) -> p s e", s=4)

            def pairs(t):
                return t[:, :].rearrange("p (s e f) -> p s e f", s=4, e=NE)

            def add_mamba(n):
                xb = xT[:, bass.ds(n * L, L)]
                wait(dve, pa, 11 * n + 3)
                wait(dve, pv, 25 * n - 18)
                v(stt(out=nT[:, :], in0=h[:, bass.ds(n * L, L)], scalar=gaf[:, bass.ds(n, 1)], in1=rf[:, :],
                      op0=ALU.mult, op1=ALU.mult), n, 1)
                v(tt(xb, nT[:, :], xb, ALU.add), n, 2)

            def centre(n):
                wait(dve, pm_mm, 6 * n + 2)
                v(tt(nT[:, :], xT[:, bass.ds(n * L, L)], bank[7][:, :], ALU.subtract))

            def modulate(n):
                wait(dve, pa, 11 * n + 6)
                v(tt(nT[:, :], nT[:, :], rf[:, :], ALU.mult), n, 4)
                v(ts(nT[:, :], nT[:, :], MOD[:, bass.ds(n + 32, 1)], MOD[:, bass.ds(n + 24, 1)], ALU.mult, ALU.add))

            def scale(n):
                wait(dve, pa, 11 * n + 9)
                v(stt(out=nT[:, :], in0=nT[:, :], scalar=PAR2[:, F_NW:F_NW + 1], in1=rf[:, :], op0=ALU.mult, op1=ALU.mult))

            def halve(n):
                par = bass.ds((n % 2) * L, L)
                wait(dve, pa, 11 * n + 10)
                v(tt(nL[:, par], nT[:, :], nH[:, par].bitcast(F32), ALU.subtract))

            def sigmoid(n):
                wait(dve, pa, 11 * n + 11)
                v(ts(prx[:, :], pr[:, :], 1.0, None, ALU.add), n, 8)
                v(nc.vector.reciprocal(pm[:, :], prx[:, :]), n, 9)

            def rank(n):
                inner, outer = four(pm).unsqueeze(2).to_broadcast([P, 4, NE, NE]), four(pm).unsqueeze(3).to_broadcast([P, 4, NE, NE])
                tri = CST[:, K_TRI:K_TRI + 64].rearrange("p (e f) -> p e f", e=NE).unsqueeze(1).to_broadcast([P, 4, NE, NE])
                v(tt(pairs(cgt), inner, outer, ALU.is_gt))
                v(tt(pairs(ceq), inner, outer, ALU.is_equal), n, 11)
                v(tt(pairs(ceq), pairs(ceq), tri, ALU.mult), n, 12)
                v(tt(cgt[:, :], cgt[:, :], ceq[:, :], ALU.add), n, 13)
                v(nc.vector.tensor_reduce(rnk[:, :], cgt[:, :].rearrange("p (q f) -> p q f", f=NE), AX.X, ALU.add), n, 14)

            def routing(n):
                v(stt(out=pm[:, :], in0=rnk[:, :], scalar=1.5, in1=pm[:, :], op0=ALU.is_lt, op1=ALU.mult), n, 15)
                v(nc.vector.tensor_reduce(csum[:, :], four(pm), AX.X, ALU.add), n, 16)
                v(ts(csum[:, :], csum[:, :], 1e-6, None, ALU.add), n, 17)
                v(nc.vector.reciprocal(csum[:, :], csum[:, :]), n, 18)
                v(tt(four(cmb), four(pm), csum[:, :].unsqueeze(2).to_broadcast([P, 4, NE]), ALU.mult), n, 19)

            def parts(n):
                c3 = C3[:, :].rearrange("p (s q e) -> p s q e", s=4, q=4)
                wait(dve, pm_mm, 6 * n)
                v(cp(c3[:, :, 0, :], four(cmb)), n, 20)
                v(tt(four(cr), four(cmb), c3[:, :, 0, :], ALU.subtract), n, 21)
                v(cp(c3[:, :, 1, :], four(cr)), n, 22)
                v(tt(four(cr), four(cr), c3[:, :, 1, :], ALU.subtract), n, 23)
                v(cp(c3[:, :, 2, :], four(cr)))

            def weights_in(n):
                wait(dve, pm_mm, 6 * n + 6)
                wait(dve, cb_mm, NE * n)
                v(cp(CT[:, :], bank[7][:, :].bitcast(BF16)[0:32, 0:L]))

            NEXT = {8: add_mamba, 12: centre, 20: modulate, 27: scale, 29: halve, 32: sigmoid, 33: rank, 34: routing, 35: parts}
            OWN = {4: weights_in}

            def weigh(q, b, e):
                count = NE * b + e
                wait(dve, cb_mm, count)
                wait(dve, eo_a, q + 1)
                wait(dve, acc_p, count - 1)
                tt(ec, bank[6][:, :], eb, ALU.mult).then_inc(ec_v, 1)

            def finish(b):
                wait(dve, acc_p, NE * (b + 1))
                wait(dve, ft_mm, b)
                stt(out=fo, in0=acc, scalar=MOD[:, bass.ds(b + 40, 1)], in1=xT[:, bass.ds(b * L, L)],
                    op0=ALU.mult, op1=ALU.add).then_inc(fo_v, 1)

            def body_ff(b, prep):
                first = isinstance(b, int) and b == 0
                for e in range(NX):
                    q = b * NX + e
                    for t in range(HT):
                        if t == HT - 1:
                            wait(dve, u_mm, HT * q + t + 1)
                            wait(dve, hi_a, HT * q)
                            wait(dve, lo_v, HT * q)
                            ts(hr[t], bank[t][:, :], PAR2[:, F_B1 + HT * e + t:F_B1 + HT * e + t + 1], 0.0,
                               ALU.add, ALU.max).then_inc(r_v, 1)
                        if t == 1:
                            if e > 2:
                                weigh(q - 2, b, e - 2)
                            elif e == 0 and not first:
                                weigh(q - 2, b - 1, NE - 1)
                        wait(dve, hi_a, HT * q + t + 1)
                        wait(dve, dn_mm, HT * (q - 1) + t + 1)
                        tt(hL[t][:, :], hr[t], hH[t][:, :].bitcast(F32), ALU.subtract).then_inc(lo_v, 1)
                        if e == 1 and t == 2 and not first:
                            weigh(q - 2, b - 1, NE)
                        if e == 1 and t == 3 and not first:
                            finish(b - 1)
                        if prep and HT * e + t in NEXT:
                            NEXT[HT * e + t](b + 1)
                        if HT * e + t in OWN:
                            OWN[HT * e + t](b)

            for e in range(NX):
                for w in range(2):
                    cs = slice(e * HE, (e + 1) * HE)
                    wait(dve, wh_a, 2 * e + w + 1)
                    tt(WL[w][:, cs], RAW[w][:, cs], WH[w][:, cs].bitcast(F32), ALU.subtract).then_inc(wl_v, 1)
            for piece in NEXT.values():
                piece(0)
            blocks(dve, body_ff)
            weigh(NB * NX - 2, NB - 1, NE - 1)
            weigh(NB * NX - 1, NB - 1, NE)
            finish(NB - 1)

        @block.gpsimd
        def _(pool):
            tt = nc.gpsimd.tensor_tensor

            def body(k, A, B, C, N):
                j, i2 = k - 1, k - 2
                if C:
                    hb = h[:, bass.ds(i2 % NB * L, L)]
                    wait(pool, o_v, i2 + 1)
                    tt(hb, hb, o_sb[:, :], ALU.add).then_inc(hup, 1)
                if B:
                    wait(pool, dta_a, 6 * k - 1)
                    for c in range(NC):
                        xv = xtok[c][:, 0:DI].rearrange("p (h d) -> p h d", h=NH)
                        wait(pool, t_ev, 4 * j + c + 1)
                        wait(pool, y_mm, 4 * j - 3 + c)
                        tt(dtx[c][:, :].rearrange("p (h d) -> p h d", h=NH), xv,
                           DTW[:, 32 * c:32 * c + NH].unsqueeze(2).to_broadcast([P, NH, HD]), ALU.mult).then_inc(px_p, 1)
                        if c < NC - 1:
                            if c == 0:
                                wait(pool, st_mm, 2 * j)
                            tt(xw[c][:, :].rearrange("p (h d) -> p h d", h=NH), xv,
                               DTW[:, P + 32 * c:P + 32 * c + NH].unsqueeze(2).to_broadcast([P, NH, HD]),
                               ALU.mult).then_inc(px_p, 1)
                if B:
                    for t in range(2):
                        wait(pool, fin_v, 4 * j + 2 + 2 * t)
                        tt(yt[t][:, 128:512], yt[t][:, 128:512], ti[t][:, :], ALU.add).then_inc(fin_p, 1)
                        wait(pool, fin_p, 4 * j + 1 + 2 * t)
                        wait(pool, silu_a, 6 * j + 5 + t)
                        wait(pool, out_mm, j)
                        tt(y2[t][:, :], yt[t][:, :], zs[:, bass.ds((j % 2) * 2 * L + t * L, L)], ALU.mult).then_inc(fin_p, 1)

            steps(pool, body)

            def add_expert(count, b):
                wait(pool, ec_v, count)
                wait(pool, eo_a, NX * b + 1)
                tt(acc, acc, ec, ALU.add).then_inc(acc_p, 1)

            for e in range(1, NX):
                add_expert(e, 0)
            with pool.Fori(1, NB) as b:
                for e in range(1, NX):
                    add_expert(NE * b + e, b)


def constants():
    import numpy as np
    c = np.zeros((P, NCST), np.float32)
    p, t = np.arange(P)[:, None], np.arange(P)[None, :]
    c[:, K_ID:K_ID + P] = p == t
    c[:, K_MASK:K_MASK + 512] = np.tile(np.where(t >= p, 0.0, -1e30), (1, 4))
    row, head = p % 32, p % 8
    used = row < 24
    c[:, K_SEL:K_SEL + 1024] = used & (head == np.arange(1024)[None, :] // P)
    c[:, K_SELX:K_SELX + 256] = used & (head == np.arange(256)[None, :] // HD)
    q = np.arange(32)[None, :]
    c[:, K_SELD:K_SELD + 32] = used & (head == q % 8) & (p // 32 == q // 8)
    c[:, K_M1] = -(row[:, 0] >= 8).astype(np.float32)
    c[:, K_M2] = -(row[:, 0] >= 16).astype(np.float32)
    c[:, K_EPS5], c[:, K_EPS8] = 1e-5, 1e-8
    e = np.arange(64)[None, :]
    c[:, K_TRI:K_TRI + 64] = (e % 8) < (e // 8)
    return c


def parameters(v):
    import numpy as np
    out = np.zeros((P, NL, NPAR), np.float32)
    w_dt = v["L0_attn_W_in"][:, :, 768:776]
    for part in range(3):
        out[:, :, C_WDT + 8 * part:C_WDT + 8 * part + 8] = w_dt.transpose(1, 0, 2)
        for c in range(NC):
            q = 32 * c + 8 * part
            out[q:q + 8, :, C_DTB] = v["L0_attn_dt_bias"].T
            out[q:q + 8, :, C_NA] = v["L0_attn_A_log"].T
    out[:, :, C_BNW] = v["L0_attn_block_norm_w"].T
    cw = v["L0_attn_conv_w"].reshape(NL, 4, P, 4)
    out[:, :, C_CW:C_CW + 16] = cw.transpose(2, 0, 1, 3).reshape(P, NL, 16)
    out[:, :, C_CB:C_CB + 4] = v["L0_attn_conv_b"].reshape(NL, 4, P).transpose(2, 0, 1)
    out[:, :, C_D:C_D + 2] = np.repeat(v["L0_attn_D"], HD, axis=1).reshape(NL, 2, P).transpose(2, 0, 1)
    out[:, :, C_GW:C_GW + 2] = v["L0_attn_gate_norm_w"].reshape(NL, 2, P).transpose(2, 0, 1)
    return out.reshape(P, NL * NPAR)


def feed_forward(v):
    import numpy as np
    out = np.zeros((P, NPAR2), np.float32)
    b1 = np.concatenate([v["L0_ffn_sb1"][None], v["L0_ffn_eb1"]])
    out[:, F_B1:F_B1 + NX * HT] = b1.reshape(NX * HT, P).T
    out[:, F_B2:F_B2 + NX] = np.concatenate([v["L0_ffn_sb2"][None], v["L0_ffn_eb2"]]).T
    out[:, F_NW] = v["L0_ffn_norm_weight"]
    out[:, F_FW] = v["L0_attn_final_norm_w"]
    out[:, F_RW:F_RW + NE] = v["L0_ffn_router_w"].T
    w1 = np.concatenate([v["L0_ffn_sw1"][None], v["L0_ffn_ew1"]]).transpose(1, 0, 2).reshape(P, NX * HE)
    w2 = np.concatenate([v["L0_ffn_sw2"][None], v["L0_ffn_ew2"]]).reshape(NX, HT, P, DM)
    w2 = w2.transpose(2, 0, 1, 3).reshape(P, NX * HE)
    return out, np.ascontiguousarray(w1), np.ascontiguousarray(w2)


def projection(v):
    import numpy as np
    return np.stack([v["L0_attn_W_in"][:, :, c:c + P] for c in W_COL], axis=1).reshape(-1)


def kernel(**inputs):
    import numpy as np
    import concourse.bacc as bacc
    from concourse.bass_utils import run_bass_kernel_spmd

    v = {n: np.asarray(a) for n, a in inputs.items()}
    par2, w1, w2 = feed_forward(v)
    arrays = {
        "x_in": v["L0_attn_x"].reshape(NB * L, DM),
        "w_in": projection(v),
        "w_out": v["L0_attn_W_out"].reshape(NL, 2, P, DM).transpose(0, 2, 1, 3).reshape(-1),
        "par_in": parameters(v),
        "cst_in": constants(),
        "c_in": np.ascontiguousarray(v["L0_c"].T),
        "wmod_in": v["L0_wmod"],
        "par2_in": par2,
        "w1_in": w1,
        "w2_in": w2,
    }
    arrays = {n: np.ascontiguousarray(a) for n, a in arrays.items()}
    nc = bacc.Bacc("TRN2", target_bir_lowering=False, num_devices=1)
    args = [nc.dram_tensor(n, a.shape, mybir.dt.from_np(a.dtype), kind="ExternalInput").ap() for n, a in arrays.items()]
    out = nc.dram_tensor("out", (NB * L, DM), F32, kind="ExternalOutput").ap()
    build(nc, *args, out)
    r = run_bass_kernel_spmd(nc, [arrays], core_ids=[0])
    return r.results[0]["out"].reshape(NB, L, DM)
```

```python
import concourse.bass as bass
from concourse import mybir
from contextlib import ExitStack

F32 = mybir.dt.float32
BF16 = mybir.dt.bfloat16
F32R = mybir.dt.float32r
ACT = mybir.ActivationFunctionType
ALU = mybir.AluOpType
AX = mybir.AxisListType

P = 128
NB, L, DM = 8, 512, 128
NL, DI, NH, HD, DS = 4, 256, 8, 32, 128
CH = 128
NC = L // CH
NE, HE = 8, 512
STEPS = NL * NB
EXPLN = "natural_log_exp_and_others"

C_WDT, C_BNW, C_CW, C_CB, C_DTB, C_NA, C_D, C_GW = 0, 32, 33, 49, 53, 54, 55, 57
NPAR = 60
NX = NE + 1
HT = HE // P
F_B1, F_B2, F_NW, F_FW, F_RW = 0, NX * HT, NX * HT + NX, NX * HT + NX + 1, NX * HT + NX + 2
NPAR2 = F_RW + NE
K_ID, K_MASK, K_SEL, K_SELX = 0, 128, 640, 1664
K_SELD, K_M1, K_M2, K_EPS5, K_EPS8, K_TRI = 1920, 1952, 1953, 1954, 1955, 1956
NCST = K_TRI + 64
W_COL = [DI, DI + P, 2 * DI, 2 * DI + DS, 0, P]
X0, X1, TB, TC = 0, 1, 2, 3
TURN_BANK = [4, 6, 7, 4]


def wait(eng, sem, value):
    if isinstance(value, int) and value <= 0:
        return
    eng.wait_ge(sem, value)


def build(nc, x, w_in, w_out, par, cst, c_t, wmod, par2, w1, w2, out):
    ctx = ExitStack()
    with ctx:
        scope = [ctx]

        def sb(name, cols, dt=F32, parts=P):
            return scope[0].enter_context(nc.sbuf_tensor(name, [parts, cols], dt))

        def sem(name):
            return ctx.enter_context(nc.semaphore(name))

        bank = [ctx.enter_context(nc.psum_tensor(f"bank{i}", [P, 512], F32)) for i in range(8)]

        h = sb("h", NB * L)
        xT = sb("xT", NB * L)
        PAR = sb("PAR", NL * NPAR)
        CST = sb("CST", NCST)
        MOD = sb("MOD", 48)
        ident = CST[:, K_ID:K_ID + P]
        eps5, eps8 = CST[:, K_EPS5:K_EPS5 + 1], CST[:, K_EPS8:K_EPS8 + 1]
        mean128 = sb("mean128", P)
        mean256 = sb("mean256", P)
        idb, onesb = sb("idb", P, BF16), sb("onesb", P, BF16)
        maskb = sb("maskb", 512, BF16)
        selb, nselb = sb("selb", 1024, BF16), sb("nselb", 1024, BF16)
        selxb = sb("selxb", 256, BF16)
        ones_row = sb("ones_row", P)
        PAR2 = sb("PAR2", NPAR2)
        RAW = [sb(f"RAW{w}", NX * HE) for w in range(2)]
        scope[0] = ExitStack()
        WA = [sb(f"WA{t}", P) for t in range(6)]
        WDT = sb("WDT", 32)
        WO_raw, WO = sb("WO_raw", 2 * DM), sb("WO", 2 * DM)
        sqh, lnm, rB, hn = sb("sqh", L), sb("lnm", L), sb("rB", L), sb("hn", L)
        cv = [sb(f"cv{t}", L) for t in range(4)]
        xbc = [sb(f"xbc{t}", L) for t in range(4)]
        zs = sb("zs", 2 * 2 * L)
        zraw = [sb(f"zraw{t}", L) for t in range(2)]
        u, ax, ex, ln1 = sb("u", P), sb("ax", P), sb("ex", P), sb("ln1", P)
        dt_, dA, cum, r1, r2 = sb("dt_", P), sb("dA", P), sb("cum", P), sb("r1", P), sb("r2", P)
        p0, p1, p2 = sb("p0", P, BF16), sb("p1", P, BF16), sb("p2", P, BF16)
        ecs, wdec, spend = sb("ecs", P), sb("wdec", P), sb("spend", 32, BF16)
        P4 = sb("P4", L, BF16, parts=32)
        DTW, dec = sb("DTW", 2 * P + 32), sb("dec", 32)
        xtok = [sb(f"xtok{c}", 384) for c in range(NC)]
        dtx = [sb(f"dtx{c}", DI) for c in range(NC)]
        xw = [sb(f"xw{c}", DI) for c in range(NC - 1)]
        E = [sb(f"E{g}", 512) for g in range(2)]
        M = [sb(f"M{i}", 512) for i in range(4)]
        S = [None] + [sb(f"S{c}", DI) for c in range(1, NC)]
        stmp = sb("stmp", DI)
        E2 = [sb(f"E2_{t}", 384) for t in range(2)]
        yt = [sb(f"yt{t}", L) for t in range(2)]
        ti = [sb(f"ti{t}", 384) for t in range(2)]
        y2 = [sb(f"y2_{t}", L) for t in range(2)]
        sqy = [sb(f"sqy{t}", L) for t in range(2)]
        lnY, rY, o_sb = sb("lnY", L), sb("rY", L), sb("o_sb", L)
        xin = sb("xin", NB * L)
        bst, mv, rstd, lnv = sb("bst", 32 * 6), sb("mv", 64), sb("rstd", 32), sb("lnv", 32)
        xn = sqy
        cT, cS, wm = sb("cT", NB), sb("cS", NB), sb("wm", 6 * DM)
        gsg = sb("gsg", 16)
        scope[0].close()

        scope[0] = ctx
        WH = [sb(f"WH{w}", NX * HE, F32R) for w in range(2)]
        WL = [sb(f"WL{w}", NX * HE, F32R) for w in range(2)]
        nH, nL = sb("nH", 2 * L, F32R), sb("nL", 2 * L, F32R)
        hr = [RAW[0][:, t * L:(t + 1) * L] for t in range(HT)]
        hH = [sb(f"hH{t}", L, F32R) for t in range(HT)]
        hL = [sb(f"hL{t}", L, F32R) for t in range(HT)]
        sqf, lnf, rf, nT = sb("sqf", L), sb("lnf", L), sb("rf", L), sb("nT", L)
        pr, prx, rnk, pm, cmb, cr = [sb(n, 32) for n in ("pr", "prx", "rnk", "pm", "cmb", "cr")]
        cgt, ceq = sb("cgt", 256), sb("ceq", 256)
        csum = sb("csum", 4)
        C3 = sb("C3", P, BF16)
        CT = sb("CT", L, BF16, parts=32)
        eb, ec, acc, fo, ob = [RAW[1][:, t * L:(t + 1) * L] for t in range(5)]
        gaf = sb("gaf", NB)

        s_cst, s_x, s_par, s_mod = sem("cst_in"), sem("x_in"), sem("par_in"), sem("mod_in")
        const_v, const_p = sem("const_v"), sem("const_p")
        bn_v, rstd_a, xn_v, xt_mm, xt_ev = sem("bn_v"), sem("rstd_a"), sem("xn_v"), sem("xt_mm"), sem("xt_ev")
        cs_a, mod_mm, mod_v = sem("cs_a"), sem("mod_mm"), sem("mod_v")
        wa = [sem(f"wa{t}") for t in range(6)]
        zc_a = sem("zc_a")
        tap_v = [sem(f"tap{t}_v") for t in range(4)]
        s_wo, p4_in = sem("wo_in"), sem("p4_in")
        wdt_a, hup, sqh_a, ms_mm, rb_a, hn_v = sem("wdt_a"), sem("hup"), sem("sqh_a"), sem("ms_mm"), sem("rb_a"), sem("hn_v")
        dt_mm, pj_mm, silu_a, dtc_v, dta_a, tr_mm = sem("dt_mm"), sem("pj_mm"), sem("silu_a"), sem("dtc_v"), sem("dta_a"), sem("tr_mm")
        g_mm, t_mm, t_ev, d_mm, e_a, m_v, y_mm = sem("g_mm"), sem("t_mm"), sem("t_ev"), sem("d_mm"), sem("e_a"), sem("m_v"), sem("y_mm")
        px_p, st_mm, s_v, e2_mm, e2_a, yi_mm = sem("px_p"), sem("st_mm"), sem("s_v"), sem("e2_mm"), sem("e2_a"), sem("yi_mm")
        dx_v, fin_v, fin_p, wos_a = sem("dx_v"), sem("fin_v"), sem("fin_p"), sem("wos_a")
        sq_a, ss_mm, ry_a, out_mm, o_v = sem("sq_a"), sem("ss_mm"), sem("ry_a"), sem("out_mm"), sem("o_v")
        s_ffw, s_out = sem("ffw_in"), sem("out_done")
        wh_a, wl_v, c3_v = sem("wh_a"), sem("wl_v"), sem("c3_v")
        pa, pv, pm_mm = sem("prep_a"), sem("prep_v"), sem("prep_mm")
        u_mm, r_a, r_v, hi_a, lo_v, dn_mm = sem("u_mm"), sem("r_a"), sem("r_v"), sem("hi_a"), sem("lo_v"), sem("dn_mm")
        cb_mm, eo_a, ec_v, acc_p, fo_v, ft_mm, ob_a = [sem(n) for n in ("cb_mm", "eo_a", "ec_v", "acc_p", "fo_v", "ft_mm", "ob_a")]

        def steps(eng, body):
            body(0, A=True, B=False, C=False, N=True)
            body(1, A=True, B=True, C=False, N=True)
            body(2, A=True, B=True, C=True, N=True)
            with eng.Fori(3, STEPS - 1) as k:
                body(k, A=True, B=True, C=True, N=True)
            body(STEPS - 1, A=True, B=True, C=True, N=False)
            body(STEPS, A=False, B=True, C=True, N=False)
            body(STEPS + 1, A=False, B=False, C=True, N=False)

        def blocks(eng, body):
            body(0, prep=True)
            body(1, prep=True)
            with eng.Fori(2, NB - 1) as b:
                body(b, prep=True)
            body(NB - 1, prep=False)

        block = ctx.enter_context(nc.Block())

        @block.sync
        def _(sp):
            def rows(src, at, n):
                return src[bass.ds(at, P * n)].rearrange("(p n) -> p n", n=n)

            sp.dma_start(CST[:, :], cst).then_inc(s_cst, 16)
            for q in range(4):
                sp.dma_start(xin[:, q * 1024:(q + 1) * 1024].rearrange("p (n d) -> p n d", d=DM),
                             x[q * 1024:(q + 1) * 1024, :].rearrange("(n p) d -> p n d", p=P)).then_inc(s_x, 16)
            sp.dma_start(cT[:, :], c_t).then_inc(s_mod, 16)
            sp.dma_start(wm[:, :], wmod).then_inc(s_mod, 16)
            sp.dma_start(PAR[:, :], par).then_inc(s_par, 16)
            for t in range(6):
                sp.dma_start(WA[t][:, :], rows(w_in, t * P * P, P)).then_inc(wa[t], 16)
            sp.dma_start(PAR2[:, :], par2).then_inc(s_ffw, 16)
            for w, src in enumerate((w1, w2)):
                sp.dma_start(RAW[w][:, :], src).then_inc(s_ffw, 16)

            def body(k, A, B, C, N):
                if B:
                    j = k - 1
                    at_j = sp.snap(j // NB * (2 * DM * P))
                    wait(sp, wos_a, 2 * j)
                    sp.dma_start(WO_raw[:, :], rows(w_out, at_j, 2 * DM)).then_inc(s_wo, 16)
                if N:
                    at = [sp.snap((k + 1) // NB * (6 * P * P) + t * P * P) for t in range(6)]
                for t in range(6):
                    if N:
                        wait(sp, pj_mm, 6 * k + t + 1)
                        sp.dma_start(WA[t][:, :], rows(w_in, at[t], P)).then_inc(wa[t], 16)
                if A:
                    if B:
                        wait(sp, e2_mm, 2 * k)
                    wait(sp, dtc_v, 11 * k + 9)
                    for c in range(NC):
                        sp.dma_start(P4[:, c * CH:(c + 1) * CH], p2[32 * c:32 * c + 32, :]).then_inc(p4_in, 16)

            steps(sp, body)

            sp.wait_ge(s_ffw, 48)

            def store(b):
                first_row = sp.snap(b * L)
                sp.wait_ge(ob_a, b + 1)
                sp.dma_start(out[bass.ds(first_row, L), :].rearrange("(s p) d -> p s d", p=P),
                             ob.rearrange("p (s d) -> p s d", s=4)).then_inc(s_out, 16)

            store(0)
            with sp.Fori(1, NB) as b:
                store(b)
            sp.wait_ge(s_out, 16 * NB)

        @block.tensor
        def _(pe):
            mm = nc.tensor.matmul
            pe.wait_ge(cs_a, 1)
            pe.wait_ge(s_mod, 32)
            for i in range(6):
                ins = mm(bank[4][:, 8 * i:8 * i + 8], wm[:, i * DM:(i + 1) * DM], cS[:, :], start=True, stop=True)
            ins.then_inc(mod_mm, 1)
            pe.wait_ge(s_cst, 16)

            def turn_input(b):
                for half, free in enumerate((hup, xt_ev)):
                    wait(pe, xn_v, 3 * b + 2 + half)
                    wait(pe, free, b)
                    for n in range(4):
                        ins = nc.tensor.transpose(bank[half][:, n * P:(n + 1) * P],
                                                  xn[half][:, n * P:(n + 1) * P], ident)
                    ins.then_inc(xt_mm, 1)

            turn_input(0)
            with pe.Fori(1, NB) as b:
                turn_input(b)

            def body(k, A, B, C, N):
                j, i2 = k - 1, k - 2
                if A:
                    wait(pe, hn_v, k + 1)
                    wait(pe, wdt_a, k + 1)
                    wait(pe, e2_a, 2 * j)
                    for c in range(NC):
                        ins = mm(bank[4][32 * c:32 * c + 32, 0:CH], WDT[:, :], hn[:, c * CH:(c + 1) * CH],
                                 start=True, stop=True, tile_position=(0, 32 * c))
                    ins.then_inc(dt_mm, 1)

                def project(t):
                    wait(pe, wa[t], 16 * (k + 1))
                    wait(pe, tap_v[t - 2], 4 * (k + 1))
                    mm(bank[t % 2][:, :], WA[t][:, :], hn[:, :], start=True, stop=True).then_inc(pj_mm, 1)

                def square_mean():
                    wait(pe, sq_a, 2 * (i2 + 1))
                    if B:
                        wait(pe, t_ev, 4 * j + 2)
                    else:
                        wait(pe, fin_v, 4 * (i2 + 1))
                    mm(bank[6][:, :], mean256[:, :], sqy[0][:, :], start=True, stop=False)
                    mm(bank[6][:, :], mean256[:, :], sqy[1][:, :], start=False, stop=True).then_inc(ss_mm, 1)

                def project_out():
                    wait(pe, wos_a, 2 * (i2 + 1))
                    if B:
                        wait(pe, t_ev, 4 * j + 3)
                    mm(bank[7][:, :], WO[:, 0:DM], y2[0][:, :], start=True, stop=False)
                    mm(bank[7][:, :], WO[:, DM:2 * DM], y2[1][:, :], start=False, stop=True).then_inc(out_mm, 1)

                def turn(c):
                    if c == 0:
                        if A:
                            wait(pe, dtc_v, 11 * k + 1)
                        else:
                            wait(pe, e2_a, 2 * j)
                    elif c == 1:
                        wait(pe, fin_v, 4 * j - 3)
                    elif c == 2:
                        wait(pe, fin_v, 4 * j - 2)
                    else:
                        wait(pe, t_ev, 4 * j + 1)
                    for n, t in enumerate((X0, X1, TB)):
                        ins = nc.tensor.transpose(bank[TURN_BANK[c]][:, n * P:(n + 1) * P],
                                                  xbc[t][:, c * CH:(c + 1) * CH], ident)
                    ins.then_inc(t_mm, 1)

                def decays(c):
                    for g in range(2):
                        i = 2 * c + g
                        if i >= 2:
                            wait(pe, e_a, 8 * j + i - 1)
                        else:
                            if i == 0:
                                wait(pe, p4_in, 64 * (j + 1))
                            wait(pe, fin_v, 4 * j - 1 + g)
                        dst = bank[2 + g]
                        pc = P4[:, c * CH:(c + 1) * CH]
                        mm(dst[:, :], idb[:, :], maskb[:, :], start=True, stop=False)
                        mm(dst[:, :], pc, nselb[0:32, g * 512:(g + 1) * 512], start=False, stop=False)
                        for n in range(4):
                            hh = 4 * g + n
                            ins = mm(dst[:, n * P:(n + 1) * P], selb[0:32, hh * P:(hh + 1) * P], pc,
                                     start=False, stop=(n == 3))
                        ins.then_inc(d_mm, 1)

                def within(c):
                    wait(pe, m_v, 8 * j + 2 * c + 2)
                    wait(pe, px_p, 7 * j + 2 * c + 1)
                    if c == 0 and C:
                        wait(pe, ry_a, 2 * i2 + 1)
                        wait(pe, o_v, i2 + 1)
                    elif c == 0:
                        wait(pe, t_ev, 4 * j + 3)
                    for hh in range(NH):
                        q = 32 * (hh % 4)
                        ins = mm(bank[6 + hh // 4][q:q + 32, c * CH:(c + 1) * CH], dtx[c][:, hh * HD:(hh + 1) * HD],
                                 M[2 * (c % 2) + hh // 4][:, (hh % 4) * CH:(hh % 4 + 1) * CH], start=True, stop=True,
                                 tile_position=(0, q))
                    ins.then_inc(y_mm, 1)

                if B:
                    decays(0)
                    wait(pe, silu_a, 6 * j + 4)
                    wait(pe, s_v, 5 * j)
                    for c in range(NC):
                        cs = slice(c * CH, (c + 1) * CH)
                        ins = mm(bank[5][:, cs], xbc[TB][:, cs], xbc[TC][:, cs], start=True, stop=True)
                    ins.then_inc(g_mm, 1)
                    for c in range(3):
                        turn(c)
                if B:
                    decays(1)
                if A:
                    project(2)
                if B:
                    turn(3)
                if C:
                    square_mean()
                    project_out()
                if A:
                    project(3)
                if B:
                    decays(2)
                if A:
                    project(4)
                if B:
                    within(0)
                    decays(3)
                if N:
                    wait(pe, sqh_a, k + 2)
                    wait(pe, zc_a, 2 * k + 1)
                    mm(bank[0][:, :], mean128[:, :], sqh[:, :], start=True, stop=True).then_inc(ms_mm, 1)
                if B:
                    within(1)
                if A:
                    project(5)
                if B:
                    within(2)
                    wait(pe, px_p, 7 * j + 4)
                    wait(pe, t_ev, 4 * j + 4)
                    mm(bank[4][:, 0:DI], xtok[0][:, 256:384], xw[0][:, :], start=True, stop=True)
                    mm(bank[4][:, DI:2 * DI], xtok[1][:, 256:384], xw[1][:, :], start=True, stop=True).then_inc(st_mm, 1)
                    wait(pe, m_v, 8 * j + 8)
                    wait(pe, px_p, 7 * j + 6)
                    mm(bank[5][:, 0:DI], xtok[2][:, 256:384], xw[2][:, :], start=True, stop=True).then_inc(st_mm, 1)
                if A:
                    wait(pe, dtc_v, 11 * k + 11)
                    if N:
                        wait(pe, rb_a, 2 * k + 3)
                    else:
                        wait(pe, zc_a, 2 * k + 1)
                    nc.tensor.transpose(bank[0][:, 0:P], dt_[:, :], ident)
                    nc.tensor.transpose(bank[0][:, P:2 * P], wdec[:, :], ident)
                    mm(bank[0][:, 2 * P:2 * P + 32], onesb[:, :], spend[:, :], start=True, stop=True).then_inc(tr_mm, 1)
                if B:
                    within(3)
                    wait(pe, zc_a, 2 * k + 2 if A else 2 * k)
                    mm(bank[1][:, 128:512], selxb[0:32, 0:P], P4[:, 128:512], start=True, stop=True).then_inc(e2_mm, 1)
                    wait(pe, s_v, 5 * j + 3)
                    mm(bank[4][:, 128:512], selxb[0:32, P:2 * P], P4[:, 128:512], start=True, stop=True).then_inc(e2_mm, 1)
                if N:
                    wait(pe, dta_a, 6 * k + 5)
                    project_early(k + 1, 0)
                if B:
                    wait(pe, s_v, 5 * j + 5)
                    for t in range(2):
                        wait(pe, e_a, 8 * j + 7 + t)
                        for c in range(1, NC):
                            cs = slice(c * CH, (c + 1) * CH)
                            ins = mm(bank[2 + t][:, cs], S[c][:, t * P:(t + 1) * P], xbc[TC][:, cs], start=True, stop=True)
                        ins.then_inc(yi_mm, 1)
                if N:
                    if B:
                        wait(pe, e2_a, 2 * j + 1)
                    else:
                        wait(pe, zc_a, 2 * k + 2)
                    project_early(k + 1, 1)

            def project_early(n, t):
                wait(pe, wa[t], 16 * (n + 1))
                wait(pe, hn_v, n + 1)
                mm(bank[t][:, :], WA[t][:, :], hn[:, :], start=True, stop=True).then_inc(pj_mm, 1)

            pe.wait_ge(const_v, 2)
            pe.wait_ge(hup, NB)
            pe.wait_ge(sqh_a, 1)
            mm(bank[0][:, :], mean128[:, :], sqh[:, :], start=True, stop=True).then_inc(ms_mm, 1)
            pe.wait_ge(const_v, 9)
            pe.wait_ge(rb_a, 1)
            pe.wait_ge(xt_ev, NB)
            project_early(0, 0)
            project_early(0, 1)
            steps(pe, body)

            def square_mean(n):
                wait(pe, pa, 11 * n + 1)
                wait(pe, pv, 25 * n)
                mm(bank[7][:, :], mean128[:, :], sqf[:, :], start=True, stop=True).then_inc(pm_mm, 1)

            def mean(n):
                wait(pe, pv, 25 * n + 2)
                wait(pe, pa, 11 * n + 2)
                mm(bank[7][:, :], mean128[:, :], xT[:, bass.ds(n * L, L)], start=True, stop=True).then_inc(pm_mm, 1)

            def variance(n):
                wait(pe, pa, 11 * n + 4)
                mm(bank[7][:, :], mean128[:, :], sqf[:, :], start=True, stop=True).then_inc(pm_mm, 1)

            def square_mean_2(n):
                wait(pe, pa, 11 * n + 7)
                mm(bank[7][:, :], mean128[:, :], sqf[:, :], start=True, stop=True).then_inc(pm_mm, 1)

            def logits(n):
                wait(pe, pv, 25 * n + 6)
                for c in range(4):
                    ins = mm(bank[7][:, 8 * c:8 * c + 8], nT[:, c * P:(c + 1) * P], PAR2[:, F_RW:F_RW + NE],
                             start=True, stop=True)
                ins.then_inc(pm_mm, 1)

            def turn_weights(n):
                wait(pe, pv, 25 * n + 24)
                for c in range(4):
                    ins = nc.tensor.transpose(bank[7][:, :].bitcast(BF16)[0:32, c * P:(c + 1) * P],
                                              C3[:, 32 * c:32 * c + 32], idb[:, :])
                ins.then_inc(pm_mm, 1)

            NEXT = {4: square_mean, 11: mean, 16: variance, 24: square_mean_2, 29: logits}
            OWN = {2: turn_weights}

            def body_ff(b, prep):
                first = isinstance(b, int) and b == 0
                for e in range(NX):
                    q = b * NX + e
                    down = not (first and e == 0)
                    ep = (e - 1) % NX
                    for t in range(HT):
                        if e == 0 and t == 0:
                            wait(pe, pv, 25 * b + 7)
                            wait(pe, pa, 11 * b + 10)
                        if first and t == 0:
                            wait(pe, wl_v, 2 * e + 1)
                        if t < HT - 1:
                            wait(pe, r_a, 3 * q - 2 + t)
                        else:
                            wait(pe, r_v, q)
                        w = slice(e * HE + t * P, e * HE + (t + 1) * P)
                        nh = nH[:, bass.ds((b % 2) * L, L)]
                        nl = nL[:, bass.ds((b % 2) * L, L)]
                        mm(bank[t][:, :], WH[0][:, w], nh, start=True, stop=False)
                        mm(bank[t][:, :], WH[0][:, w], nl, start=False, stop=False)
                        mm(bank[t][:, :], WL[0][:, w], nh, start=False, stop=True).then_inc(u_mm, 1)
                        if down:
                            down_product(q - 1, ep, t, first)
                        if prep and HT * e + t in NEXT:
                            NEXT[HT * e + t](b + 1)
                        if HT * e + t in OWN:
                            OWN[HT * e + t](b)
                    if down and ep > 0:
                        wait(pe, ec_v, b * NE - 1 if e == 0 else b * NE + ep - 1)
                        if ep == 1:
                            wait(pe, pv, 25 * b + 25)
                            wait(pe, ob_a, b)
                        mm(bank[6][:, :], selb[0:32, (ep - 1) * P:ep * P], CT[:, :],
                           start=True, stop=True).then_inc(cb_mm, 1)
                    if e == 1 and not first:
                        turn_out(b - 1)

            def down_product(q, e, t, first):
                if t == 0:
                    wait(pe, eo_a, q if e == 0 else q - 1)
                    if first:
                        wait(pe, wl_v, 2 * e + 2)
                wait(pe, lo_v, HT * q + t + 1)
                wait(pe, hi_a, HT * q + t + 1)
                w = slice(e * HE + t * P, e * HE + (t + 1) * P)
                dst = bank[4 + e % 2]
                mm(dst[:, :], WH[1][:, w], hH[t][:, :], start=(t == 0), stop=False)
                mm(dst[:, :], WH[1][:, w], hL[t][:, :], start=False, stop=False)
                mm(dst[:, :], WL[1][:, w], hH[t][:, :], start=False, stop=(t == HT - 1)).then_inc(dn_mm, 1)

            def turn_out(b):
                wait(pe, fo_v, b + 1)
                wait(pe, ec_v, NE * (b + 1))
                for c in range(4):
                    ins = nc.tensor.transpose(bank[6][:, c * P:(c + 1) * P], fo[:, c * P:(c + 1) * P], ident)
                ins.then_inc(ft_mm, 1)

            pe.wait_ge(s_ffw, 48)
            for piece in NEXT.values():
                piece(0)
            blocks(pe, body_ff)
            for t in range(HT):
                down_product(NB * NX - 1, NX - 1, t, False)
            wait(pe, ec_v, NB * NE - 1)
            mm(bank[6][:, :], selb[0:32, (NE - 1) * P:NE * P], CT[:, :],
               start=True, stop=True).then_inc(cb_mm, 1)
            turn_out(NB - 1)

        @block.scalar
        def _(act):
            f = nc.scalar.activation
            act.wait_ge(s_mod, 32)
            f(cS[:, :], cT[:, :], ACT.Silu).then_inc(cs_a, 1)
            nc.scalar.preload_act_table_set(EXPLN)
            act.wait_ge(s_par, 16)
            act.wait_ge(s_cst, 16)
            na = PAR[:, :].rearrange("p (l n) -> p l n", n=NPAR)[:, :, C_NA]
            f(na, na, ACT.Exp).then_inc(rstd_a, 1)
            act.wait_ge(bn_v, 64)
            f(lnv[:, :], mv[:, :].rearrange("p (n two) -> p n two", two=2)[:, :, 1], ACT.Ln, bias=eps5).then_inc(rstd_a, 1)
            act.wait_ge(rstd_a, 2)
            f(rstd[:, :], lnv[:, :], ACT.Exp, scale=-0.5).then_inc(rstd_a, 1)
            act.wait_ge(mod_v, 6)
            with act.Fori(0, NB) as b:
                hb = act.snap(b * L)
                act.wait_ge(xt_mm, 2 * b + 1)
                f(h[:, bass.ds(hb, L)], bank[0][:, :], ACT.Identity, scale=MOD[:, bass.ds(b + 8, 1)],
                  bias=MOD[:, bass.ds(b, 1)]).then_inc(hup, 1)
                act.wait_ge(xt_mm, 2 * b + 2)
                f(xT[:, bass.ds(hb, L)], bank[1][:, :], ACT.Copy).then_inc(xt_ev, 1)

            def norm_square(n):
                wait(act, dt_mm, n)
                f(WDT[:, :], PAR[:, bass.ds(n // NB * NPAR + C_WDT, 32)], ACT.Copy).then_inc(wdt_a, 1)
                wait(act, hup, n + 1)
                wait(act, ms_mm, n)
                f(sqh[:, :], h[:, bass.ds(n % NB * L, L)], ACT.Square).then_inc(sqh_a, 1)

            def norm_root(n):
                wait(act, ms_mm, n + 1)
                wait(act, hn_v, n)
                f(lnm[:, :], bank[0][:, :], ACT.Ln, bias=eps5).then_inc(rb_a, 1)
                wait(act, rb_a, 2 * n + 1)
                f(rB[:, :], lnm[:, :], ACT.Exp, scale=-0.5).then_inc(rb_a, 1)

            def body(k, A, B, C, N):
                j, i2 = k - 1, k - 2

                def decay_exp(i):
                    wait(act, d_mm, 8 * j + i + 1)
                    wait(act, m_v, 8 * j + i - 1)
                    f(E[i % 2][:, :], bank[2 + i % 2][:, :], ACT.Exp).then_inc(e_a, 1)

                def turned(c):
                    wait(act, t_mm, 4 * j + c + 1)
                    if c == 0:
                        wait(act, px_p, 7 * j)
                        wait(act, st_mm, 2 * j)
                    f(xtok[c][:, :], bank[TURN_BANK[c]][:, 0:384], ACT.Copy).then_inc(t_ev, 1)

                nc.scalar.preload_act_table_set(EXPLN)
                if A:
                    wait(act, dtc_v, 11 * k + 1)
                    f(ax[:, :], u[:, :], ACT.Abs).then_inc(dta_a, 1)
                if B:
                    decay_exp(0)
                if A:
                    wait(act, dta_a, 6 * k + 1)
                    f(ex[:, :], ax[:, :], ACT.Exp, scale=-1.0).then_inc(dta_a, 1)
                if B:
                    decay_exp(1)
                if A:
                    wait(act, dta_a, 6 * k + 2)
                    f(ln1[:, :], ex[:, :], ACT.Ln, bias=1.0).then_inc(dta_a, 1)
                if B:
                    for c in range(3):
                        turned(c)
                if C:
                    for t in range(2):
                        wait(act, fin_p, 4 * i2 + 2 + 2 * t)
                        wait(act, ss_mm, i2)
                        f(sqy[t][:, :], y2[t][:, :], ACT.Square).then_inc(sq_a, 1)
                if B:
                    decay_exp(2)
                    turned(3)
                    decay_exp(3)
                if C:
                    wait(act, ss_mm, i2 + 1)
                    wait(act, o_v, i2)
                    f(lnY[:, :], bank[6][:, :], ACT.Ln, bias=eps5).then_inc(ry_a, 1)
                    wait(act, ry_a, 2 * i2 + 1)
                    f(rY[:, :], lnY[:, :], ACT.Exp, scale=-0.5).then_inc(ry_a, 1)
                if A:
                    wait(act, dtc_v, 11 * k + 4)
                    f(ecs[:, :], cum[:, :], ACT.Exp, scale=-1.0, bias=cum[:, CH - 1:CH]).then_inc(dta_a, 1)
                if N:
                    norm_square(k + 1)
                if B:
                    for i in range(4, 6):
                        decay_exp(i)
                if A:
                    wait(act, silu_a, 6 * k)
                    wait(act, pj_mm, 6 * k + 5)
                    f(zraw[0][:, :], bank[0][:, :], ACT.Copy).then_inc(zc_a, 1)
                if B:
                    wait(act, s_wo, 16 * (j + 1))
                    wait(act, out_mm, j)
                    gw = act.snap(j // NB * NPAR + C_GW)
                    for t in range(2):
                        f(WO[:, t * DM:(t + 1) * DM], WO_raw[:, t * DM:(t + 1) * DM], ACT.Copy,
                          scale=PAR[:, bass.ds(gw + t, 1)]).then_inc(wos_a, 1)
                    for i in range(6, 8):
                        decay_exp(i)
                if N:
                    norm_root(k + 1)
                if A:
                    wait(act, pj_mm, 6 * k + 6)
                    f(zraw[1][:, :], bank[1][:, :], ACT.Copy).then_inc(zc_a, 1)
                    wait(act, tr_mm, k + 1)
                    wait(act, px_p, 7 * k)
                    wait(act, dta_a, 6 * k)
                    f(DTW[:, :], bank[0][:, 0:288], ACT.Copy).then_inc(dta_a, 1)
                if B:
                    wait(act, e2_mm, 2 * j + 1)
                    wait(act, fin_v, 4 * j)
                    f(E2[0][:, :], bank[1][:, 128:512], ACT.Exp).then_inc(e2_a, 1)
                    wait(act, e2_mm, 2 * j + 2)
                    f(E2[1][:, :], bank[4][:, 128:512], ACT.Exp).then_inc(e2_a, 1)
                if A:
                    wait(act, dta_a, 6 * k + 5)
                    wait(act, s_v, 5 * k - 1)
                    f(dec[:, :], DTW[:, 2 * P:], ACT.Exp).then_inc(dta_a, 1)
                    for t in (X0, X1, TB, TC):
                        wait(act, tap_v[t], 4 * (k + 1))
                        if t == X0:
                            wait(act, t_mm, 4 * k)
                            wait(act, dx_v, 2 * k)
                        elif t == TC:
                            wait(act, yi_mm, 2 * k)
                        f(xbc[t][:, :], cv[t][:, :], ACT.Silu).then_inc(silu_a, 1)
                    for t in range(2):
                        if t == 0:
                            wait(act, zc_a, 2 * k + 2)
                        wait(act, fin_p, 4 * (k - 1))
                        f(zs[:, bass.ds((k % 2) * 2 * L + t * L, L)], zraw[t][:, :], ACT.Silu).then_inc(silu_a, 1)

            norm_square(0)
            norm_root(0)
            steps(act, body)

            act.wait_ge(s_ffw, 48)
            act.wait_ge(hup, NB + STEPS)
            act.wait_ge(fin_v, 4 * STEPS)
            for e in range(NX):
                for w in range(2):
                    cs = slice(e * HE, (e + 1) * HE)
                    f(WH[w][:, cs], RAW[w][:, cs], ACT.Copy).then_inc(wh_a, 1)

            def root(n, count, eps):
                f(lnf[:, :], bank[7][:, :], ACT.Ln, bias=eps).then_inc(pa, 1)
                wait(act, pa, 11 * n + count)
                f(rf[:, :], lnf[:, :], ACT.Exp, scale=-0.5).then_inc(pa, 1)

            def square_h(n):
                f(sqf[:, :], h[:, bass.ds(n * L, L)], ACT.Square).then_inc(pa, 1)

            def root_h(n):
                wait(act, pm_mm, 6 * n + 1)
                root(n, 2, eps5)

            def square_x(n):
                wait(act, pv, 25 * n + 3)
                f(sqf[:, :], nT[:, :], ACT.Square).then_inc(pa, 1)

            def root_x(n):
                wait(act, pm_mm, 6 * n + 3)
                root(n, 5, eps5)

            def square_m(n):
                wait(act, pv, 25 * n + 5)
                f(sqf[:, :], nT[:, :], ACT.Square).then_inc(pa, 1)

            def root_m(n):
                wait(act, pm_mm, 6 * n + 4)
                root(n, 8, eps8)

            def halve(n):
                wait(act, pv, 25 * n + 6)
                f(nH[:, bass.ds((n % 2) * L, L)], nT[:, :], ACT.Copy).then_inc(pa, 1)

            def exp_logits(n):
                wait(act, pm_mm, 6 * n + 5)
                f(pr[:, :], bank[7][:, 0:32], ACT.Exp, scale=-1.0).then_inc(pa, 1)

            NEXT = {2: square_h, 6: root_h, 14: square_x, 18: root_x, 22: square_m, 26: root_m, 28: halve, 31: exp_logits}

            def finish(q, e):
                wait(act, dn_mm, HT * (q + 1))
                if e == 0:
                    f(acc, bank[4][:, :], ACT.Identity, bias=PAR2[:, F_B2:F_B2 + 1]).then_inc(eo_a, 1)
                else:
                    f(eb, bank[4 + e % 2][:, :], ACT.Identity,
                      bias=PAR2[:, F_B2 + e:F_B2 + e + 1]).then_inc(eo_a, 1)

            def body_ff(b, prep):
                first = isinstance(b, int) and b == 0
                for e in range(NX):
                    q = b * NX + e
                    for t in range(HT):
                        if t < HT - 1:
                            wait(act, u_mm, HT * q + t + 1)
                            wait(act, lo_v, HT * (q - 1) + t + 1)
                            f(hr[t], bank[t][:, :], ACT.Relu,
                              bias=PAR2[:, F_B1 + HT * e + t:F_B1 + HT * e + t + 1]).then_inc(r_a, 1)
                            wait(act, r_a, 3 * q + t + 1)
                        else:
                            wait(act, r_v, q + 1)
                        wait(act, dn_mm, HT * (q - 1) + t + 1)
                        f(hH[t][:, :], hr[t], ACT.Copy).then_inc(hi_a, 1)
                        if prep and HT * e + t in NEXT:
                            NEXT[HT * e + t](b + 1)
                    if not (first and e == 0):
                        ep = (e - 1) % NX
                        if ep == 0:
                            wait(act, fo_v, b)
                        elif ep == 1:
                            if not first:
                                wait(act, ec_v, NE * b)
                        else:
                            wait(act, ec_v, NE * b + ep - 1 if e > 0 else NE * b - 1)
                        finish(q - 1, ep)
                    if e == 2 and not first:
                        copy_out(b - 1)

            def copy_out(b):
                wait(act, ft_mm, b + 1)
                wait(act, s_out, 16 * b)
                f(ob, bank[6][:, :], ACT.Copy).then_inc(ob_a, 1)

            for piece in NEXT.values():
                piece(0)
            blocks(act, body_ff)
            wait(act, ec_v, NE * NB - 1)
            finish(NB * NX - 1, NX - 1)
            copy_out(NB - 1)

        @block.vector
        def _(dve):
            tt, ts, stt = nc.vector.tensor_tensor, nc.vector.tensor_scalar, nc.vector.scalar_tensor_tensor
            cp = nc.vector.tensor_copy
            nc.vector.memset(mean128[:, :], 1.0 / DM).then_inc(const_v, 1)
            nc.vector.memset(mean256[:, :], 1.0 / DI).then_inc(const_v, 1)
            nc.vector.memset(ones_row[:, :], 1.0).then_inc(const_v, 1)
            nc.vector.memset(onesb[:, :], 1.0).then_inc(const_v, 1)
            dve.wait_ge(s_cst, 16)
            cp(idb[:, :], ident).then_inc(const_v, 1)
            cp(maskb[:, :], CST[:, K_MASK:K_MASK + 512]).then_inc(const_v, 1)
            cp(selb[:, :], CST[:, K_SEL:K_SEL + 1024]).then_inc(const_v, 1)
            ts(nselb[:, :], CST[:, K_SEL:K_SEL + 1024], -1.0, None, ALU.mult).then_inc(const_v, 1)
            cp(selxb[:, :], CST[:, K_SELX:K_SELX + 256]).then_inc(const_v, 1)
            dve.wait_ge(s_x, 64)
            with dve.Fori(0, 32) as n:
                nc.vector.bn_stats(bst[:, bass.ds(n * 6, 6)], xin[:, bass.ds(n * P, P)]).then_inc(bn_v, 1)
            dve.wait_ge(bn_v, 32)
            for n in range(32):
                nc.vector.bn_aggr(mv[:, 2 * n:2 * n + 2], bst[:, 6 * n:6 * n + 6]).then_inc(bn_v, 1)
            dve.wait_ge(mod_mm, 1)
            dve.wait_ge(rstd_a, 1)
            cp(MOD[:, :], bank[4][:, 0:48]).then_inc(mod_v, 1)
            ts(PAR[:, :].rearrange("p (l n) -> p l n", n=NPAR)[:, :, C_NA],
               PAR[:, :].rearrange("p (l n) -> p l n", n=NPAR)[:, :, C_NA], -1.0, None, ALU.mult).then_inc(const_p, 1)
            dve.wait_ge(mod_v, 1)
            m3 = MOD[:, :].rearrange("p (a i b) -> p a i b", a=2, i=3)
            g2 = gsg[:, :].rearrange("p (a b) -> p a b", a=2)
            ts(m3[:, :, 1, :], m3[:, :, 1, :], 1.0, None, ALU.add).then_inc(mod_v, 1)
            ts(g2, m3[:, :, 2, :], 0.0, 2.0, ALU.is_ge, ALU.mult).then_inc(mod_v, 1)
            dve.wait_ge(mod_v, 3)
            ts(g2, g2, -1.0, None, ALU.add).then_inc(mod_v, 1)
            dve.wait_ge(mod_v, 4)
            tt(m3[:, :, 2, :], m3[:, :, 2, :], g2, ALU.mult).then_inc(mod_v, 1)
            dve.wait_ge(mod_v, 5)
            stt(out=m3[:, :, 2, :], in0=m3[:, :, 2, :], scalar=0.25, in1=g2, op0=ALU.max, op1=ALU.mult).then_inc(mod_v, 1)
            dve.wait_ge(rstd_a, 3)
            mvv = mv[:, :].rearrange("p (n two) -> p n two", two=2)

            def normalise(b):
                xb = xin[:, bass.ds(b * L, L)]
                xnv = xn[0][:, :].rearrange("p (n d) -> p n d", d=DM)
                mean = mv[:, bass.ds(b * 8, 8)].rearrange("p (n two) -> p n two", two=2)[:, :, 0:1].to_broadcast([P, 4, DM])
                rs = rstd[:, bass.ds(b * 4, 4)].unsqueeze(2).to_broadcast([P, 4, DM])
                wait(dve, xt_mm, 2 * b)
                tt(xnv, xb.rearrange("p (n d) -> p n d", d=DM), mean, ALU.subtract).then_inc(xn_v, 1)
                wait(dve, xn_v, 3 * b + 1)
                tt(xnv, xnv, rs, ALU.mult).then_inc(xn_v, 1)
                cp(xn[1][:, :], xb).then_inc(xn_v, 1)

            normalise(0)
            with dve.Fori(1, NB) as b:
                normalise(b)

            def body(k, A, B, C, N):
                j, i2 = k - 1, k - 2
                if A:
                    pk = dve.snap(k // NB * NPAR)
                    wait(dve, dt_mm, k + 1)
                    ts(u[:, :], bank[4][:, 0:CH], PAR[:, bass.ds(pk + C_DTB, 1)], None, ALU.add).then_inc(dtc_v, 1)

                def tap(t, s):
                    cw = pk + C_CW + 4 * t
                    src = bank[t % 2]
                    if s == 0:
                        wait(dve, pj_mm, 6 * k + t + 1)
                        wait(dve, silu_a, 6 * (k - 1) + t + 1)
                        ts(cv[t][:, :], src[:, :], PAR[:, bass.ds(cw + 3, 1)], PAR[:, bass.ds(pk + C_CB + t, 1)],
                           ALU.mult, ALU.add).then_inc(tap_v[t], 1)
                    else:
                        wait(dve, tap_v[t], 4 * k + s)
                        stt(out=cv[t][:, s:L], in0=src[:, 0:L - s], scalar=PAR[:, bass.ds(cw + 3 - s, 1)],
                            in1=cv[t][:, s:L], op0=ALU.mult, op1=ALU.add).then_inc(tap_v[t], 1)

                def apply_decay(i):
                    c = i // 2
                    wait(dve, e_a, 8 * j + i + 1)
                    if i == 0:
                        wait(dve, g_mm, j + 1)
                    wait(dve, y_mm, 4 * j + c - 1)
                    tt(M[i % 4][:, :].rearrange("p (n t) -> p n t", n=4),
                       E[i % 2][:, :].rearrange("p (n t) -> p n t", n=4),
                       bank[5][:, c * CH:(c + 1) * CH].unsqueeze(1).to_broadcast([P, 4, CH]),
                       ALU.mult).then_inc(m_v, 1)

                def through(t):
                    wait(dve, silu_a, 6 * j + 1 + t)
                    wait(dve, fin_p, 4 * j - 2 + 2 * t)
                    ts(yt[t][:, :], xbc[t][:, :], PAR[:, bass.ds(pj + C_D + t, 1)], None, ALU.mult).then_inc(dx_v, 1)

                def softplus():
                    wait(dve, dta_a, 6 * k + 3)
                    wait(dve, tr_mm, k)
                    stt(out=dt_[:, :], in0=u[:, :], scalar=0.0, in1=ln1[:, :], op0=ALU.max, op1=ALU.add).then_inc(dtc_v, 1)

                def step_decay():
                    wait(dve, dtc_v, 11 * k + 2)
                    ts(dA[:, :], dt_[:, :], PAR[:, bass.ds(pk + C_NA, 1)], None, ALU.mult).then_inc(dtc_v, 1)

                def running_sum():
                    wait(dve, dtc_v, 11 * k + 3)
                    nc.vector.tensor_tensor_scan(cum[:, :], ones_row[:, :], dA[:, :], 0.0, ALU.mult, ALU.add).then_inc(dtc_v, 1)

                def part_0():
                    wait(dve, dtc_v, 11 * k + 4)
                    cp(p0[:, :], cum[:, :]).then_inc(dtc_v, 1)

                def rest_1():
                    wait(dve, dtc_v, 11 * k + 5)
                    stt(out=r1[:, :], in0=p0[:, :], scalar=CST[:, K_M1:K_M1 + 1], in1=cum[:, :],
                        op0=ALU.mult, op1=ALU.add).then_inc(dtc_v, 1)

                def part_1():
                    wait(dve, dtc_v, 11 * k + 6)
                    cp(p1[:, :], r1[:, :]).then_inc(dtc_v, 1)

                def rest_2():
                    wait(dve, dtc_v, 11 * k + 7)
                    stt(out=r2[:, :], in0=p1[:, :], scalar=CST[:, K_M2:K_M2 + 1], in1=r1[:, :],
                        op0=ALU.mult, op1=ALU.add).then_inc(dtc_v, 1)

                def part_2():
                    wait(dve, dtc_v, 11 * k + 8)
                    wait(dve, p4_in, 64 * k)
                    cp(p2[:, :], r2[:, :]).then_inc(dtc_v, 1)

                def decay_to_end():
                    wait(dve, dta_a, 6 * k + 4)
                    tt(wdec[:, :], dt_[:, :], ecs[:, :], ALU.mult).then_inc(dtc_v, 1)

                def chunk_decay():
                    wait(dve, dtc_v, 11 * k + 9)
                    ts(spend[:, :], CST[:, K_SELD:K_SELD + 32], p2[:, CH - 1:CH], None, ALU.mult).then_inc(dtc_v, 1)

                def scale_out():
                    wait(dve, out_mm, i2 + 1)
                    wait(dve, ry_a, 2 * i2 + 2)
                    wait(dve, hup, NB + i2)
                    tt(o_sb[:, :], bank[7][:, :], rY[:, :], ALU.mult).then_inc(o_v, 1)

                if B:
                    pj = dve.snap(j // NB * NPAR)
                if A:
                    tap(0, 0)
                if B:
                    through(0)
                if A:
                    tap(0, 1)
                    tap(1, 0)
                    tap(0, 2)
                    tap(1, 1)
                    tap(0, 3)
                if B:
                    apply_decay(0)
                if A:
                    softplus()
                    tap(1, 2)
                if B:
                    through(1)
                if B:
                    apply_decay(1)
                if A:
                    step_decay()
                    tap(1, 3)
                    running_sum()
                    tap(2, 0)
                    part_0()
                if B:
                    apply_decay(2)
                if A:
                    tap(2, 1)
                    rest_1()
                if B:
                    apply_decay(3)
                if A:
                    tap(2, 2)
                    part_1()
                    tap(2, 3)
                if C:
                    scale_out()
                if A:
                    tap(3, 0)
                    rest_2()
                    tap(3, 1)
                    part_2()
                    tap(3, 2)
                    decay_to_end()
                    chunk_decay()
                if B:
                    apply_decay(4)
                if A:
                    tap(3, 3)
                if B:
                    for i in range(5, 8):
                        apply_decay(i)
                if N:
                    norm_apply(k + 1)
                if B:
                    wait(dve, st_mm, 2 * j + 1)
                    wait(dve, yi_mm, 2 * j)
                    cp(S[1][:, :], bank[4][:, 0:DI]).then_inc(s_v, 1)
                    for c in range(2, NC):
                        wait(dve, s_v, 5 * j + 2 * c - 3)
                        tt(stmp[:, :].rearrange("p (h d) -> p h d", h=NH), S[c - 1][:, :].rearrange("p (h d) -> p h d", h=NH),
                           dec[:, (c - 1) * NH:c * NH].unsqueeze(2).to_broadcast([P, NH, HD]), ALU.mult).then_inc(s_v, 1)
                        wait(dve, s_v, 5 * j + 2 * c - 2)
                        if c == 3:
                            wait(dve, st_mm, 2 * j + 2)
                        new = bank[4][:, DI:2 * DI] if c == 2 else bank[5][:, 0:DI]
                        tt(S[c][:, :], stmp[:, :], new, ALU.add).then_inc(s_v, 1)
                    for t in range(2):
                        if t == 0:
                            wait(dve, y_mm, 4 * j + 4)
                        wait(dve, dx_v, 2 * j + 1 + t)
                        tt(yt[t][:, :], yt[t][:, :], bank[6 + t][:, :], ALU.add).then_inc(fin_v, 1)
                    for t in range(2):
                        wait(dve, yi_mm, 2 * j + 1 + t)
                        wait(dve, e2_a, 2 * j + 1 + t)
                        tt(ti[t][:, :], bank[2 + t][:, 128:512], E2[t][:, :], ALU.mult).then_inc(fin_v, 1)

            def norm_apply(n):
                wait(dve, rb_a, 2 * n + 2)
                wait(dve, pj_mm, 6 * n)
                stt(out=hn[:, :], in0=h[:, bass.ds(n % NB * L, L)], scalar=PAR[:, bass.ds(n // NB * NPAR + C_BNW, 1)],
                    in1=rB[:, :], op0=ALU.mult, op1=ALU.mult).then_inc(hn_v, 1)

            norm_apply(0)
            steps(dve, body)

            dve.wait_ge(s_ffw, 48)
            dve.wait_ge(hup, NB + STEPS)
            tt(gaf[:, :], MOD[:, 16:24], PAR2[:, F_FW:F_FW + 1].to_broadcast([P, NB]), ALU.mult).then_inc(c3_v, 1)
            nc.vector.memset(C3[:, :], 0.0).then_inc(c3_v, 1)
            dve.wait_ge(c3_v, 2)

            def v(ins, n=0, own=None):
                ins.then_inc(pv, 1)
                if own:
                    wait(dve, pv, 25 * n + own)

            def four(t):
                return t[:, :].rearrange("p (s e) -> p s e", s=4)

            def pairs(t):
                return t[:, :].rearrange("p (s e f) -> p s e f", s=4, e=NE)

            def add_mamba(n):
                xb = xT[:, bass.ds(n * L, L)]
                wait(dve, pa, 11 * n + 3)
                wait(dve, pv, 25 * n - 18)
                v(stt(out=nT[:, :], in0=h[:, bass.ds(n * L, L)], scalar=gaf[:, bass.ds(n, 1)], in1=rf[:, :],
                      op0=ALU.mult, op1=ALU.mult), n, 1)
                v(tt(xb, nT[:, :], xb, ALU.add), n, 2)

            def centre(n):
                wait(dve, pm_mm, 6 * n + 2)
                v(tt(nT[:, :], xT[:, bass.ds(n * L, L)], bank[7][:, :], ALU.subtract))

            def modulate(n):
                wait(dve, pa, 11 * n + 6)
                v(tt(nT[:, :], nT[:, :], rf[:, :], ALU.mult), n, 4)
                v(ts(nT[:, :], nT[:, :], MOD[:, bass.ds(n + 32, 1)], MOD[:, bass.ds(n + 24, 1)], ALU.mult, ALU.add))

            def scale(n):
                wait(dve, pa, 11 * n + 9)
                v(stt(out=nT[:, :], in0=nT[:, :], scalar=PAR2[:, F_NW:F_NW + 1], in1=rf[:, :], op0=ALU.mult, op1=ALU.mult))

            def halve(n):
                par = bass.ds((n % 2) * L, L)
                wait(dve, pa, 11 * n + 10)
                v(tt(nL[:, par], nT[:, :], nH[:, par].bitcast(F32), ALU.subtract))

            def sigmoid(n):
                wait(dve, pa, 11 * n + 11)
                v(ts(prx[:, :], pr[:, :], 1.0, None, ALU.add), n, 8)
                v(nc.vector.reciprocal(pm[:, :], prx[:, :]), n, 9)

            def rank(n):
                inner, outer = four(pm).unsqueeze(2).to_broadcast([P, 4, NE, NE]), four(pm).unsqueeze(3).to_broadcast([P, 4, NE, NE])
                tri = CST[:, K_TRI:K_TRI + 64].rearrange("p (e f) -> p e f", e=NE).unsqueeze(1).to_broadcast([P, 4, NE, NE])
                v(tt(pairs(cgt), inner, outer, ALU.is_gt))
                v(tt(pairs(ceq), inner, outer, ALU.is_equal), n, 11)
                v(tt(pairs(ceq), pairs(ceq), tri, ALU.mult), n, 12)
                v(tt(cgt[:, :], cgt[:, :], ceq[:, :], ALU.add), n, 13)
                v(nc.vector.tensor_reduce(rnk[:, :], cgt[:, :].rearrange("p (q f) -> p q f", f=NE), AX.X, ALU.add), n, 14)

            def routing(n):
                v(stt(out=pm[:, :], in0=rnk[:, :], scalar=1.5, in1=pm[:, :], op0=ALU.is_lt, op1=ALU.mult), n, 15)
                v(nc.vector.tensor_reduce(csum[:, :], four(pm), AX.X, ALU.add), n, 16)
                v(ts(csum[:, :], csum[:, :], 1e-6, None, ALU.add), n, 17)
                v(nc.vector.reciprocal(csum[:, :], csum[:, :]), n, 18)
                v(tt(four(cmb), four(pm), csum[:, :].unsqueeze(2).to_broadcast([P, 4, NE]), ALU.mult), n, 19)

            def parts(n):
                c3 = C3[:, :].rearrange("p (s q e) -> p s q e", s=4, q=4)
                wait(dve, pm_mm, 6 * n)
                v(cp(c3[:, :, 0, :], four(cmb)), n, 20)
                v(tt(four(cr), four(cmb), c3[:, :, 0, :], ALU.subtract), n, 21)
                v(cp(c3[:, :, 1, :], four(cr)), n, 22)
                v(tt(four(cr), four(cr), c3[:, :, 1, :], ALU.subtract), n, 23)
                v(cp(c3[:, :, 2, :], four(cr)))

            def weights_in(n):
                wait(dve, pm_mm, 6 * n + 6)
                wait(dve, cb_mm, NE * n)
                v(cp(CT[:, :], bank[7][:, :].bitcast(BF16)[0:32, 0:L]))

            NEXT = {8: add_mamba, 12: centre, 20: modulate, 27: scale, 29: halve, 32: sigmoid, 33: rank, 34: routing, 35: parts}
            OWN = {4: weights_in}

            def weigh(q, b, e):
                count = NE * b + e
                wait(dve, cb_mm, count)
                wait(dve, eo_a, q + 1)
                wait(dve, acc_p, count - 1)
                tt(ec, bank[6][:, :], eb, ALU.mult).then_inc(ec_v, 1)

            def finish(b):
                wait(dve, acc_p, NE * (b + 1))
                wait(dve, ft_mm, b)
                stt(out=fo, in0=acc, scalar=MOD[:, bass.ds(b + 40, 1)], in1=xT[:, bass.ds(b * L, L)],
                    op0=ALU.mult, op1=ALU.add).then_inc(fo_v, 1)

            def body_ff(b, prep):
                first = isinstance(b, int) and b == 0
                for e in range(NX):
                    q = b * NX + e
                    for t in range(HT):
                        if t == HT - 1:
                            wait(dve, u_mm, HT * q + t + 1)
                            wait(dve, hi_a, HT * q)
                            wait(dve, lo_v, HT * q)
                            ts(hr[t], bank[t][:, :], PAR2[:, F_B1 + HT * e + t:F_B1 + HT * e + t + 1], 0.0,
                               ALU.add, ALU.max).then_inc(r_v, 1)
                        if t == 1:
                            if e > 2:
                                weigh(q - 2, b, e - 2)
                            elif e == 0 and not first:
                                weigh(q - 2, b - 1, NE - 1)
                        wait(dve, hi_a, HT * q + t + 1)
                        wait(dve, dn_mm, HT * (q - 1) + t + 1)
                        tt(hL[t][:, :], hr[t], hH[t][:, :].bitcast(F32), ALU.subtract).then_inc(lo_v, 1)
                        if e == 1 and t == 2 and not first:
                            weigh(q - 2, b - 1, NE)
                        if e == 1 and t == 3 and not first:
                            finish(b - 1)
                        if prep and HT * e + t in NEXT:
                            NEXT[HT * e + t](b + 1)
                        if HT * e + t in OWN:
                            OWN[HT * e + t](b)

            for e in range(NX):
                for w in range(2):
                    cs = slice(e * HE, (e + 1) * HE)
                    wait(dve, wh_a, 2 * e + w + 1)
                    tt(WL[w][:, cs], RAW[w][:, cs], WH[w][:, cs].bitcast(F32), ALU.subtract).then_inc(wl_v, 1)
            for piece in NEXT.values():
                piece(0)
            blocks(dve, body_ff)
            weigh(NB * NX - 2, NB - 1, NE - 1)
            weigh(NB * NX - 1, NB - 1, NE)
            finish(NB - 1)

        @block.gpsimd
        def _(pool):
            tt = nc.gpsimd.tensor_tensor

            def body(k, A, B, C, N):
                j, i2 = k - 1, k - 2
                if B:
                    wait(pool, dta_a, 6 * j + 5)
                    for c in range(NC):
                        xv = xtok[c][:, 0:DI].rearrange("p (h d) -> p h d", h=NH)
                        wait(pool, t_ev, 4 * j + c + 1)
                        wait(pool, y_mm, 4 * j - 3 + c)
                        tt(dtx[c][:, :].rearrange("p (h d) -> p h d", h=NH), xv,
                           DTW[:, 32 * c:32 * c + NH].unsqueeze(2).to_broadcast([P, NH, HD]), ALU.mult).then_inc(px_p, 1)
                        if c < NC - 1:
                            if c == 0:
                                wait(pool, st_mm, 2 * j)
                            tt(xw[c][:, :].rearrange("p (h d) -> p h d", h=NH), xv,
                               DTW[:, P + 32 * c:P + 32 * c + NH].unsqueeze(2).to_broadcast([P, NH, HD]),
                               ALU.mult).then_inc(px_p, 1)
                if C:
                    hb = h[:, bass.ds(i2 % NB * L, L)]
                    wait(pool, o_v, i2 + 1)
                    tt(hb, hb, o_sb[:, :], ALU.add).then_inc(hup, 1)
                if B:
                    for t in range(2):
                        wait(pool, fin_v, 4 * j + 3 + t)
                        tt(yt[t][:, 128:512], yt[t][:, 128:512], ti[t][:, :], ALU.add).then_inc(fin_p, 1)
                        wait(pool, fin_p, 4 * j + 1 + 2 * t)
                        wait(pool, silu_a, 6 * j + 5 + t)
                        wait(pool, out_mm, j)
                        tt(y2[t][:, :], yt[t][:, :], zs[:, bass.ds((j % 2) * 2 * L + t * L, L)], ALU.mult).then_inc(fin_p, 1)

            steps(pool, body)

            def add_expert(count, b):
                wait(pool, ec_v, count)
                wait(pool, eo_a, NX * b + 1)
                tt(acc, acc, ec, ALU.add).then_inc(acc_p, 1)

            for e in range(1, NX):
                add_expert(e, 0)
            with pool.Fori(1, NB) as b:
                for e in range(1, NX):
                    add_expert(NE * b + e, b)


def constants():
    import numpy as np
    c = np.zeros((P, NCST), np.float32)
    p, t = np.arange(P)[:, None], np.arange(P)[None, :]
    c[:, K_ID:K_ID + P] = p == t
    c[:, K_MASK:K_MASK + 512] = np.tile(np.where(t >= p, 0.0, -1e30), (1, 4))
    row, head = p % 32, p % 8
    used = row < 24
    c[:, K_SEL:K_SEL + 1024] = used & (head == np.arange(1024)[None, :] // P)
    c[:, K_SELX:K_SELX + 256] = used & (head == np.arange(256)[None, :] // HD)
    q = np.arange(32)[None, :]
    c[:, K_SELD:K_SELD + 32] = used & (head == q % 8) & (p // 32 == q // 8)
    c[:, K_M1] = -(row[:, 0] >= 8).astype(np.float32)
    c[:, K_M2] = -(row[:, 0] >= 16).astype(np.float32)
    c[:, K_EPS5], c[:, K_EPS8] = 1e-5, 1e-8
    e = np.arange(64)[None, :]
    c[:, K_TRI:K_TRI + 64] = (e % 8) < (e // 8)
    return c


def parameters(v):
    import numpy as np
    out = np.zeros((P, NL, NPAR), np.float32)
    w_dt = v["L0_attn_W_in"][:, :, 768:776]
    for part in range(3):
        out[:, :, C_WDT + 8 * part:C_WDT + 8 * part + 8] = w_dt.transpose(1, 0, 2)
        for c in range(NC):
            q = 32 * c + 8 * part
            out[q:q + 8, :, C_DTB] = v["L0_attn_dt_bias"].T
            out[q:q + 8, :, C_NA] = v["L0_attn_A_log"].T
    out[:, :, C_BNW] = v["L0_attn_block_norm_w"].T
    cw = v["L0_attn_conv_w"].reshape(NL, 4, P, 4)
    out[:, :, C_CW:C_CW + 16] = cw.transpose(2, 0, 1, 3).reshape(P, NL, 16)
    out[:, :, C_CB:C_CB + 4] = v["L0_attn_conv_b"].reshape(NL, 4, P).transpose(2, 0, 1)
    out[:, :, C_D:C_D + 2] = np.repeat(v["L0_attn_D"], HD, axis=1).reshape(NL, 2, P).transpose(2, 0, 1)
    out[:, :, C_GW:C_GW + 2] = v["L0_attn_gate_norm_w"].reshape(NL, 2, P).transpose(2, 0, 1)
    return out.reshape(P, NL * NPAR)


def feed_forward(v):
    import numpy as np
    out = np.zeros((P, NPAR2), np.float32)
    b1 = np.concatenate([v["L0_ffn_sb1"][None], v["L0_ffn_eb1"]])
    out[:, F_B1:F_B1 + NX * HT] = b1.reshape(NX * HT, P).T
    out[:, F_B2:F_B2 + NX] = np.concatenate([v["L0_ffn_sb2"][None], v["L0_ffn_eb2"]]).T
    out[:, F_NW] = v["L0_ffn_norm_weight"]
    out[:, F_FW] = v["L0_attn_final_norm_w"]
    out[:, F_RW:F_RW + NE] = v["L0_ffn_router_w"].T
    w1 = np.concatenate([v["L0_ffn_sw1"][None], v["L0_ffn_ew1"]]).transpose(1, 0, 2).reshape(P, NX * HE)
    w2 = np.concatenate([v["L0_ffn_sw2"][None], v["L0_ffn_ew2"]]).reshape(NX, HT, P, DM)
    w2 = w2.transpose(2, 0, 1, 3).reshape(P, NX * HE)
    return out, np.ascontiguousarray(w1), np.ascontiguousarray(w2)


def projection(v):
    import numpy as np
    return np.stack([v["L0_attn_W_in"][:, :, c:c + P] for c in W_COL], axis=1).reshape(-1)


def kernel(**inputs):
    import numpy as np
    import concourse.bacc as bacc
    from concourse.bass_utils import run_bass_kernel_spmd

    v = {n: np.asarray(a) for n, a in inputs.items()}
    par2, w1, w2 = feed_forward(v)
    arrays = {
        "x_in": v["L0_attn_x"].reshape(NB * L, DM),
        "w_in": projection(v),
        "w_out": v["L0_attn_W_out"].reshape(NL, 2, P, DM).transpose(0, 2, 1, 3).reshape(-1),
        "par_in": parameters(v),
        "cst_in": constants(),
        "c_in": np.ascontiguousarray(v["L0_c"].T),
        "wmod_in": v["L0_wmod"],
        "par2_in": par2,
        "w1_in": w1,
        "w2_in": w2,
    }
    arrays = {n: np.ascontiguousarray(a) for n, a in arrays.items()}
    nc = bacc.Bacc("TRN2", target_bir_lowering=False, num_devices=1)
    args = [nc.dram_tensor(n, a.shape, mybir.dt.from_np(a.dtype), kind="ExternalInput").ap() for n, a in arrays.items()]
    out = nc.dram_tensor("out", (NB * L, DM), F32, kind="ExternalOutput").ap()
    build(nc, *args, out)
    r = run_bass_kernel_spmd(nc, [arrays], core_ids=[0])
    return r.results[0]["out"].reshape(NB, L, DM)
```

```python
import concourse.bass as bass
from concourse import mybir
from contextlib import ExitStack

F32 = mybir.dt.float32
BF16 = mybir.dt.bfloat16
F32R = mybir.dt.float32r
ACT = mybir.ActivationFunctionType
ALU = mybir.AluOpType
AX = mybir.AxisListType

P = 128
NB, L, DM = 8, 512, 128
NL, DI, NH, HD, DS = 4, 256, 8, 32, 128
CH = 128
NC = L // CH
NE, HE = 8, 512
STEPS = NL * NB
EXPLN = "natural_log_exp_and_others"

C_WDT, C_BNW, C_CW, C_CB, C_DTB, C_NA, C_D, C_GW = 0, 32, 33, 49, 53, 54, 55, 57
NPAR = 60
NX = NE + 1
HT = HE // P
F_B1, F_B2, F_NW, F_FW, F_RW = 0, NX * HT, NX * HT + NX, NX * HT + NX + 1, NX * HT + NX + 2
NPAR2 = F_RW + NE
K_ID, K_MASK, K_SEL, K_SELX = 0, 128, 640, 1664
K_SELD, K_M1, K_M2, K_EPS5, K_EPS8, K_TRI = 1920, 1952, 1953, 1954, 1955, 1956
NCST = K_TRI + 64
W_COL = [DI, DI + P, 2 * DI, 2 * DI + DS, 0, P]
X0, X1, TB, TC = 0, 1, 2, 3
SILU_TURN = [3, 4, 0, 5]
TURN_BANK = [4, 6, 7, 4]


def wait(eng, sem, value):
    if isinstance(value, int) and value <= 0:
        return
    eng.wait_ge(sem, value)


def build(nc, x, w_in, w_out, par, cst, c_t, wmod, par2, w1, w2, out):
    ctx = ExitStack()
    with ctx:
        scope = [ctx]

        def sb(name, cols, dt=F32, parts=P):
            return scope[0].enter_context(nc.sbuf_tensor(name, [parts, cols], dt))

        def sem(name):
            return ctx.enter_context(nc.semaphore(name))

        bank = [ctx.enter_context(nc.psum_tensor(f"bank{i}", [P, 512], F32)) for i in range(8)]

        h = sb("h", NB * L)
        xT = sb("xT", NB * L)
        PAR = sb("PAR", NL * NPAR)
        CST = sb("CST", NCST)
        MOD = sb("MOD", 48)
        ident = CST[:, K_ID:K_ID + P]
        eps5, eps8 = CST[:, K_EPS5:K_EPS5 + 1], CST[:, K_EPS8:K_EPS8 + 1]
        mean128 = sb("mean128", P)
        mean256 = sb("mean256", P)
        idb, onesb = sb("idb", P, BF16), sb("onesb", P, BF16)
        maskb = sb("maskb", 512, BF16)
        selb = sb("selb", 1024, BF16)
        selxb = sb("selxb", 256, BF16)
        ones_row = sb("ones_row", P)
        PAR2 = sb("PAR2", NPAR2)
        RAW = [sb(f"RAW{w}", NX * HE) for w in range(2)]
        scope[0] = ExitStack()
        xin = sb("xin", NB * L)
        bst, mv, rstd, lnv = sb("bst", 32 * 6), sb("mv", 64), sb("rstd", 32), sb("lnv", 32)
        cT, cS, wm = sb("cT", NB), sb("cS", NB), sb("wm", 6 * DM)
        gsg = sb("gsg", 16)
        scope[0].close()
        scope[0] = ctx
        nH, nL = sb("nH", 2 * L, F32R), sb("nL", 2 * L, F32R)
        sqf, lnf, rf, nT = sb("sqf", L), sb("lnf", L), sb("rf", L), sb("nT", L)
        pr, prx, rnk, pm, cmb, cr = [sb(n, 32) for n in ("pr", "prx", "rnk", "pm", "cmb", "cr")]
        cgt, ceq = sb("cgt", 256), sb("ceq", 256)
        csum = sb("csum", 4)
        C3 = sb("C3", P, BF16)
        CT = sb("CT", L, BF16, parts=32)
        B2 = sb("B2", NX)
        nb1 = sb("nb1", NX)
        gaf = sb("gaf", NB)
        scope[0] = ExitStack()
        stmp = sb("stmp", DI)
        nselb = sb("nselb", 1024, BF16)
        WA = [sb(f"WA{t}", P) for t in range(6)]
        WDT = sb("WDT", 32)
        WO_raw = sb("WO_raw", 2 * DM)
        sqh, lnm, rB, hn = sb("sqh", L), sb("lnm", L), sb("rB", L), sb("hn", L)
        cv = [sb(f"cv{t}", L) for t in range(4)]
        xbc = [sb(f"xbc{t}", L) for t in range(4)]
        zraw = [sb(f"zraw{t}", L) for t in range(2)]
        u, ax, ex, ln1 = sb("u", P), sb("ax", P), sb("ex", P), sb("ln1", P)
        dt_, dA, cum, r1, r2 = sb("dt_", P), sb("dA", P), sb("cum", P), sb("r1", P), sb("r2", P)
        p0, p1, p2 = sb("p0", P, BF16), sb("p1", P, BF16), sb("p2", P, BF16)
        ecs, wdec, spend = sb("ecs", P), sb("wdec", P), sb("spend", 32, BF16)
        P4 = sb("P4", L, BF16, parts=32)
        DTW, dec = sb("DTW", 2 * P + 32), sb("dec", 32)
        xtok = [sb(f"xtok{c}", 384) for c in range(NC)]
        dtx = [sb(f"dtx{c}", DI) for c in range(NC)]
        xw = [sb(f"xw{c}", DI) for c in range(NC - 1)]
        E = [sb(f"E{g}", 512) for g in range(2)]
        M = [sb(f"M{i}", 512) for i in range(4)]
        S = [None] + [sb(f"S{c}", DI) for c in range(1, NC)]
        E2 = [sb(f"E2_{t}", 384) for t in range(2)]
        zs = sb("zs", 2 * 2 * L)
        yt = [sb(f"yt{t}", L) for t in range(2)]
        ti = [sb(f"ti{t}", 384) for t in range(2)]
        WO = sb("WO", 2 * DM)
        y2 = [sb(f"y2_{t}", L) for t in range(2)]
        sqy = [sb(f"sqy{t}", L) for t in range(2)]
        lnY, rY, o_sb = sb("lnY", L), sb("rY", L), sb("o_sb", L)
        xn = sqy
        scope[0].close()

        scope[0] = ctx
        WH = [sb(f"WH{w}", NX * HE, F32R) for w in range(2)]
        WL = [sb(f"WL{w}", NX * HE, F32R) for w in range(2)]
        hr = [RAW[0][:, t * L:(t + 1) * L] for t in range(HT - 1)]
        hH = [sb(f"hH{t}", L, F32R) for t in range(HT)]
        hL = [sb(f"hL{t}", L, F32R) for t in range(HT)]
        es, eb, ec, acc, fo, ob = [RAW[1][:, t * L:(t + 1) * L] for t in range(6)]

        def prep_bank(n):
            return bank[0 if isinstance(n, int) and n == 0 else 7]

        s_x = [sem(f"x{q}_in") for q in range(4)]
        s_cst, s_par, s_mod = sem("cst_in"), sem("par_in"), sem("mod_in")
        const_v, const_p = sem("const_v"), sem("const_p")
        bn_v, rstd_a, xn_v, xt_mm, xt_ev = sem("bn_v"), sem("rstd_a"), sem("xn_v"), sem("xt_mm"), sem("xt_ev")
        xr_mm = sem("xr_mm")
        cs_a, mod_mm, mod_v = sem("cs_a"), sem("mod_mm"), sem("mod_v")
        wa = [sem(f"wa{t}") for t in range(6)]
        zc_a, dec_a = sem("zc_a"), sem("dec_a")
        tap_v = [sem(f"tap{t}_v") for t in range(4)]
        s_wo, p4_in = sem("wo_in"), sem("p4_in")
        wdt_a, hup, sqh_a, ms_mm, rb_a, hn_v = sem("wdt_a"), sem("hup"), sem("sqh_a"), sem("ms_mm"), sem("rb_a"), sem("hn_v")
        dt_mm, pj_mm, silu_a, dtc_v, dta_a, tr_mm = sem("dt_mm"), sem("pj_mm"), sem("silu_a"), sem("dtc_v"), sem("dta_a"), sem("tr_mm")
        g_mm, t_mm, t_ev, d_mm, e_a, m_v, y_mm = sem("g_mm"), sem("t_mm"), sem("t_ev"), sem("d_mm"), sem("e_a"), sem("m_v"), sem("y_mm")
        px_p, st_mm, s_v, e2_mm, e2_a, yi_mm = sem("px_p"), sem("st_mm"), sem("s_v"), sem("e2_mm"), sem("e2_a"), sem("yi_mm")
        fin_v, fin_p, wos_a = sem("fin_v"), sem("fin_p"), sem("wos_a")
        sq_a, ss_mm, ry_a, out_mm, o_v = sem("sq_a"), sem("ss_mm"), sem("ry_a"), sem("out_mm"), sem("o_v")
        s_ffw, s_out = sem("ffw_in"), sem("out_done")
        wh_a, wl_v, wl_p, c3_v = sem("wh_a"), sem("wl_v"), sem("wl_p"), sem("c3_v")
        pa, pv, pm_mm = sem("prep_a"), sem("prep_v"), sem("prep_mm")
        u_mm, r_a, hi_v, lo_v, dn_mm = sem("u_mm"), sem("r_a"), sem("hi_v"), sem("lo_v"), sem("dn_mm")
        bc_mm, b2_v = sem("bc_mm"), sem("b2_v")
        cb_mm, eo_a, ec_v, acc_p, fo_v, ft_mm, ob_a = [sem(n) for n in ("cb_mm", "eo_a", "ec_v", "acc_p", "fo_v", "ft_mm", "ob_a")]

        def steps(eng, body):
            body(0, A=True, B=False, C=False, N=True)
            body(1, A=True, B=True, C=False, N=True)
            body(2, A=True, B=True, C=True, N=True)
            with eng.Fori(3, STEPS - 1) as k:
                body(k, A=True, B=True, C=True, N=True)
            body(STEPS - 1, A=True, B=True, C=True, N=False)
            body(STEPS, A=False, B=True, C=True, N=False)
            body(STEPS + 1, A=False, B=False, C=True, N=False)

        def blocks(eng, body):
            body(0, prep=True)
            body(1, prep=True)
            with eng.Fori(2, NB - 1) as b:
                body(b, prep=True)
            body(NB - 1, prep=False)

        block = ctx.enter_context(nc.Block())

        @block.sync
        def _(sp):
            def rows(src, at, n):
                return src[bass.ds(at, P * n)].rearrange("(p n) -> p n", n=n)

            def load_input(q):
                sp.dma_start(xin[:, q * 1024:(q + 1) * 1024].rearrange("p (n d) -> p n d", d=DM),
                             x[q * 1024:(q + 1) * 1024, :].rearrange("(n p) d -> p n d", p=P)).then_inc(s_x[q], 16)

            load_input(0)
            sp.dma_start(CST[:, :], cst).then_inc(s_cst, 16)
            sp.dma_start(cT[:, :], c_t).then_inc(s_mod, 16)
            sp.dma_start(wm[:, :], wmod).then_inc(s_mod, 16)
            for q in range(1, 4):
                load_input(q)
            sp.dma_start(PAR[:, :], par).then_inc(s_par, 16)
            for t in range(6):
                sp.dma_start(WA[t][:, :], rows(w_in, t * P * P, P)).then_inc(wa[t], 16)
            sp.dma_start(PAR2[:, :], par2).then_inc(s_ffw, 16)
            for w, src in enumerate((w1, w2)):
                sp.dma_start(RAW[w][:, :], src).then_inc(s_ffw, 16)

            def body(k, A, B, C, N):
                if B:
                    j = k - 1
                    at_j = sp.snap(j // NB * (2 * DM * P))
                    wait(sp, wos_a, 2 * j)
                    sp.dma_start(WO_raw[:, :], rows(w_out, at_j, 2 * DM)).then_inc(s_wo, 16)
                if N:
                    at = [sp.snap((k + 1) // NB * (6 * P * P) + t * P * P) for t in range(6)]
                for t in range(6):
                    if N:
                        wait(sp, pj_mm, 6 * k + t + 1)
                        sp.dma_start(WA[t][:, :], rows(w_in, at[t], P)).then_inc(wa[t], 16)
                if A:
                    if B:
                        wait(sp, d_mm, 8 * k)
                    wait(sp, dtc_v, 11 * k + 9)
                    for c in range(NC):
                        sp.dma_start(P4[:, c * CH:(c + 1) * CH], p2[32 * c:32 * c + 32, :]).then_inc(p4_in, 16)

            steps(sp, body)

            sp.wait_ge(s_ffw, 48)

            def store(b):
                first_row = sp.snap(b * L)
                sp.wait_ge(ob_a, b + 1)
                sp.dma_start(out[bass.ds(first_row, L), :].rearrange("(s p) d -> p s d", p=P),
                             ob.rearrange("p (s d) -> p s d", s=4)).then_inc(s_out, 16)

            store(0)
            with sp.Fori(1, NB) as b:
                store(b)
            sp.wait_ge(s_out, 16 * NB)

        @block.tensor
        def _(pe):
            mm = nc.tensor.matmul
            pe.wait_ge(cs_a, 1)
            pe.wait_ge(s_mod, 32)
            for i in range(6):
                ins = mm(bank[4][:, 8 * i:8 * i + 8], wm[:, i * DM:(i + 1) * DM], cS[:, :], start=True, stop=True)
            ins.then_inc(mod_mm, 1)
            pe.wait_ge(s_cst, 16)
            for q in range(4):
                pe.wait_ge(s_x[q], 16)
                for odd in range(2):
                    wait(pe, xt_ev, 2 * q + odd - 1)
                    for n in range(4):
                        at = ((2 * q + odd) * 4 + n) * P
                        ins = nc.tensor.transpose(bank[2 * odd + 1][:, n * P:(n + 1) * P], xin[:, at:at + P], ident)
                    ins.then_inc(xr_mm, 1)

            def turn_input(b, odd):
                wait(pe, xn_v, b + 1)
                wait(pe, hup, b - 1)
                for n in range(4):
                    ins = nc.tensor.transpose(bank[2 + 4 * odd][:, n * P:(n + 1) * P], xn[odd][:, n * P:(n + 1) * P], ident)
                ins.then_inc(xt_mm, 1)

            for b in range(4):
                turn_input(b, b % 2)
            pe.wait_ge(const_v, 2)
            pe.wait_ge(sqh_a, 1)
            mm(bank[0][:, :], mean128[:, :], sqh[:, :], start=True, stop=True).then_inc(ms_mm, 1)
            with pe.Fori(2, NB // 2) as i:
                turn_input(2 * i, 0)
                turn_input(2 * i + 1, 1)

            def square_mean(n):
                wait(pe, pa, 11 * n + 1)
                wait(pe, pv, 25 * n)
                mm(prep_bank(n)[:, :], mean128[:, :], sqf[:, :], start=True, stop=True).then_inc(pm_mm, 1)

            def mean(n):
                wait(pe, pv, 25 * n + 2)
                wait(pe, pa, 11 * n + 2)
                wait(pe, ob_a, n - 1)
                mm(prep_bank(n)[:, :], mean128[:, :], xT[:, bass.ds(n * L, L)], start=True, stop=True).then_inc(pm_mm, 1)

            def variance(n):
                wait(pe, pa, 11 * n + 4)
                mm(prep_bank(n)[:, :], mean128[:, :], sqf[:, :], start=True, stop=True).then_inc(pm_mm, 1)

            def square_mean_2(n):
                wait(pe, pa, 11 * n + 7)
                mm(prep_bank(n)[:, :], mean128[:, :], sqf[:, :], start=True, stop=True).then_inc(pm_mm, 1)

            def logits(n):
                wait(pe, pv, 25 * n + 6)
                for c in range(4):
                    ins = mm(prep_bank(n)[:, 8 * c:8 * c + 8], nT[:, c * P:(c + 1) * P], PAR2[:, F_RW:F_RW + NE],
                             start=True, stop=True)
                ins.then_inc(pm_mm, 1)

            NEXT = {9: square_mean, 15: mean, 19: variance, 25: square_mean_2, 31: logits}
            prepare = list(NEXT.values())

            def body(k, A, B, C, N):
                j, i2 = k - 1, k - 2
                if B and not A:
                    wait(pe, dta_a, 5 * STEPS)
                    prepare[1](0)
                    pe.wait_ge(s_ffw, 48)
                    wait(pe, zc_a, 2 * STEPS)
                    for e in range(NX):
                        ins = mm(bank[1][:, e:e + 1], RAW[1][:, e * HE + (HT - 1) * P:(e + 1) * HE],
                                 PAR2[:, F_B1 + HT * e + HT - 1:F_B1 + HT * e + HT], start=True, stop=True)
                    ins.then_inc(bc_mm, 1)
                if A:
                    wait(pe, hn_v, k + 1)
                    wait(pe, wdt_a, k + 1)
                    wait(pe, s_v, 5 * j - 2)
                    for c in range(NC):
                        ins = mm(bank[4][32 * c:32 * c + 32, 0:CH], WDT[:, :], hn[:, c * CH:(c + 1) * CH],
                                 start=True, stop=True, tile_position=(0, 32 * c))
                    ins.then_inc(dt_mm, 1)

                def project(t):
                    wait(pe, wa[t], 16 * (k + 1))
                    wait(pe, tap_v[t - 2], 4 * (k + 1))
                    mm(bank[t % 2][:, :], WA[t][:, :], hn[:, :], start=True, stop=True).then_inc(pj_mm, 1)

                def square_mean():
                    wait(pe, sq_a, 2 * (i2 + 1))
                    if B:
                        wait(pe, t_ev, 4 * j + 2)
                    else:
                        wait(pe, fin_v, 4 * (i2 + 1))
                    mm(bank[6][:, :], mean256[:, :], sqy[0][:, :], start=True, stop=False)
                    mm(bank[6][:, :], mean256[:, :], sqy[1][:, :], start=False, stop=True).then_inc(ss_mm, 1)

                def project_out():
                    wait(pe, wos_a, 2 * (i2 + 1))
                    if B:
                        wait(pe, t_ev, 4 * j + 3)
                    mm(bank[7][:, :], WO[:, 0:DM], y2[0][:, :], start=True, stop=False)
                    mm(bank[7][:, :], WO[:, DM:2 * DM], y2[1][:, :], start=False, stop=True).then_inc(out_mm, 1)

                def turn(c):
                    if c == 0:
                        if A:
                            wait(pe, dtc_v, 11 * k + 1)
                        else:
                            wait(pe, s_v, 5 * j - 2)
                    elif c == 1:
                        wait(pe, fin_v, 4 * j - 3)
                    elif c == 2:
                        wait(pe, fin_v, 4 * j - 2)
                    else:
                        wait(pe, t_ev, 4 * j + 1)
                    for n, t in enumerate((X0, X1, TB)):
                        ins = nc.tensor.transpose(bank[TURN_BANK[c]][:, n * P:(n + 1) * P],
                                                  xbc[t][:, c * CH:(c + 1) * CH], ident)
                    ins.then_inc(t_mm, 1)

                def decays(c):
                    for g in range(2):
                        i = 2 * c + g
                        if i >= 2:
                            wait(pe, e_a, 8 * j + i - 1)
                        else:
                            if i == 0:
                                wait(pe, p4_in, 64 * (j + 1))
                            wait(pe, fin_v, 4 * j - 1 + g)
                        dst = bank[2 + g]
                        pc = P4[:, c * CH:(c + 1) * CH]
                        mm(dst[:, :], idb[:, :], maskb[:, :], start=True, stop=False)
                        mm(dst[:, :], pc, nselb[0:32, g * 512:(g + 1) * 512], start=False, stop=False)
                        for n in range(4):
                            hh = 4 * g + n
                            ins = mm(dst[:, n * P:(n + 1) * P], selb[0:32, hh * P:(hh + 1) * P], pc,
                                     start=False, stop=(n == 3))
                        ins.then_inc(d_mm, 1)

                def within(c):
                    wait(pe, m_v, 8 * j + 2 * c + 2)
                    wait(pe, px_p, 7 * j + 2 * c + 1)
                    if c == 0 and C:
                        wait(pe, ry_a, 2 * i2 + 1)
                        wait(pe, o_v, i2 + 1)
                    elif c == 0:
                        wait(pe, t_ev, 4 * j + 3)
                    for hh in range(NH):
                        q = 32 * (hh % 4)
                        ins = mm(bank[6 + hh // 4][q:q + 32, c * CH:(c + 1) * CH], dtx[c][:, hh * HD:(hh + 1) * HD],
                                 M[2 * (c % 2) + hh // 4][:, (hh % 4) * CH:(hh % 4 + 1) * CH], start=True, stop=True,
                                 tile_position=(0, q))
                    ins.then_inc(y_mm, 1)

                if B:
                    decays(0)
                    wait(pe, silu_a, 6 * j + 6)
                    wait(pe, s_v, 5 * j)
                    for c in range(NC):
                        cs = slice(c * CH, (c + 1) * CH)
                        ins = mm(bank[5][:, cs], xbc[TB][:, cs], xbc[TC][:, cs], start=True, stop=True)
                    ins.then_inc(g_mm, 1)
                    for c in range(3):
                        turn(c)
                if B:
                    decays(1)
                if A:
                    project(2)
                if B:
                    turn(3)
                def rows_of_heads(t):
                    if t == 0:
                        wait(pe, t_ev, 4 * j + 4)
                    else:
                        wait(pe, e2_a, 2 * j + 1)
                    mm(bank[4][:, 128:512], selxb[0:32, t * P:(t + 1) * P], P4[:, 128:512],
                       start=True, stop=True).then_inc(e2_mm, 1)

                if C and not B:
                    wait(pe, b2_v, 2)
                    wait(pe, pa, 11)
                    wait(pe, fin_v, 4 * STEPS)
                    network(0, 0, prep=True)
                if C:
                    square_mean()
                if A:
                    project(3)
                if C:
                    project_out()
                if B and not A:
                    prepare[2](0)
                if B:
                    decays(2)
                    rows_of_heads(0)
                    within(0)
                if A:
                    project(4)
                if B:
                    rows_of_heads(1)
                    decays(3)
                if B and not A:
                    prepare[3](0)
                if N:
                    wait(pe, sqh_a, k + 2)
                    wait(pe, zc_a, 2 * k + 1)
                    mm(bank[0][:, :], mean128[:, :], sqh[:, :], start=True, stop=True).then_inc(ms_mm, 1)
                elif A:
                    wait(pe, zc_a, 2 * k + 1)
                    prepare[0](0)
                if B:
                    within(1)
                if A:
                    project(5)
                    wait(pe, dtc_v, 11 * k + 11)
                    if N:
                        wait(pe, rb_a, 2 * k + 3)
                    else:
                        wait(pe, pa, 2)
                    nc.tensor.transpose(bank[0][:, 0:P], dt_[:, :], ident)
                    nc.tensor.transpose(bank[0][:, P:2 * P], wdec[:, :], ident)
                    mm(bank[0][:, 2 * P:2 * P + 32], onesb[:, :], spend[:, :], start=True, stop=True).then_inc(tr_mm, 1)
                if B:
                    within(2)
                    wait(pe, px_p, 7 * j + 4)
                    wait(pe, e2_a, 2 * j + 2)
                    mm(bank[4][:, 0:DI], xtok[0][:, 256:384], xw[0][:, :], start=True, stop=True)
                    mm(bank[4][:, DI:2 * DI], xtok[1][:, 256:384], xw[1][:, :], start=True, stop=True).then_inc(st_mm, 1)
                    wait(pe, m_v, 8 * j + 8)
                    wait(pe, px_p, 7 * j + 6)
                    mm(bank[5][:, 0:DI], xtok[2][:, 256:384], xw[2][:, :], start=True, stop=True).then_inc(st_mm, 1)
                if B:
                    within(3)
                if N:
                    wait(pe, dta_a, 5 * k + 5)
                    project_early(k + 1, 0)
                    wait(pe, zc_a, 2 * k + 2)
                    project_early(k + 1, 1)
                if B:
                    wait(pe, s_v, 5 * j + 5)
                    for t in range(2):
                        wait(pe, e_a, 8 * j + 7 + t)
                        for c in range(1, NC):
                            cs = slice(c * CH, (c + 1) * CH)
                            ins = mm(bank[2 + t][:, cs], S[c][:, t * P:(t + 1) * P], xbc[TC][:, cs], start=True, stop=True)
                        ins.then_inc(yi_mm, 1)
                if B and not A:
                    prepare[4](0)

            def project_early(n, t):
                wait(pe, wa[t], 16 * (n + 1))
                wait(pe, hn_v, n + 1)
                mm(bank[t][:, :], WA[t][:, :], hn[:, :], start=True, stop=True).then_inc(pj_mm, 1)

            pe.wait_ge(rb_a, 1)
            pe.wait_ge(xt_ev, NB)
            project_early(0, 0)
            project_early(0, 1)
            pe.wait_ge(const_v, 9)
            pe.wait_ge(hup, NB)
            def turn_weights(n):
                wait(pe, pv, 25 * n + 24)
                for c in range(4):
                    ins = nc.tensor.transpose(bank[7][:, :].bitcast(BF16)[0:32, c * P:(c + 1) * P],
                                              C3[:, 32 * c:32 * c + 32], idb[:, :])
                ins.then_inc(pm_mm, 1)

            OWN = {5: turn_weights}

            def network(b, e, prep):
                first = isinstance(b, int) and b == 0
                q = b * NX + e
                down = not (first and e == 0)
                ep = (e - 1) % NX
                for t in range(HT):
                    if e == 0 and t == 0:
                        wait(pe, pv, 25 * b + 7)
                        wait(pe, pa, 11 * b + 10)
                    if first and t == 0:
                        wait(pe, wl_v, e + 1)
                    if t < HT - 1:
                        wait(pe, r_a, 2 * (HT - 1) * (q - 1) + 2 * t + 2)
                    else:
                        wait(pe, lo_v, HT * q)
                    w = slice(e * HE + t * P, e * HE + (t + 1) * P)
                    nh = nH[:, bass.ds((b % 2) * L, L)]
                    nl = nL[:, bass.ds((b % 2) * L, L)]
                    mm(bank[t][:, :], WH[0][:, w], nh, start=True, stop=False)
                    mm(bank[t][:, :], WL[0][:, w], nh, start=False, stop=False)
                    mm(bank[t][:, :], WH[0][:, w], nl, start=False, stop=True).then_inc(u_mm, 1)
                    if down:
                        down_product(q - 1, ep, t, first)
                    if prep and HT * e + t in NEXT:
                        NEXT[HT * e + t](b + 1)
                    if HT * e + t in OWN:
                        if first:
                            wait(pe, o_v, STEPS)
                        OWN[HT * e + t](b)
                    if HT * e + t == 12 and not first:
                        if prep:
                            wait(pe, pa, 11 * b + 13)
                        else:
                            wait(pe, pv, 25 * b + 25)
                        turn_out(b - 1)
                if down and ep > 0:
                    wait(pe, ec_v, b * NE - 1 if e == 0 else b * NE + ep - 1)
                    if ep == 1:
                        wait(pe, pv, 25 * b + 25)
                    mm(bank[6][:, :], selb[0:32, (ep - 1) * P:ep * P], CT[:, :],
                       start=True, stop=True).then_inc(cb_mm, 1)

            def body_ff(b, prep):
                for e in range(1 if isinstance(b, int) and b == 0 else 0, NX):
                    network(b, e, prep)

            def down_product(q, e, t, first):
                if t == 0:
                    wait(pe, eo_a, q if e == 0 else q - 1)
                    if first:
                        wait(pe, wl_p, e + 1)
                if t < HT - 1:
                    wait(pe, r_a, 2 * (HT - 1) * q + 2 * t + 1)
                else:
                    wait(pe, hi_v, q + 1)
                w = slice(e * HE + t * P, e * HE + (t + 1) * P)
                dst = bank[4 + e % 2]
                mm(dst[:, :], WH[1][:, w], hH[t][:, :], start=(t == 0), stop=False)
                mm(dst[:, :], WL[1][:, w], hH[t][:, :], start=False, stop=False)
                wait(pe, lo_v, HT * q + t + 1)
                mm(dst[:, :], WH[1][:, w], hL[t][:, :], start=False, stop=(t == HT - 1)).then_inc(dn_mm, 1)

            def turn_out(b):
                wait(pe, fo_v, b + 1)
                for c in range(4):
                    ins = nc.tensor.transpose(bank[7][:, c * P:(c + 1) * P], fo[:, c * P:(c + 1) * P], ident)
                ins.then_inc(ft_mm, 1)

            steps(pe, body)
            blocks(pe, body_ff)
            for t in range(HT):
                down_product(NB * NX - 1, NX - 1, t, False)
            wait(pe, ec_v, NB * NE - 1)
            mm(bank[6][:, :], selb[0:32, (NE - 1) * P:NE * P], CT[:, :],
               start=True, stop=True).then_inc(cb_mm, 1)
            turn_out(NB - 1)

        @block.scalar
        def _(act):
            f = nc.scalar.activation
            act.wait_ge(s_mod, 32)
            f(cS[:, :], cT[:, :], ACT.Silu).then_inc(cs_a, 1)
            nc.scalar.preload_act_table_set(EXPLN)
            act.wait_ge(s_par, 16)
            act.wait_ge(s_cst, 16)
            na = PAR[:, :].rearrange("p (l n) -> p l n", n=NPAR)[:, :, C_NA]
            f(na, na, ACT.Exp).then_inc(rstd_a, 1)
            def take_input(first, last):
                with act.Fori(first, last) as i:
                    for odd in range(2):
                        b = 2 * i + odd
                        act.wait_ge(xr_mm, b + 1)
                        f(xT[:, bass.ds(act.snap(b * L), L)], bank[2 * odd + 1][:, :], ACT.Copy).then_inc(xt_ev, 1)

            take_input(0, NB // 4)
            act.wait_ge(bn_v, 64)
            f(lnv[:, :], mv[:, :].rearrange("p (n two) -> p n two", two=2)[:, :, 1], ACT.Ln, bias=eps5).then_inc(rstd_a, 1)
            act.wait_ge(rstd_a, 2)
            f(rstd[:, :], lnv[:, :], ACT.Exp, scale=-0.5).then_inc(rstd_a, 1)
            take_input(NB // 4, NB // 2)

            def modulate_input(b, odd):
                act.wait_ge(xt_mm, b + 1)
                f(h[:, bass.ds(act.snap(b * L), L)], bank[2 + 4 * odd][:, :], ACT.Identity, scale=MOD[:, bass.ds(b + 8, 1)],
                  bias=MOD[:, bass.ds(b, 1)]).then_inc(hup, 1)

            def norm_square(n):
                wait(act, dt_mm, n)
                f(WDT[:, :], PAR[:, bass.ds(n // NB * NPAR + C_WDT, 32)], ACT.Copy).then_inc(wdt_a, 1)
                wait(act, hup, n + 1)
                wait(act, ms_mm, n)
                f(sqh[:, :], h[:, bass.ds(n % NB * L, L)], ACT.Square).then_inc(sqh_a, 1)

            def norm_log(n):
                wait(act, ms_mm, n + 1)
                f(lnm[:, :], bank[0][:, :], ACT.Ln, bias=eps5).then_inc(rb_a, 1)

            def norm_root(n):
                wait(act, rb_a, 2 * n + 1)
                wait(act, hn_v, n)
                f(rB[:, :], lnm[:, :], ACT.Exp, scale=-0.5).then_inc(rb_a, 1)

            act.wait_ge(mod_v, 6)
            modulate_input(0, 0)
            norm_square(0)
            for b in range(1, 4):
                modulate_input(b, b % 2)
            norm_log(0)
            norm_root(0)
            with act.Fori(2, NB // 2) as i:
                modulate_input(2 * i, 0)
                modulate_input(2 * i + 1, 1)

            def split(e):
                for w in range(2):
                    cs = slice(e * HE, (e + 1) * HE)
                    f(WH[w][:, cs], RAW[w][:, cs], ACT.Copy).then_inc(wh_a, 1)

            def root(n, count, eps):
                f(lnf[:, :], prep_bank(n)[:, :], ACT.Ln, bias=eps).then_inc(pa, 1)
                wait(act, pa, 11 * n + count)
                f(rf[:, :], lnf[:, :], ACT.Exp, scale=-0.5).then_inc(pa, 1)

            def square_h(n):
                if isinstance(n, int) and n == 0:
                    wait(act, hup, NB + STEPS - NB + 1)
                f(sqf[:, :], h[:, bass.ds(n * L, L)], ACT.Square).then_inc(pa, 1)

            def root_h(n):
                wait(act, pm_mm, 6 * n + 1)
                root(n, 2, eps5)

            def square_x(n):
                wait(act, pv, 25 * n + 3)
                f(sqf[:, :], nT[:, :], ACT.Square).then_inc(pa, 1)

            def root_x(n):
                wait(act, pm_mm, 6 * n + 3)
                root(n, 5, eps5)

            def square_m(n):
                wait(act, pv, 25 * n + 5)
                f(sqf[:, :], nT[:, :], ACT.Square).then_inc(pa, 1)

            def root_m(n):
                wait(act, pm_mm, 6 * n + 4)
                root(n, 8, eps8)

            def halve(n):
                wait(act, pv, 25 * n + 6)
                f(nH[:, bass.ds((n % 2) * L, L)], nT[:, :], ACT.Copy).then_inc(pa, 1)

            def exp_logits(n):
                wait(act, pm_mm, 6 * n + 5)
                f(pr[:, :], prep_bank(n)[:, 0:32], ACT.Exp, scale=-1.0).then_inc(pa, 1)

            NEXT = {2: square_h, 9: root_h, 17: square_x, 20: root_x, 23: square_m, 26: root_m, 29: halve, 32: exp_logits}
            prepare = list(NEXT.values())

            def body(k, A, B, C, N):
                j, i2 = k - 1, k - 2

                def decay_exp(i):
                    wait(act, d_mm, 8 * j + i + 1)
                    wait(act, m_v, 8 * j + i - 1)
                    f(E[i % 2][:, :], bank[2 + i % 2][:, :], ACT.Exp).then_inc(e_a, 1)

                def row_exp(t):
                    wait(act, e2_mm, 2 * j + 1 + t)
                    if t == 0:
                        wait(act, fin_v, 4 * j)
                    f(E2[t][:, :], bank[4][:, 128:512], ACT.Exp).then_inc(e2_a, 1)

                def tap(t):
                    wait(act, pj_mm, 6 * k + t + 1)
                    wait(act, silu_a, 6 * (k - 1) + SILU_TURN[t] + 1)
                    f(cv[t][:, :], bank[t % 2][:, :], ACT.Identity, scale=PAR[:, bass.ds(pk + C_CW + 4 * t + 3, 1)],
                      bias=PAR[:, bass.ds(pk + C_CB + t, 1)]).then_inc(tap_v[t], 1)

                def turned(c):
                    wait(act, t_mm, 4 * j + c + 1)
                    if c == 0:
                        wait(act, px_p, 7 * j)
                        wait(act, st_mm, 2 * j)
                    f(xtok[c][:, :], bank[TURN_BANK[c]][:, 0:384], ACT.Copy).then_inc(t_ev, 1)

                nc.scalar.preload_act_table_set(EXPLN)
                if not B and C:
                    act.wait_ge(s_ffw, 48)
                    wait(act, fin_v, 4 * STEPS)
                    split(0)
                    split(1)
                if A:
                    pk = act.snap(k // NB * NPAR)
                    wait(act, dtc_v, 11 * k + 1)
                    f(ax[:, :], u[:, :], ACT.Abs).then_inc(dta_a, 1)
                if B:
                    decay_exp(0)
                if A:
                    wait(act, dta_a, 5 * k + 1)
                    f(ex[:, :], ax[:, :], ACT.Exp, scale=-1.0).then_inc(dta_a, 1)
                if B:
                    decay_exp(1)
                if A:
                    wait(act, dta_a, 5 * k + 2)
                    f(ln1[:, :], ex[:, :], ACT.Ln, bias=1.0).then_inc(dta_a, 1)
                if B:
                    for c in range(3):
                        turned(c)
                    wait(act, s_v, 5 * j - 1)
                    f(dec[:, :], DTW[:, 2 * P:], ACT.Exp).then_inc(dec_a, 1)
                if C:
                    for t in range(2):
                        wait(act, fin_p, 4 * i2 + 2 + 2 * t)
                        wait(act, ss_mm, i2)
                        f(sqy[t][:, :], y2[t][:, :], ACT.Square).then_inc(sq_a, 1)
                        if not B:
                            split(2 + t)
                if B:
                    decay_exp(2)
                    turned(3)
                if A:
                    tap(2)
                if B:
                    decay_exp(3)
                if B and not A:
                    prepare[2](0)
                if C and not B:
                    wait(act, wl_v, HT - 1)
                    network(0, 0, prep=True)
                if C:
                    wait(act, ss_mm, i2 + 1)
                    wait(act, o_v, i2)
                    f(lnY[:, :], bank[6][:, :], ACT.Ln, bias=eps5).then_inc(ry_a, 1)
                    wait(act, ry_a, 2 * i2 + 1)
                    f(rY[:, :], lnY[:, :], ACT.Exp, scale=-0.5).then_inc(ry_a, 1)
                if B and not A:
                    prepare[3](0)
                if A:
                    wait(act, dtc_v, 11 * k + 4)
                    f(ecs[:, :], cum[:, :], ACT.Exp, scale=-1.0, bias=cum[:, CH - 1:CH]).then_inc(dta_a, 1)
                if N:
                    norm_square(k + 1)
                elif A:
                    prepare[0](0)
                if A:
                    tap(3)
                if B:
                    decay_exp(4)
                    decay_exp(5)
                    row_exp(0)
                if B and not A:
                    prepare[4](0)
                if A:
                    wait(act, silu_a, 6 * k)
                    wait(act, pj_mm, 6 * k + 5)
                    f(zraw[0][:, :], bank[0][:, :], ACT.Copy).then_inc(zc_a, 1)
                if B:
                    row_exp(1)
                    wait(act, s_wo, 16 * (j + 1))
                    wait(act, out_mm, j)
                    gw = act.snap(j // NB * NPAR + C_GW)
                    for t in range(2):
                        f(WO[:, t * DM:(t + 1) * DM], WO_raw[:, t * DM:(t + 1) * DM], ACT.Copy,
                          scale=PAR[:, bass.ds(gw + t, 1)]).then_inc(wos_a, 1)
                    decay_exp(6)
                if N:
                    norm_log(k + 1)
                if B:
                    decay_exp(7)
                if N:
                    norm_root(k + 1)
                elif A:
                    prepare[1](0)
                if B and not A:
                    for piece in prepare[5:]:
                        piece(0)
                if A:
                    wait(act, pj_mm, 6 * k + 6)
                    f(zraw[1][:, :], bank[1][:, :], ACT.Copy).then_inc(zc_a, 1)
                    wait(act, tr_mm, k + 1)
                    wait(act, px_p, 7 * k)
                    wait(act, dec_a, k)
                    f(DTW[:, :], bank[0][:, 0:288], ACT.Copy).then_inc(dta_a, 1)
                if A:
                    def silu(t):
                        wait(act, tap_v[t], 4 * (k + 1))
                        if t == TB:
                            wait(act, t_mm, 4 * k)
                        elif t == TC:
                            wait(act, yi_mm, 2 * k)
                        else:
                            wait(act, fin_v, 4 * (k - 1) + 1 + t)
                        f(xbc[t][:, :], cv[t][:, :], ACT.Silu).then_inc(silu_a, 1)

                    silu(TB)
                    for t in range(2):
                        if t == 0:
                            wait(act, zc_a, 2 * k + 2)
                        wait(act, fin_p, 4 * (k - 1))
                        f(zs[:, bass.ds((k % 2) * 2 * L + t * L, L)], zraw[t][:, :], ACT.Silu).then_inc(silu_a, 1)
                    silu(X0)
                    silu(X1)
                    silu(TC)

            def finish(q, e):
                wait(act, dn_mm, HT * (q + 1))
                f(es if e == 0 else eb, bank[4 + e % 2][:, :], ACT.Identity, bias=B2[:, e:e + 1]).then_inc(eo_a, 1)

            def network(b, e, prep):
                first = isinstance(b, int) and b == 0
                q = b * NX + e
                for t in range(HT):
                    if t < HT - 1:
                        bias = PAR2[:, F_B1 + HT * e + t:F_B1 + HT * e + t + 1]
                        wait(act, u_mm, HT * q + t + 1)
                        wait(act, dn_mm, HT * (q - 1) + t + 1)
                        f(hH[t][:, :], bank[t][:, :], ACT.Relu, bias=bias).then_inc(r_a, 1)
                        wait(act, lo_v, HT * (q - 1) + t + 1)
                        f(hr[t], bank[t][:, :], ACT.Relu, bias=bias).then_inc(r_a, 1)
                    if prep and HT * e + t in NEXT:
                        NEXT[HT * e + t](b + 1)
                    if HT * e + t == 13 and not first:
                        copy_out(b - 1)
                if not (first and e == 0):
                    ep = (e - 1) % NX
                    if ep == 0:
                        if not first:
                            wait(act, acc_p, NE * (b - 1) + 1)
                    elif ep == 1:
                        if not first:
                            wait(act, ec_v, NE * b)
                    else:
                        wait(act, ec_v, NE * b + ep - 1 if e > 0 else NE * b - 1)
                    finish(q - 1, ep)

            def body_ff(b, prep):
                for e in range(1 if isinstance(b, int) and b == 0 else 0, NX):
                    network(b, e, prep)

            def copy_out(b):
                wait(act, ft_mm, b + 1)
                wait(act, s_out, 16 * b)
                f(ob, bank[7][:, :], ACT.Copy).then_inc(ob_a, 1)

            steps(act, body)
            for e in range(4, NX):
                split(e)
            act.wait_ge(b2_v, 2)
            blocks(act, body_ff)
            wait(act, ec_v, NE * NB - 1)
            finish(NB * NX - 1, NX - 1)
            copy_out(NB - 1)

        @block.vector
        def _(dve):
            tt, ts, stt = nc.vector.tensor_tensor, nc.vector.tensor_scalar, nc.vector.scalar_tensor_tensor
            cp = nc.vector.tensor_copy
            nc.vector.memset(mean128[:, :], 1.0 / DM).then_inc(const_v, 1)
            nc.vector.memset(mean256[:, :], 1.0 / DI).then_inc(const_v, 1)
            nc.vector.memset(ones_row[:, :], 1.0).then_inc(const_v, 1)
            nc.vector.memset(onesb[:, :], 1.0).then_inc(const_v, 1)
            for n in range(32):
                if n % 8 == 0:
                    dve.wait_ge(s_x[n // 8], 16)
                nc.vector.bn_stats(bst[:, 6 * n:6 * n + 6], xin[:, n * P:(n + 1) * P]).then_inc(bn_v, 1)
            dve.wait_ge(bn_v, 32)
            for n in range(32):
                nc.vector.bn_aggr(mv[:, 2 * n:2 * n + 2], bst[:, 6 * n:6 * n + 6]).then_inc(bn_v, 1)
            dve.wait_ge(mod_mm, 1)
            dve.wait_ge(rstd_a, 1)
            cp(MOD[:, :], bank[4][:, 0:48]).then_inc(mod_v, 1)
            ts(PAR[:, :].rearrange("p (l n) -> p l n", n=NPAR)[:, :, C_NA],
               PAR[:, :].rearrange("p (l n) -> p l n", n=NPAR)[:, :, C_NA], -1.0, None, ALU.mult).then_inc(const_p, 1)
            dve.wait_ge(mod_v, 1)
            m3 = MOD[:, :].rearrange("p (a i b) -> p a i b", a=2, i=3)
            g2 = gsg[:, :].rearrange("p (a b) -> p a b", a=2)
            ts(m3[:, :, 1, :], m3[:, :, 1, :], 1.0, None, ALU.add).then_inc(mod_v, 1)
            ts(g2, m3[:, :, 2, :], 0.0, 2.0, ALU.is_ge, ALU.mult).then_inc(mod_v, 1)
            dve.wait_ge(mod_v, 3)
            ts(g2, g2, -1.0, None, ALU.add).then_inc(mod_v, 1)
            dve.wait_ge(mod_v, 4)
            tt(m3[:, :, 2, :], m3[:, :, 2, :], g2, ALU.mult).then_inc(mod_v, 1)
            dve.wait_ge(mod_v, 5)
            stt(out=m3[:, :, 2, :], in0=m3[:, :, 2, :], scalar=0.25, in1=g2, op0=ALU.max, op1=ALU.mult).then_inc(mod_v, 1)
            dve.wait_ge(rstd_a, 3)
            def normalise(b, odd):
                xb = xin[:, bass.ds(b * L, L)]
                wait(dve, xt_mm, b - 1)
                for n in range(4):
                    ins = ts(xn[odd][:, n * P:(n + 1) * P], xb[:, n * P:(n + 1) * P], mv[:, bass.ds(b * 8 + 2 * n, 1)],
                             rstd[:, bass.ds(b * 4 + n, 1)], ALU.subtract, ALU.mult)
                ins.then_inc(xn_v, 1)

            normalise(0, 0)
            normalise(1, 1)
            with dve.Fori(1, NB // 2) as i:
                normalise(2 * i, 0)
                normalise(2 * i + 1, 1)

            def v(ins, n=0, own=None):
                ins.then_inc(pv, 1)
                if own:
                    wait(dve, pv, 25 * n + own)

            def four(t):
                return t[:, :].rearrange("p (s e) -> p s e", s=4)

            def pairs(t):
                return t[:, :].rearrange("p (s e f) -> p s e f", s=4, e=NE)

            def add_mamba(n):
                xb = xT[:, bass.ds(n * L, L)]
                wait(dve, pa, 11 * n + 3)
                wait(dve, pv, 25 * n - 18)
                v(stt(out=nT[:, :], in0=h[:, bass.ds(n * L, L)], scalar=gaf[:, bass.ds(n, 1)], in1=rf[:, :],
                      op0=ALU.mult, op1=ALU.mult), n, 1)
                v(tt(xb, nT[:, :], xb, ALU.add), n, 2)

            def centre(n):
                wait(dve, pm_mm, 6 * n + 2)
                v(tt(nT[:, :], xT[:, bass.ds(n * L, L)], prep_bank(n)[:, :], ALU.subtract))

            def modulate(n):
                wait(dve, pa, 11 * n + 6)
                v(tt(nT[:, :], nT[:, :], rf[:, :], ALU.mult), n, 4)
                v(ts(nT[:, :], nT[:, :], MOD[:, bass.ds(n + 32, 1)], MOD[:, bass.ds(n + 24, 1)], ALU.mult, ALU.add))

            def scale(n):
                wait(dve, pa, 11 * n + 9)
                v(stt(out=nT[:, :], in0=nT[:, :], scalar=PAR2[:, F_NW:F_NW + 1], in1=rf[:, :], op0=ALU.mult, op1=ALU.mult))

            def halve(n):
                par = bass.ds((n % 2) * L, L)
                wait(dve, pa, 11 * n + 10)
                v(tt(nL[:, par], nT[:, :], nH[:, par].bitcast(F32), ALU.subtract))

            def sigmoid(n):
                wait(dve, pa, 11 * n + 11)
                v(ts(prx[:, :], pr[:, :], 1.0, None, ALU.add), n, 8)
                v(nc.vector.reciprocal(pm[:, :], prx[:, :]), n, 9)

            def rank(n):
                inner, outer = four(pm).unsqueeze(2).to_broadcast([P, 4, NE, NE]), four(pm).unsqueeze(3).to_broadcast([P, 4, NE, NE])
                tri = CST[:, K_TRI:K_TRI + 64].rearrange("p (e f) -> p e f", e=NE).unsqueeze(1).to_broadcast([P, 4, NE, NE])
                v(tt(pairs(cgt), inner, outer, ALU.is_gt))
                v(tt(pairs(ceq), inner, outer, ALU.is_equal), n, 11)
                v(tt(pairs(ceq), pairs(ceq), tri, ALU.mult), n, 12)

            def split(e):
                cs = slice(e * HE, (e + 1) * HE)
                wait(dve, wh_a, 2 * e + 1)
                tt(WL[0][:, cs], RAW[0][:, cs], WH[0][:, cs].bitcast(F32), ALU.subtract).then_inc(wl_v, 1)

            NEXT = {10: add_mamba, 16: centre, 21: modulate, 28: scale, 30: halve, 33: sigmoid, 34: rank}
            prepare = list(NEXT.values())

            def gate_and_bias():
                dve.wait_ge(s_ffw, 48)
                tt(gaf[:, :], MOD[:, 16:24], PAR2[:, F_FW:F_FW + 1].to_broadcast([P, NB]), ALU.mult).then_inc(c3_v, 1)
                nc.vector.memset(C3[:, :], 0.0).then_inc(c3_v, 1)
                b1_last = PAR2[:, F_B1:F_B1 + NX * HT].rearrange("p (e t) -> p e t", t=HT)[:, :, HT - 1]
                ts(nb1[:, :], b1_last, -1.0, None, ALU.mult).then_inc(b2_v, 1)
                dve.wait_ge(c3_v, 2)

            def second_bias():
                dve.wait_ge(bc_mm, 1)
                tt(B2[:, :], bank[1][:, 0:NX], PAR2[:, F_B2:F_B2 + NX], ALU.add).then_inc(b2_v, 1)

            def body(k, A, B, C, N):
                j, i2 = k - 1, k - 2
                if B and not A:
                    second_bias()
                if A:
                    pk = dve.snap(k // NB * NPAR)

                def step_size():
                    wait(dve, dt_mm, k + 1)
                    ts(u[:, :], bank[4][:, 0:CH], PAR[:, bass.ds(pk + C_DTB, 1)], None, ALU.add).then_inc(dtc_v, 1)

                def tap(t, s):
                    cw = pk + C_CW + 4 * t
                    src = bank[t % 2]
                    if s == 0:
                        wait(dve, pj_mm, 6 * k + t + 1)
                        wait(dve, silu_a, 6 * (k - 1) + SILU_TURN[t] + 1)
                        ts(cv[t][:, :], src[:, :], PAR[:, bass.ds(cw + 3, 1)], PAR[:, bass.ds(pk + C_CB + t, 1)],
                           ALU.mult, ALU.add).then_inc(tap_v[t], 1)
                    else:
                        wait(dve, tap_v[t], 4 * k + s)
                        stt(out=cv[t][:, s:L], in0=src[:, 0:L - s], scalar=PAR[:, bass.ds(cw + 3 - s, 1)],
                            in1=cv[t][:, s:L], op0=ALU.mult, op1=ALU.add).then_inc(tap_v[t], 1)

                def apply_decay(i):
                    c = i // 2
                    wait(dve, e_a, 8 * j + i + 1)
                    if i == 0:
                        wait(dve, g_mm, j + 1)
                    wait(dve, y_mm, 4 * j + c - 1)
                    tt(M[i % 4][:, :].rearrange("p (n t) -> p n t", n=4),
                       E[i % 2][:, :].rearrange("p (n t) -> p n t", n=4),
                       bank[5][:, c * CH:(c + 1) * CH].unsqueeze(1).to_broadcast([P, 4, CH]),
                       ALU.mult).then_inc(m_v, 1)

                def softplus():
                    wait(dve, dta_a, 5 * k + 3)
                    wait(dve, tr_mm, k)
                    stt(out=dt_[:, :], in0=u[:, :], scalar=0.0, in1=ln1[:, :], op0=ALU.max, op1=ALU.add).then_inc(dtc_v, 1)

                def step_decay():
                    wait(dve, dtc_v, 11 * k + 2)
                    ts(dA[:, :], dt_[:, :], PAR[:, bass.ds(pk + C_NA, 1)], None, ALU.mult).then_inc(dtc_v, 1)

                def running_sum():
                    wait(dve, dtc_v, 11 * k + 3)
                    nc.vector.tensor_tensor_scan(cum[:, :], ones_row[:, :], dA[:, :], 0.0, ALU.mult, ALU.add).then_inc(dtc_v, 1)

                def part_0():
                    wait(dve, dtc_v, 11 * k + 4)
                    cp(p0[:, :], cum[:, :]).then_inc(dtc_v, 1)

                def rest_1():
                    wait(dve, dtc_v, 11 * k + 5)
                    stt(out=r1[:, :], in0=p0[:, :], scalar=CST[:, K_M1:K_M1 + 1], in1=cum[:, :],
                        op0=ALU.mult, op1=ALU.add).then_inc(dtc_v, 1)

                def part_1():
                    wait(dve, dtc_v, 11 * k + 6)
                    cp(p1[:, :], r1[:, :]).then_inc(dtc_v, 1)

                def rest_2():
                    wait(dve, dtc_v, 11 * k + 7)
                    stt(out=r2[:, :], in0=p1[:, :], scalar=CST[:, K_M2:K_M2 + 1], in1=r1[:, :],
                        op0=ALU.mult, op1=ALU.add).then_inc(dtc_v, 1)

                def part_2():
                    wait(dve, dtc_v, 11 * k + 8)
                    wait(dve, p4_in, 64 * k)
                    cp(p2[:, :], r2[:, :]).then_inc(dtc_v, 1)

                def decay_to_end():
                    wait(dve, dta_a, 5 * k + 4)
                    tt(wdec[:, :], dt_[:, :], ecs[:, :], ALU.mult).then_inc(dtc_v, 1)

                def chunk_decay():
                    wait(dve, dtc_v, 11 * k + 9)
                    ts(spend[:, :], CST[:, K_SELD:K_SELD + 32], p2[:, CH - 1:CH], None, ALU.mult).then_inc(dtc_v, 1)

                def scale_out():
                    wait(dve, out_mm, i2 + 1)
                    wait(dve, ry_a, 2 * i2 + 2)
                    wait(dve, hup, NB + i2)
                    tt(o_sb[:, :], bank[7][:, :], rY[:, :], ALU.mult).then_inc(o_v, 1)

                if B:
                    pj = dve.snap(j // NB * NPAR)
                if A:
                    tap(0, 0)
                    step_size()
                    tap(0, 1)
                    tap(1, 0)
                    tap(0, 2)
                    tap(1, 1)
                    tap(0, 3)
                    tap(1, 2)
                if B:
                    apply_decay(0)
                if A:
                    softplus()
                if B:
                    apply_decay(1)
                if B and not A:
                    prepare[1](0)
                if A:
                    step_decay()
                    tap(1, 3)
                    running_sum()
                    part_0()
                if B:
                    apply_decay(2)
                if A:
                    tap(2, 1)
                    rest_1()
                if B:
                    apply_decay(3)
                if not B and C:
                    for e in range(4):
                        split(e)
                    prepare[5](0)
                    prepare[6](0)
                    network(0, 0, prep=True)
                if A:
                    tap(2, 2)
                    part_1()
                if C:
                    scale_out()
                if B and not A:
                    prepare[2](0)
                if A:
                    tap(2, 3)
                    rest_2()
                    tap(3, 1)
                    part_2()
                    tap(3, 2)
                    decay_to_end()
                    chunk_decay()
                if B:
                    apply_decay(4)
                if A:
                    tap(3, 3)
                if B:
                    for i in range(5, 8):
                        apply_decay(i)
                if N:
                    norm_apply(k + 1)
                elif A:
                    gate_and_bias()
                    prepare[0](0)
                if B:
                    wait(dve, st_mm, 2 * j + 1)
                    wait(dve, yi_mm, 2 * j)
                    cp(S[1][:, :], bank[4][:, 0:DI]).then_inc(s_v, 1)
                    wait(dve, dec_a, j + 1)
                    for c in range(2, NC):
                        wait(dve, s_v, 5 * j + 2 * c - 3)
                        tt(stmp[:, :].rearrange("p (h d) -> p h d", h=NH), S[c - 1][:, :].rearrange("p (h d) -> p h d", h=NH),
                           dec[:, (c - 1) * NH:c * NH].unsqueeze(2).to_broadcast([P, NH, HD]), ALU.mult).then_inc(s_v, 1)
                        wait(dve, s_v, 5 * j + 2 * c - 2)
                        if c == 3:
                            wait(dve, st_mm, 2 * j + 2)
                        new = bank[4][:, DI:2 * DI] if c == 2 else bank[5][:, 0:DI]
                        tt(S[c][:, :], stmp[:, :], new, ALU.add).then_inc(s_v, 1)
                    if not A:
                        prepare[3](0)
                        prepare[4](0)
                    for t in range(2):
                        if t == 0:
                            wait(dve, y_mm, 4 * j + 4)
                        wait(dve, fin_p, 4 * j - 2 + 2 * t)
                        stt(out=yt[t][:, :], in0=xbc[t][:, :], scalar=PAR[:, bass.ds(pj + C_D + t, 1)],
                            in1=bank[6 + t][:, :], op0=ALU.mult, op1=ALU.add).then_inc(fin_v, 1)
                    for t in range(2):
                        wait(dve, yi_mm, 2 * j + 1 + t)
                        wait(dve, e2_a, 2 * j + 1 + t)
                        tt(ti[t][:, :], bank[2 + t][:, 128:512], E2[t][:, :], ALU.mult).then_inc(fin_v, 1)

            def norm_apply(n):
                wait(dve, rb_a, 2 * n + 2)
                wait(dve, pj_mm, 6 * n)
                stt(out=hn[:, :], in0=h[:, bass.ds(n % NB * L, L)], scalar=PAR[:, bass.ds(n // NB * NPAR + C_BNW, 1)],
                    in1=rB[:, :], op0=ALU.mult, op1=ALU.mult).then_inc(hn_v, 1)

            norm_apply(0)
            dve.wait_ge(s_cst, 16)
            cp(idb[:, :], ident).then_inc(const_v, 1)
            cp(maskb[:, :], CST[:, K_MASK:K_MASK + 512]).then_inc(const_v, 1)
            cp(selb[:, :], CST[:, K_SEL:K_SEL + 1024]).then_inc(const_v, 1)
            ts(nselb[:, :], CST[:, K_SEL:K_SEL + 1024], -1.0, None, ALU.mult).then_inc(const_v, 1)
            cp(selxb[:, :], CST[:, K_SELX:K_SELX + 256]).then_inc(const_v, 1)
            def rank_2(n):
                v(tt(cgt[:, :], cgt[:, :], ceq[:, :], ALU.add), n, 13)
                v(nc.vector.tensor_reduce(rnk[:, :], cgt[:, :].rearrange("p (q f) -> p q f", f=NE), AX.X, ALU.add), n, 14)

            def routing(n):
                v(stt(out=pm[:, :], in0=rnk[:, :], scalar=1.5, in1=pm[:, :], op0=ALU.is_lt, op1=ALU.mult), n, 15)
                v(nc.vector.tensor_reduce(csum[:, :], four(pm), AX.X, ALU.add), n, 16)
                v(ts(csum[:, :], csum[:, :], 1e-6, None, ALU.add), n, 17)
                v(nc.vector.reciprocal(csum[:, :], csum[:, :]), n, 18)
                v(tt(four(cmb), four(pm), csum[:, :].unsqueeze(2).to_broadcast([P, 4, NE]), ALU.mult), n, 19)

            def parts(n):
                c3 = C3[:, :].rearrange("p (s q e) -> p s q e", s=4, q=4)
                wait(dve, pm_mm, 6 * n)
                v(cp(c3[:, :, 0, :], four(cmb)), n, 20)
                v(tt(four(cr), four(cmb), c3[:, :, 0, :], ALU.subtract), n, 21)
                v(cp(c3[:, :, 1, :], four(cr)), n, 22)
                v(tt(four(cr), four(cr), c3[:, :, 1, :], ALU.subtract), n, 23)
                v(cp(c3[:, :, 2, :], four(cr)))

            def weights_in(n):
                wait(dve, pm_mm, 6 * n + 6)
                wait(dve, cb_mm, NE * n)
                v(cp(CT[:, :], bank[7][:, :].bitcast(BF16)[0:32, 0:L]))

            OWN = {0: rank_2, 1: routing, 2: parts, 6: weights_in}

            def weigh(q, b, e):
                count = NE * b + e
                wait(dve, cb_mm, count)
                wait(dve, eo_a, q + 1)
                wait(dve, acc_p, count - 1)
                tt(ec, bank[6][:, :], eb, ALU.mult).then_inc(ec_v, 1)

            def finish(b):
                wait(dve, acc_p, NE * (b + 1))
                wait(dve, ft_mm, b)
                stt(out=fo, in0=acc, scalar=MOD[:, bass.ds(b + 40, 1)], in1=xT[:, bass.ds(b * L, L)],
                    op0=ALU.mult, op1=ALU.add).then_inc(fo_v, 1)

            def network(b, e, prep):
                first = isinstance(b, int) and b == 0
                q = b * NX + e
                for t in range(HT):
                    if t == 0:
                        if e > 2:
                            weigh(q - 2, b, e - 2)
                        elif e == 0 and not first:
                            weigh(q - 2, b - 1, NE - 1)
                        elif e == 1 and not first:
                            weigh(q - 2, b - 1, NE)
                        elif e == 2 and not first:
                            finish(b - 1)
                    if t < HT - 1:
                        wait(dve, r_a, 2 * (HT - 1) * q + 2 * t + 2)
                        wait(dve, dn_mm, HT * (q - 1) + t + 1)
                        tt(hL[t][:, :], hr[t], hH[t][:, :].bitcast(F32), ALU.subtract).then_inc(lo_v, 1)
                    else:
                        neg = nb1[:, e:e + 1]
                        wait(dve, u_mm, HT * q + t + 1)
                        wait(dve, dn_mm, HT * q)
                        ts(hH[t][:, :], bank[t][:, :], neg, None, ALU.max).then_inc(hi_v, 1)
                        wait(dve, hi_v, q + 1)
                        stt(out=hL[t][:, :], in0=bank[t][:, :], scalar=neg, in1=hH[t][:, :].bitcast(F32),
                            op0=ALU.max, op1=ALU.subtract).then_inc(lo_v, 1)
                    if prep and HT * e + t in NEXT:
                        NEXT[HT * e + t](b + 1)
                    if HT * e + t in OWN:
                        OWN[HT * e + t](b)

            def body_ff(b, prep):
                for e in range(1 if isinstance(b, int) and b == 0 else 0, NX):
                    network(b, e, prep)

            steps(dve, body)
            for e in range(4, NX):
                split(e)
            dve.wait_ge(wl_p, 3)
            blocks(dve, body_ff)
            weigh(NB * NX - 2, NB - 1, NE - 1)
            weigh(NB * NX - 1, NB - 1, NE)
            finish(NB - 1)

        @block.gpsimd
        def _(pool):
            tt = nc.gpsimd.tensor_tensor

            def body(k, A, B, C, N):
                j, i2 = k - 1, k - 2
                if B:
                    wait(pool, dta_a, 5 * j + 5)
                    for c in range(NC):
                        xv = xtok[c][:, 0:DI].rearrange("p (h d) -> p h d", h=NH)
                        wait(pool, t_ev, 4 * j + c + 1)
                        wait(pool, y_mm, 4 * j - 3 + c)
                        tt(dtx[c][:, :].rearrange("p (h d) -> p h d", h=NH), xv,
                           DTW[:, 32 * c:32 * c + NH].unsqueeze(2).to_broadcast([P, NH, HD]), ALU.mult).then_inc(px_p, 1)
                        if c < NC - 1:
                            if c == 0:
                                wait(pool, st_mm, 2 * j)
                            tt(xw[c][:, :].rearrange("p (h d) -> p h d", h=NH), xv,
                               DTW[:, P + 32 * c:P + 32 * c + NH].unsqueeze(2).to_broadcast([P, NH, HD]),
                               ALU.mult).then_inc(px_p, 1)
                if not B and C:
                    wait(pool, fin_p, 4 * STEPS)
                    for e in range(NX):
                        cs = slice(e * HE, (e + 1) * HE)
                        wait(pool, wh_a, 2 * e + 2)
                        tt(WL[1][:, cs], RAW[1][:, cs], WH[1][:, cs].bitcast(F32), ALU.subtract).then_inc(wl_p, 1)
                if C:
                    hb = h[:, bass.ds(i2 % NB * L, L)]
                    wait(pool, o_v, i2 + 1)
                    tt(hb, hb, o_sb[:, :], ALU.add).then_inc(hup, 1)
                if B:
                    for t in range(2):
                        wait(pool, fin_v, 4 * j + 3 + t)
                        tt(yt[t][:, 128:512], yt[t][:, 128:512], ti[t][:, :], ALU.add).then_inc(fin_p, 1)
                        wait(pool, fin_p, 4 * j + 1 + 2 * t)
                        wait(pool, silu_a, 6 * j + 2 + t)
                        wait(pool, out_mm, j)
                        tt(y2[t][:, :], yt[t][:, :], zs[:, bass.ds((j % 2) * 2 * L + t * L, L)], ALU.mult).then_inc(fin_p, 1)

            steps(pool, body)

            pool.wait_ge(wl_p, NX)

            def add_expert(e, b):
                wait(pool, ec_v, NE * b + e)
                if e == 1:
                    wait(pool, eo_a, NX * b + 1)
                    wait(pool, fo_v, b)
                    tt(acc, es, ec, ALU.add).then_inc(acc_p, 1)
                else:
                    wait(pool, acc_p, NE * b + e - 1)
                    tt(acc, acc, ec, ALU.add).then_inc(acc_p, 1)

            for e in range(1, NX):
                add_expert(e, 0)
            with pool.Fori(1, NB) as b:
                for e in range(1, NX):
                    add_expert(e, b)


def constants():
    import numpy as np
    c = np.zeros((P, NCST), np.float32)
    p, t = np.arange(P)[:, None], np.arange(P)[None, :]
    c[:, K_ID:K_ID + P] = p == t
    c[:, K_MASK:K_MASK + 512] = np.tile(np.where(t >= p, 0.0, -1e30), (1, 4))
    row, head = p % 32, p % 8
    used = row < 24
    c[:, K_SEL:K_SEL + 1024] = used & (head == np.arange(1024)[None, :] // P)
    c[:, K_SELX:K_SELX + 256] = used & (head == np.arange(256)[None, :] // HD)
    q = np.arange(32)[None, :]
    c[:, K_SELD:K_SELD + 32] = used & (head == q % 8) & (p // 32 == q // 8)
    c[:, K_M1] = -(row[:, 0] >= 8).astype(np.float32)
    c[:, K_M2] = -(row[:, 0] >= 16).astype(np.float32)
    c[:, K_EPS5], c[:, K_EPS8] = 1e-5, 1e-8
    e = np.arange(64)[None, :]
    c[:, K_TRI:K_TRI + 64] = (e % 8) < (e // 8)
    return c


def parameters(v):
    import numpy as np
    out = np.zeros((P, NL, NPAR), np.float32)
    w_dt = v["L0_attn_W_in"][:, :, 768:776]
    for part in range(3):
        out[:, :, C_WDT + 8 * part:C_WDT + 8 * part + 8] = w_dt.transpose(1, 0, 2)
        for c in range(NC):
            q = 32 * c + 8 * part
            out[q:q + 8, :, C_DTB] = v["L0_attn_dt_bias"].T
            out[q:q + 8, :, C_NA] = v["L0_attn_A_log"].T
    out[:, :, C_BNW] = v["L0_attn_block_norm_w"].T
    cw = v["L0_attn_conv_w"].reshape(NL, 4, P, 4)
    out[:, :, C_CW:C_CW + 16] = cw.transpose(2, 0, 1, 3).reshape(P, NL, 16)
    out[:, :, C_CB:C_CB + 4] = v["L0_attn_conv_b"].reshape(NL, 4, P).transpose(2, 0, 1)
    out[:, :, C_D:C_D + 2] = np.repeat(v["L0_attn_D"], HD, axis=1).reshape(NL, 2, P).transpose(2, 0, 1)
    out[:, :, C_GW:C_GW + 2] = v["L0_attn_gate_norm_w"].reshape(NL, 2, P).transpose(2, 0, 1)
    return out.reshape(P, NL * NPAR)


def feed_forward(v):
    import numpy as np
    out = np.zeros((P, NPAR2), np.float32)
    b1 = np.concatenate([v["L0_ffn_sb1"][None], v["L0_ffn_eb1"]])
    out[:, F_B1:F_B1 + NX * HT] = b1.reshape(NX * HT, P).T
    out[:, F_B2:F_B2 + NX] = np.concatenate([v["L0_ffn_sb2"][None], v["L0_ffn_eb2"]]).T
    out[:, F_NW] = v["L0_ffn_norm_weight"]
    out[:, F_FW] = v["L0_attn_final_norm_w"]
    out[:, F_RW:F_RW + NE] = v["L0_ffn_router_w"].T
    w1 = np.concatenate([v["L0_ffn_sw1"][None], v["L0_ffn_ew1"]]).transpose(1, 0, 2).reshape(P, NX * HE)
    w2 = np.concatenate([v["L0_ffn_sw2"][None], v["L0_ffn_ew2"]]).reshape(NX, HT, P, DM)
    w2 = w2.transpose(2, 0, 1, 3).reshape(P, NX * HE)
    return out, np.ascontiguousarray(w1), np.ascontiguousarray(w2)


def projection(v):
    import numpy as np
    return np.stack([v["L0_attn_W_in"][:, :, c:c + P] for c in W_COL], axis=1).reshape(-1)


def kernel(**inputs):
    import numpy as np
    import concourse.bacc as bacc
    from concourse.bass_utils import run_bass_kernel_spmd

    v = {n: np.asarray(a) for n, a in inputs.items()}
    par2, w1, w2 = feed_forward(v)
    arrays = {
        "x_in": v["L0_attn_x"].reshape(NB * L, DM),
        "w_in": projection(v),
        "w_out": v["L0_attn_W_out"].reshape(NL, 2, P, DM).transpose(0, 2, 1, 3).reshape(-1),
        "par_in": parameters(v),
        "cst_in": constants(),
        "c_in": np.ascontiguousarray(v["L0_c"].T),
        "wmod_in": v["L0_wmod"],
        "par2_in": par2,
        "w1_in": w1,
        "w2_in": w2,
    }
    arrays = {n: np.ascontiguousarray(a) for n, a in arrays.items()}
    nc = bacc.Bacc("TRN2", target_bir_lowering=False, num_devices=1)
    args = [nc.dram_tensor(n, a.shape, mybir.dt.from_np(a.dtype), kind="ExternalInput").ap() for n, a in arrays.items()]
    out = nc.dram_tensor("out", (NB * L, DM), F32, kind="ExternalOutput").ap()
    build(nc, *args, out)
    r = run_bass_kernel_spmd(nc, [arrays], core_ids=[0])
    return r.results[0]["out"].reshape(NB, L, DM)
```
